# Optimizing a Trainium2 kernel written in Bass

```python
import numpy as np
import jax
import jax.numpy as jnp

def _softmax(x, axis=-1):
    return jax.nn.softmax(x, axis=axis)

def _gelu(x):
    return jax.nn.gelu(x, approximate=True)

def _silu(x):
    return jax.nn.silu(x)

def _sigmoid(x):
    return jax.nn.sigmoid(x)

def _layernorm(x, axis=-1, eps=1e-05):
    m = jnp.mean(x, axis=axis, keepdims=True)
    v = jnp.var(x, axis=axis, keepdims=True)
    return (x - m) / jnp.sqrt(v + eps)

def _scatter_add(tgt, idx, src, axis=0):
    return tgt.at[idx].add(src)

def _segment_sum(src, seg, n):
    return jax.ops.segment_sum(src, seg, n)
kernel_name = 'mk_perceiver_d1_seqx_r4_6d8b02'

def setup_inputs(seed: int=0):
    np.random.seed(seed)
    _w = jnp.asarray

    def _rec_inputs():
        import jax
        import jax.numpy as jnp
        _rk = jax.random.key(seed)
        x = 7.22e-05 + 1 * jax.random.normal(jax.random.fold_in(_rk, 1), (4, 256, 256), jnp.float32)
        _lenS = 256 - jax.random.randint(jax.random.fold_in(_rk, 7), (4,), 0, max(1, 256 // 4) + 1, jnp.int32)
        _lenS2 = 4096 - jax.random.randint(jax.random.fold_in(_rk, 8), (4,), 0, max(1, 4096 // 4) + 1, jnp.int32)
        _ctx_768P = jax.random.normal(jax.random.fold_in(_rk, 11), (4, 16, 192), jnp.float32)
        _ctx_768c = jax.random.dirichlet(jax.random.fold_in(_rk, 511), 0.3 * jnp.ones((16,), jnp.float32), (4, 4096))
        _ctx_768t = jnp.einsum('bsk,bkd->bsd', _ctx_768c, _ctx_768P)
        _ctx_768t = _ctx_768t * jax.lax.rsqrt(jnp.mean(jnp.square(_ctx_768t)) + 1e-12) * 0.953939
        ctx_768 = -0.000191848 + 0.999787 * (_ctx_768t + 0.3 * jax.random.normal(jax.random.fold_in(_rk, 611), (4, 4096, 192), jnp.float32))
        return (x, ctx_768)
    x, ctx_768 = _rec_inputs()

    def _L0_xattn_setup():
        import jax, jax.numpy as jnp
        import numpy as np
        NUM_HEADS = 16
        CLAMP = 10000.0
        key = jax.random.key(seed)
        ks = jax.random.split(key, 8)
        B, Nq, Nkv, Cq, Ckv = (4, 512, 512, 256, 192)
        s_q = 1.0 / np.sqrt(Cq)
        s_kv = 1.0 / np.sqrt(Ckv)
        return {'query': jax.random.normal(ks[0], (B, Nq, Cq), jnp.float32), 'key_value': jax.random.normal(ks[1], (B, Nkv, Ckv), jnp.float32), 'Wq': jax.random.normal(ks[2], (Cq, Cq), jnp.float32) * s_q, 'bq': jnp.zeros((Cq,), jnp.float32), 'Wk': jax.random.normal(ks[3], (Ckv, Cq), jnp.float32) * s_kv, 'bk': jnp.zeros((Cq,), jnp.float32), 'Wv': jax.random.normal(ks[4], (Ckv, Cq), jnp.float32) * s_kv, 'bv': jnp.zeros((Cq,), jnp.float32), 'Wo': jax.random.normal(ks[5], (Cq, Cq), jnp.float32) * s_q, 'bo': jnp.zeros((Cq,), jnp.float32)}
    _L0_xattn_all = _L0_xattn_setup()
    _L0_xattn_in = {k: v for k, v in _L0_xattn_all.items() if k in ('Wq', 'bq', 'Wk', 'bk', 'Wv', 'bv', 'Wo', 'bo')}
    del _L0_xattn_all

    def _L0_attn_setup():
        import jax, jax.numpy as jnp
        import numpy as np
        EMB = 256
        HEADS = 16
        HEADSIZE = EMB // HEADS
        EPS = 1e-05

        def _layernorm(x, g, b):
            m = jnp.mean(x, axis=-1, keepdims=True)
            v = jnp.mean((x - m) ** 2, axis=-1, keepdims=True)
            return (x - m) * jax.lax.rsqrt(v + EPS) * g + b
        key = jax.random.key(seed)
        ks = jax.random.split(key, 6)
        B, T = (4, 512)
        s = 1.0 / np.sqrt(EMB)
        return {'x': jax.random.normal(ks[0], (B, T, EMB), dtype=jnp.float32), 'Wk': jax.random.normal(ks[1], (EMB, EMB), dtype=jnp.float32) * s, 'Wq': jax.random.normal(ks[2], (EMB, EMB), dtype=jnp.float32) * s, 'Wv': jax.random.normal(ks[3], (EMB, EMB), dtype=jnp.float32) * s, 'Wo': jax.random.normal(ks[4], (EMB, EMB), dtype=jnp.float32) * s, 'bo': jnp.zeros((EMB,), dtype=jnp.float32), 'kln_g': jnp.ones((HEADSIZE,), dtype=jnp.float32), 'kln_b': jnp.zeros((HEADSIZE,), dtype=jnp.float32), 'qln_g': jnp.ones((HEADSIZE,), dtype=jnp.float32), 'qln_b': jnp.zeros((HEADSIZE,), dtype=jnp.float32)}
    _L0_attn_all = _L0_attn_setup()
    _L0_attn_in = {k: v for k, v in _L0_attn_all.items() if k in ('Wk', 'Wq', 'Wv', 'Wo', 'bo', 'kln_g', 'kln_b', 'qln_g', 'qln_b')}
    del _L0_attn_all

    def _L0_ffn_setup():
        import jax, jax.numpy as jnp
        import numpy as np
        B, T, D = (8, 1024, 256)
        NUM_SLOTS = 64
        TOP_K = 8
        DQ = D // 4
        DH = D // 2

        def _forward(x, slot_init, w1, b1, w2, b2, tau, Wih, Whh, bih, bhh, wq, bq, wk, bk, wv, bv, ln_g, ln_b, wvp, bvp, wo, bo):
            Bx, Tx, Dx = x.shape
            S = jnp.broadcast_to(slot_init[None], (Bx, NUM_SLOTS, Dx)).astype(x.dtype)
            slot_mean = jnp.broadcast_to(S.mean(axis=1, keepdims=True), (Bx, Tx, Dx))
            ctx = jnp.concatenate([x, slot_mean], axis=-1)
            h = jax.nn.gelu(ctx @ w1 + b1, approximate=False)
            route_logits = (h @ w2 + b2) / (jnp.abs(tau) + 0.1)
            topk_vals, topk_idx = jax.lax.top_k(route_logits, TOP_K)
            topk_w = jax.nn.softmax(topk_vals, axis=-1)
            alpha = (jax.nn.one_hot(topk_idx, NUM_SLOTS, dtype=x.dtype) * topk_w[..., None]).sum(axis=-2)
            slot_input = jnp.einsum('bts,btd->bsd', alpha, x)
            denom = alpha.sum(axis=1) + 1e-08
            si = slot_input / denom[..., None]
            gi = si @ Wih.T + bih
            gh = S @ Whh.T + bhh
            i_r, i_z, i_n = jnp.split(gi, 3, axis=-1)
            h_r, h_z, h_n = jnp.split(gh, 3, axis=-1)
            r = jax.nn.sigmoid(i_r + h_r)
            z = jax.nn.sigmoid(i_z + h_z)
            n = jnp.tanh(i_n + r * h_n)
            S_new = (1.0 - z) * n + z * S
            q = S_new @ wq + bq
            k = S_new @ wk + bk
            v = S_new @ wv + bv
            scale = DQ ** (-0.5)
            attn = jax.nn.softmax(jnp.einsum('bsq,btq->bst', q, k) * scale, axis=-1)
            S_comm = jnp.einsum('bst,btd->bsd', attn, v)
            y = S_new + S_comm
            mu = y.mean(axis=-1, keepdims=True)
            var = y.var(axis=-1, keepdims=True)
            y = (y - mu) * jax.lax.rsqrt(var + 1e-05) * ln_g + ln_b
            slot_values = y @ wvp + bvp
            out = jnp.einsum('bts,bsd->btd', alpha, slot_values)
            return out @ wo + bo
        key = jax.random.key(seed)
        ks = jax.random.split(key, 24)
        n = lambda k, shp, s=0.02: jax.random.normal(k, shp, dtype=jnp.float32) * s
        return {'x': jax.random.normal(ks[0], (B, T, D), dtype=jnp.float32), 'slot_init': n(ks[1], (NUM_SLOTS, D)), 'w1': n(ks[2], (2 * D, DH)), 'b1': jnp.zeros((DH,)), 'w2': n(ks[3], (DH, NUM_SLOTS)), 'b2': jnp.zeros((NUM_SLOTS,)), 'tau': jnp.ones((1,)), 'Wih': n(ks[4], (3 * D, D)), 'Whh': n(ks[5], (3 * D, D)), 'bih': jnp.zeros((3 * D,)), 'bhh': jnp.zeros((3 * D,)), 'wq': n(ks[6], (D, DQ)), 'bq': jnp.zeros((DQ,)), 'wk': n(ks[7], (D, DQ)), 'bk': jnp.zeros((DQ,)), 'wv': n(ks[8], (D, D)), 'bv': jnp.zeros((D,)), 'ln_g': jnp.ones((D,)), 'ln_b': jnp.zeros((D,)), 'wvp': n(ks[9], (D, D)), 'bvp': jnp.zeros((D,)), 'wo': n(ks[10], (D, D)), 'bo': jnp.zeros((D,))}
    _L0_ffn_all = _L0_ffn_setup()
    _L0_ffn_in = {k: v for k, v in _L0_ffn_all.items() if k in ('slot_init', 'w1', 'b1', 'w2', 'b2', 'tau', 'Wih', 'Whh', 'bih', 'bhh', 'wq', 'bq', 'wk', 'bk', 'wv', 'bv', 'ln_g', 'ln_b', 'wvp', 'bvp', 'wo', 'bo')}
    del _L0_ffn_all
    return {'x': x, 'ctx_768': ctx_768, 'L0_xattn_Wq': _L0_xattn_in['Wq'], 'L0_xattn_bq': _L0_xattn_in['bq'], 'L0_xattn_Wk': _L0_xattn_in['Wk'], 'L0_xattn_bk': _L0_xattn_in['bk'], 'L0_xattn_Wv': _L0_xattn_in['Wv'], 'L0_xattn_bv': _L0_xattn_in['bv'], 'L0_xattn_Wo': _L0_xattn_in['Wo'], 'L0_xattn_bo': _L0_xattn_in['bo'], 'L0_attn_Wk': _L0_attn_in['Wk'], 'L0_attn_Wq': _L0_attn_in['Wq'], 'L0_attn_Wv': _L0_attn_in['Wv'], 'L0_attn_Wo': _L0_attn_in['Wo'], 'L0_attn_bo': _L0_attn_in['bo'], 'L0_attn_kln_g': _L0_attn_in['kln_g'], 'L0_attn_kln_b': _L0_attn_in['kln_b'], 'L0_attn_qln_g': _L0_attn_in['qln_g'], 'L0_attn_qln_b': _L0_attn_in['qln_b'], 'L0_ffn_slot_init': _L0_ffn_in['slot_init'], 'L0_ffn_w1': _L0_ffn_in['w1'], 'L0_ffn_b1': _L0_ffn_in['b1'], 'L0_ffn_w2': _L0_ffn_in['w2'], 'L0_ffn_b2': _L0_ffn_in['b2'], 'L0_ffn_tau': _L0_ffn_in['tau'], 'L0_ffn_Wih': _L0_ffn_in['Wih'], 'L0_ffn_Whh': _L0_ffn_in['Whh'], 'L0_ffn_bih': _L0_ffn_in['bih'], 'L0_ffn_bhh': _L0_ffn_in['bhh'], 'L0_ffn_wq': _L0_ffn_in['wq'], 'L0_ffn_bq': _L0_ffn_in['bq'], 'L0_ffn_wk': _L0_ffn_in['wk'], 'L0_ffn_bk': _L0_ffn_in['bk'], 'L0_ffn_wv': _L0_ffn_in['wv'], 'L0_ffn_bv': _L0_ffn_in['bv'], 'L0_ffn_ln_g': _L0_ffn_in['ln_g'], 'L0_ffn_ln_b': _L0_ffn_in['ln_b'], 'L0_ffn_wvp': _L0_ffn_in['wvp'], 'L0_ffn_bvp': _L0_ffn_in['bvp'], 'L0_ffn_wo': _L0_ffn_in['wo'], 'L0_ffn_bo': _L0_ffn_in['bo']}

def reference(x, ctx_768, L0_xattn_Wq, L0_xattn_bq, L0_xattn_Wk, L0_xattn_bk, L0_xattn_Wv, L0_xattn_bv, L0_xattn_Wo, L0_xattn_bo, L0_attn_Wk, L0_attn_Wq, L0_attn_Wv, L0_attn_Wo, L0_attn_bo, L0_attn_kln_g, L0_attn_kln_b, L0_attn_qln_g, L0_attn_qln_b, L0_ffn_slot_init, L0_ffn_w1, L0_ffn_b1, L0_ffn_w2, L0_ffn_b2, L0_ffn_tau, L0_ffn_Wih, L0_ffn_Whh, L0_ffn_bih, L0_ffn_bhh, L0_ffn_wq, L0_ffn_bq, L0_ffn_wk, L0_ffn_bk, L0_ffn_wv, L0_ffn_bv, L0_ffn_ln_g, L0_ffn_ln_b, L0_ffn_wvp, L0_ffn_bvp, L0_ffn_wo, L0_ffn_bo):
    import jax
    import jax.numpy as jnp

    def _L0_xattn_ref(query, key_value, Wq, bq, Wk, bk, Wv, bv, Wo, bo):
        import jax, jax.numpy as jnp
        import numpy as np
        NUM_HEADS = 16
        CLAMP = 10000.0
        B, Nq, Cq = query.shape
        Nkv = key_value.shape[1]
        H = NUM_HEADS
        D = Cq // H
        scale = D ** (-0.5)
        q = (query @ Wq + bq).reshape(B, Nq, H, D).transpose(0, 2, 1, 3)
        k = (key_value @ Wk + bk).reshape(B, Nkv, H, D).transpose(0, 2, 1, 3)
        v = (key_value @ Wv + bv).reshape(B, Nkv, H, D).transpose(0, 2, 1, 3)
        attn = jnp.einsum('bhqd,bhkd->bhqk', q, k) * scale
        attn = jnp.clip(attn, -CLAMP, CLAMP)
        attn = jax.nn.softmax(attn, axis=-1)
        attn = jnp.where(jnp.any(jnp.isnan(attn)), jnp.asarray(1.0 / Nkv, attn.dtype), attn)
        x = jnp.einsum('bhqk,bhkd->bqhd', attn, v).reshape(B, Nq, Cq)
        return x @ Wo + bo

    def _L0_attn_ref(x, Wk, Wq, Wv, Wo, bo, kln_g, kln_b, qln_g, qln_b):
        import jax, jax.numpy as jnp
        import numpy as np
        EMB = 256
        HEADS = 16
        HEADSIZE = EMB // HEADS
        EPS = 1e-05

        def _layernorm(x, g, b):
            m = jnp.mean(x, axis=-1, keepdims=True)
            v = jnp.mean((x - m) ** 2, axis=-1, keepdims=True)
            return (x - m) * jax.lax.rsqrt(v + EPS) * g + b
        B, T, E = x.shape
        k = jnp.einsum('bte,fe->btf', x, Wk).reshape(B, T, HEADS, HEADSIZE)
        q = jnp.einsum('bte,fe->btf', x, Wq).reshape(B, T, HEADS, HEADSIZE)
        v = jnp.einsum('bte,fe->btf', x, Wv).reshape(B, T, HEADS, HEADSIZE)
        k = _layernorm(k, kln_g, kln_b)
        q = _layernorm(q, qln_g, qln_b)
        scale = E ** (-0.25)
        q = q * scale
        k = k * scale
        dot = jnp.einsum('bihd,bjhd->bhij', q, k)
        causal = jnp.triu(jnp.ones((T, T), dtype=bool), k=1)
        dot = jnp.where(causal, -jnp.inf, dot)
        att = jax.nn.softmax(dot, axis=-1)
        out = jnp.einsum('bhij,bjhd->bihd', att, v).reshape(B, T, E)
        return jnp.einsum('bte,fe->btf', out, Wo) + bo

    def _L0_ffn_ref(x, slot_init, w1, b1, w2, b2, tau, Wih, Whh, bih, bhh, wq, bq, wk, bk, wv, bv, ln_g, ln_b, wvp, bvp, wo, bo):
        import jax, jax.numpy as jnp
        import numpy as np
        B, T, D = (8, 1024, 256)
        NUM_SLOTS = 64
        TOP_K = 8
        DQ = D // 4
        DH = D // 2

        def _forward(x, slot_init, w1, b1, w2, b2, tau, Wih, Whh, bih, bhh, wq, bq, wk, bk, wv, bv, ln_g, ln_b, wvp, bvp, wo, bo):
            Bx, Tx, Dx = x.shape
            S = jnp.broadcast_to(slot_init[None], (Bx, NUM_SLOTS, Dx)).astype(x.dtype)
            slot_mean = jnp.broadcast_to(S.mean(axis=1, keepdims=True), (Bx, Tx, Dx))
            ctx = jnp.concatenate([x, slot_mean], axis=-1)
            h = jax.nn.gelu(ctx @ w1 + b1, approximate=False)
            route_logits = (h @ w2 + b2) / (jnp.abs(tau) + 0.1)
            topk_vals, topk_idx = jax.lax.top_k(route_logits, TOP_K)
            topk_w = jax.nn.softmax(topk_vals, axis=-1)
            alpha = (jax.nn.one_hot(topk_idx, NUM_SLOTS, dtype=x.dtype) * topk_w[..., None]).sum(axis=-2)
            slot_input = jnp.einsum('bts,btd->bsd', alpha, x)
            denom = alpha.sum(axis=1) + 1e-08
            si = slot_input / denom[..., None]
            gi = si @ Wih.T + bih
            gh = S @ Whh.T + bhh
            i_r, i_z, i_n = jnp.split(gi, 3, axis=-1)
            h_r, h_z, h_n = jnp.split(gh, 3, axis=-1)
            r = jax.nn.sigmoid(i_r + h_r)
            z = jax.nn.sigmoid(i_z + h_z)
            n = jnp.tanh(i_n + r * h_n)
            S_new = (1.0 - z) * n + z * S
            q = S_new @ wq + bq
            k = S_new @ wk + bk
            v = S_new @ wv + bv
            scale = DQ ** (-0.5)
            attn = jax.nn.softmax(jnp.einsum('bsq,btq->bst', q, k) * scale, axis=-1)
            S_comm = jnp.einsum('bst,btd->bsd', attn, v)
            y = S_new + S_comm
            mu = y.mean(axis=-1, keepdims=True)
            var = y.var(axis=-1, keepdims=True)
            y = (y - mu) * jax.lax.rsqrt(var + 1e-05) * ln_g + ln_b
            slot_values = y @ wvp + bvp
            out = jnp.einsum('bts,bsd->btd', alpha, slot_values)
            return out @ wo + bo
        return _forward(x, slot_init, w1, b1, w2, b2, tau, Wih, Whh, bih, bhh, wq, bq, wk, bk, wv, bv, ln_g, ln_b, wvp, bvp, wo, bo)
    x = x + _L0_xattn_ref(_layernorm(x, axis=-1), ctx_768, L0_xattn_Wq, L0_xattn_bq, L0_xattn_Wk, L0_xattn_bk, L0_xattn_Wv, L0_xattn_bv, L0_xattn_Wo, L0_xattn_bo)
    x = x + _L0_attn_ref(_layernorm(x, axis=-1), L0_attn_Wk, L0_attn_Wq, L0_attn_Wv, L0_attn_Wo, L0_attn_bo, L0_attn_kln_g, L0_attn_kln_b, L0_attn_qln_g, L0_attn_qln_b)
    x = x + _L0_ffn_ref(_layernorm(x, axis=-1), L0_ffn_slot_init, L0_ffn_w1, L0_ffn_b1, L0_ffn_w2, L0_ffn_b2, L0_ffn_tau, L0_ffn_Wih, L0_ffn_Whh, L0_ffn_bih, L0_ffn_bhh, L0_ffn_wq, L0_ffn_bq, L0_ffn_wk, L0_ffn_bk, L0_ffn_wv, L0_ffn_bv, L0_ffn_ln_g, L0_ffn_ln_b, L0_ffn_wvp, L0_ffn_bvp, L0_ffn_wo, L0_ffn_bo)
    return x

_drawn_inputs = setup_inputs


def setup_inputs(seed=0):
    import zlib

    import numpy as np

    out = dict(_drawn_inputs(seed))
    spreads = {'L0_xattn_bq': (0.0, 0.329),
     'L0_xattn_bk': (0.0, 2.0),
     'L0_xattn_bv': (0.0, 0.1),
     'L0_xattn_bo': (0.0, 0.1),
     'L0_attn_bo': (0.0, 0.1),
     'L0_attn_kln_g': (1.0, 0.6),
     'L0_attn_kln_b': (0.0, 2.0),
     'L0_attn_qln_g': (1.0, 0.6),
     'L0_attn_qln_b': (0.0, 2.0),
     'L0_ffn_b1': (0.0, 2.0),
     'L0_ffn_b2': (0.0, 2.0),
     'L0_ffn_bih': (0.0, 0.1),
     'L0_ffn_bhh': (0.0, 0.621),
     'L0_ffn_bq': (0.0, 2.0),
     'L0_ffn_bk': (0.0, 2.0),
     'L0_ffn_bv': (0.0, 0.1),
     'L0_ffn_ln_g': (1.0, 0.6),
     'L0_ffn_ln_b': (0.0, 0.8),
     'L0_ffn_bvp': (0.0, 0.295),
     'L0_ffn_bo': (0.0, 0.1)}
    factors = {'L0_ffn_slot_init': 8.0,
     'L0_ffn_w1': 8.0,
     'L0_ffn_w2': 8.0,
     'L0_ffn_Whh': 8.0,
     'L0_ffn_wq': 64.0,
     'L0_ffn_wk': 64.0,
     'L0_ffn_wv': 4.588}
    for name, (base, spread) in spreads.items():
        noise = np.random.default_rng([zlib.crc32(name.encode()), seed]).standard_normal(out[name].shape)
        drawn = base * np.exp(spread * noise) if base else spread * noise
        out[name] = jnp.asarray(drawn.astype(out[name].dtype))
    for name, factor in factors.items():
        out[name] = (out[name] * factor).astype(out[name].dtype)
    return out
```

```python
from contextlib import ExitStack

import concourse.bass as bass
from concourse import mybir

ALU = mybir.AluOpType
ACT = mybir.ActivationFunctionType
F32 = mybir.dt.float32
BF16 = mybir.dt.bfloat16
I32 = mybir.dt.int32
AX = mybir.AxisListType

P = 128
B, T, D = 4, 256, 256
S, C = 4096, 192
H = 16
DH = D // H
NT = B * T // P
QT = T // P
NH = B * H
C2 = C - P
CH = 256
NCH = B * S // CH
KLEAD, VLEAD = 20, 16
ST = 16
CLIP = 10000.0
EPS = 1e-5
SL = 64
FH = 128
QS = D // 4
NEAR = 9800.0


def build(nc, a, out):
    with ExitStack() as ctx:
        def sb(name, shape, dt=F32):
            return ctx.enter_context(nc.sbuf_tensor(name, shape, dt))

        def psum(name):
            return ctx.enter_context(nc.psum_tensor(name, [P, 512], F32))

        def sem(name):
            return ctx.enter_context(nc.semaphore(name))

        st = [psum(f"st{n}") for n in range(3)]
        mxb = [psum(f"mx{n}") for n in range(2)]
        acc = psum("acc")
        misc = psum("misc")
        kps = psum("kps")

        x_sb = sb("x_sb", [P, NT, D])
        xn = sb("xn", [P, NT, D])
        xnT = sb("xnT", [P, 2, B * T])
        o_sb = sb("o_sb", [P, B, QT, D])
        v_sb = sb("v_sb", [P, 64, D])
        kst = sb("kst", [P, 4, S], BF16)
        qst = sb("qst", [P, 4, T], BF16)
        prob = sb("prob", [P, 8, 512])
        vh = sb("vh", [P, 2, 32, 32])
        ctxk = sb("ctxk", [P, 2, 2, CH])
        ctxv = sb("ctxv", [P, 2, 2, CH])
        wk = sb("wk", [P, 2, D])
        wv = sb("wv", [P, 2, D])
        wq = sb("wq", [P, 2, D])
        bq = sb("bq", [P, 2])
        kparts = sb("kparts", [P, 2, 3, CH], BF16)
        kres = sb("kres", [P, 2, CH])
        low = sb("low", [P, T])
        accs = sb("accs", [P, T])
        mxp = sb("mxp", [P, QT, 8])
        rowmax = sb("rowmax", [P, QT])
        shift = sb("shift", [P, QT])
        sres = sb("sres", [P, QT])
        sparts = sb("sparts", [P, QT, 3], BF16)
        flagf = sb("flagf", [P, 1])
        flag = sb("flag", [P, 1], I32)
        rcp = sb("rcp", [P, QT])
        stats = sb("stats", [P, NT, 6])
        mv = sb("mv", [P, NT, 2])
        rstd = sb("rstd", [P, NT, 2])
        ident = sb("ident", [P, P])
        identb = sb("identb", [P, P], BF16)
        gsum = sb("gsum", [P, DH + 1])
        shrow = sb("shrow", [P, P], BF16)
        negclip = sb("negclip", [P, 1])
        epsc = sb("epsc", [P, 1])

        ones = sb("ones", [1, 512])
        onescol = sb("onescol", [P, 1])
        brow = sb("brow", [1, 2880])
        slotT = sb("slotT", [P, 2, 2 * SL])
        slots = sb("slots", [P, D])
        colv = sb("colv", [P, 3, 2])
        tau = sb("tau", [P, 4])
        gb16 = sb("gb16", [DH, 4])
        spread = sb("spread", [DH, 3, P])
        gbp = sb("gbp", [P, 3, 2])
        causal = sb("causal", [P, 2, P], BF16)
        bias = {}
        at = 0
        for name, n in (("L0_xattn_bo", D), ("L0_attn_bo", D), ("L0_ffn_bih", 3 * D), ("L0_ffn_bhh", 3 * D),
                        ("L0_ffn_b1", FH), ("L0_ffn_b2", SL), ("L0_ffn_bq", QS), ("L0_ffn_bk", QS),
                        ("L0_ffn_bv", D), ("L0_ffn_bo", D)):
            bias[name] = brow[0:1, at:at + n]
            at += n

        late = v_sb[:, 0:32, :].rearrange("p t d -> p (t d)")
        wt = {}
        at = 0
        for name, c, n in (("L0_xattn_Wo", 2, D), ("attn_WkqT", 2, 2 * D), ("attn_WvT", 2, D), ("attn_WoT", 2, D),
                           ("L0_ffn_w1", 4, FH), ("L0_ffn_w2", 1, SL), ("ffn_WihT", 2, 3 * D),
                           ("ffn_WhhT", 2, 3 * D), ("L0_ffn_wq", 2, QS), ("L0_ffn_wk", 2, QS),
                           ("L0_ffn_wv", 2, D), ("L0_ffn_wvp", 2, D), ("L0_ffn_wo", 2, D)):
            wt[name] = late[:, at:at + c * n].rearrange("p (c n) -> p c n", c=c)
            at += c * n
        assert at <= 32 * D
        free_v = v_sb[:, 32:64, :].rearrange("p t d -> p (t d)")
        v2 = free_v[:, 0:2048].rearrange("p (t d) -> p t d", t=NT)
        kqc = free_v[:, 2048:6144].rearrange("p (t h d) -> p t h d", t=NT, d=DH)
        probT = free_v[:, 6144:8192].rearrange("p (n q) -> p n q", n=4)
        free_k = kst[:, :, :].rearrange("p a s -> p (a s)").bitcast(F32)
        kT = free_k[:, 0:2048].rearrange("p (g t) -> p g t", g=2)
        qeT = free_k[:, 2048:4096].rearrange("p (g t) -> p g t", g=2)
        qoT = free_k[:, 4096:6144].rearrange("p (g t) -> p g t", g=2)
        sq = free_k[:, 6144:8192].rearrange("p (t h d) -> p t h d", t=4, d=DH)
        hsum = sb("hsum", [P, NT, 2 * H])
        hvar = sb("hvar", [P, NT, 2 * H])
        hsd = sb("hsd", [P, NT, 2 * H])
        hrs = sb("hrs", [P, NT, 2 * H])
        amax = sb("amax", [P, NT, H])
        asum = sb("asum", [P, NT, H])
        arcp = sb("arcp", [P, NT, H])
        hT = kqc.rearrange("p t h d -> p (t h d)")[:, 0:1024]
        lg = kqc.rearrange("p t h d -> p (t h d)")[:, 1024:1536].rearrange("p (t s) -> p t s", t=NT)
        lrep = kqc.rearrange("p t h d -> p (t h d)")[:, 1536:2048].rearrange("p (t s) -> p t s", t=NT)
        lmask = kqc.rearrange("p t h d -> p (t h d)")[:, 2048:2560].rearrange("p (t s) -> p t s", t=NT)
        lsub = kqc.rearrange("p t h d -> p (t h d)")[:, 2560:3072].rearrange("p (t s) -> p t s", t=NT)
        alpha = kqc.rearrange("p t h d -> p (t h d)")[:, 3072:3584].rearrange("p (t s) -> p t s", t=NT)
        lexp = kqc.rearrange("p t h d -> p (t h d)")[:, 3584:4096].rearrange("p (t s) -> p t s", t=NT)
        si = v2.rearrange("p t d -> p (t d)")[:, 0:512].rearrange("p (r d) -> p r d", r=2)
        siT = v2.rearrange("p t d -> p (t d)")[:, 512:1024].rearrange("p (c s) -> p c s", c=2)
        rz = v2.rearrange("p t d -> p (t d)")[:, 1024:2048].rearrange("p (r d) -> p r d", r=2)
        pT = probT.rearrange("p n q -> p (n q)")
        cand = pT[:, 0:512].rearrange("p (r d) -> p r d", r=2)
        snew = pT[:, 512:1024].rearrange("p (r d) -> p r d", r=2)
        snT = pT[:, 1024:1536].rearrange("p (c s) -> p c s", c=2)
        yT = pT[:, 1536:2048].rearrange("p (c s) -> p c s", c=2)
        fk = kT.rearrange("p g t -> p (g t)")
        qkT = fk[0:SL, 0:512].rearrange("p (n s) -> p n s", n=2)
        v4 = fk[0:SL, 512:1536].rearrange("p (b d) -> p b d", b=B)
        att = fk[:, 1536:1664].rearrange("p (r s) -> p r s", r=2)
        attT = fk[0:SL, 1664:1920].rearrange("p (r s) -> p r s", r=2)
        fq = qeT.rearrange("p g t -> p (g t)")
        y = fq[:, 0:512].rearrange("p (r d) -> p r d", r=2)
        svT = fq[:, 512:1024].rearrange("p (c s) -> p c s", c=2)
        svo = fq[0:SL, 1024:2048].rearrange("p (b d) -> p b d", b=B)
        alphaT = qoT.rearrange("p g t -> p (g t)")[0:SL, 0:1024].rearrange("p (t q) -> p t q", t=NT)
        cvec = sb("cvec", [P, 1])
        smean = sb("smean", [P, 2, 2])
        top8 = sb("top8", [P, NT, 8])
        lsum = sb("lsum", [P, NT, 2])
        den = sb("den", [P, 2, 3])
        smx = sb("smx", [P, 2, 4])

        kq = kst[:, :, :].rearrange("p a s -> p (a s)")
        q_sb = kq[:, 0:4096].bitcast(F32).rearrange("p (g t) -> p g t", g=2)
        qres = kq[:, 4096:8192].bitcast(F32).rearrange("p (g t) -> p g t", g=2)
        q1 = kq[:, 8192:10240].rearrange("p (g t) -> p g t", g=2)
        q2 = kq[:, 10240:12288].rearrange("p (g t) -> p g t", g=2)
        q3 = kq[:, 12288:14336].rearrange("p (g t) -> p g t", g=2)

        kscr = nc.dram_tensor("kscr", [D, 3, B * S], BF16, kind="Internal").ap()
        qscr1 = nc.dram_tensor("qscr1", [D, 3, B * T], BF16, kind="Internal").ap()
        qscr2 = nc.dram_tensor("qscr2", [D, B * T], BF16, kind="Internal").ap()
        qscr3 = nc.dram_tensor("qscr3", [D, B * T], BF16, kind="Internal").ap()

        x_in, w_in, bq_in = sem("x_in"), sem("w_in"), sem("bq_in")
        consts, rest_set = sem("consts"), sem("rest_set")
        ln_st, ln_ag, ln_sq, ln_rc, ln_xn = (sem(f"ln_{n}") for n in ("stats", "aggr", "sqrt", "recip", "out"))
        xnT_ps, xnT_act, xnT_dve = sem("xnT_ps"), sem("xnT_act"), sem("xnT_dve")
        q_ps, q_full, q_1, q_r1, q_2, q_3 = (sem(f"q_{n}") for n in ("ps", "full", "1", "r1", "2", "3"))
        qscr_w = sem("qscr_written")
        rows_set, ones_set = sem("rows_set"), sem("ones_set")
        ctxk_in = [sem(f"ctxk_in{n}") for n in range(2)]
        ctxv_in = [sem(f"ctxv_in{n}") for n in range(2)]
        k_ps, k_1, k_r, k_2, k_3, kscr_w = (sem(f"k_{n}") for n in ("ps", "1", "res", "2", "3", "written"))
        v_ps, v_out = sem("v_ps"), sem("v_out")
        stacks_in = [sem(f"stacks_in{n}") for n in range(4)]
        vh_ready = sem("vh_ready")
        max_ps, max_red = sem("max_ps"), sem("max_red")
        m_row, m_clip, m_1, m_res, m_2, m_3 = (sem(f"m_{n}") for n in ("row", "clip", "1", "res", "2", "3"))
        shift_ps, shift_set, flag_abs, flag_set = (sem(n) for n in ("shift_ps", "shift_set", "flag_abs", "flag_set"))
        low_ps, low_set = sem("low_ps"), sem("low_set")
        st_ps, exp_done, clip_step, clip_done = (sem(n) for n in ("st_ps", "exp_done", "clip_step", "clip_done"))
        pv_done, acc_out, fin_ps, fin_rcp, head_out = (
            sem(n) for n in ("pv_done", "acc_out", "fin_ps", "fin_rcp", "head_out"))
        stored = sem("stored")
        rows_in, late_in, small_in = sem("rows_in"), sem("late_in"), sem("small_in")
        gb_ps, gb_out = sem("gb_ps"), sem("gb_out")
        out_ps, x_new = sem("out_ps"), sem("x_new")
        kq_ps, kq_sum, kq_c, kq_sq, kq_var, kq_sd, kq_rs, kq_n = (
            sem(f"kq_{n}") for n in ("ps", "sum", "centred", "square", "var", "sd", "rs", "normed"))
        v2_ps, v2_out = sem("v2_ps"), sem("v2_out")
        kqT_ps, kT_out, qT_out = sem("kqT_ps"), sem("kT_out"), sem("qT_out")
        a_ps, a_max, a_exp, pT_ps, pT_out, o2_ps, o2_rc, o2_out = (
            sem(f"a_{n}") for n in ("ps", "max", "exp", "pT_ps", "pT_out", "o_ps", "o_recip", "o_out"))
        sm_a, sm_out, cv_ps, cv_out, tau_a, tau_out = (
            sem(n) for n in ("sm_sum", "sm_out", "cv_ps", "cv_out", "tau_abs", "tau_out"))
        h_ps, h_out, lg_ps, lg_out, l_top, l_rep, l_mask, l_sub, l_exp, l_al, l_sum, l_rc, l_out = (
            sem(f"l_{n}") for n in ("h_ps", "h", "ps", "logits", "top", "replaced", "mask", "sub", "exp", "masked",
                                    "sum", "recip", "alpha"))
        si_ps, si_den, si_rc, si_out, siT_ps, siT_out = (
            sem(f"si_{n}") for n in ("ps", "den", "recip", "out", "T_ps", "T_out"))
        g_ps, g_rz, g_rh, g_sum, g_n, g_d, g_zd, g_new = (
            sem(f"g_{n}") for n in ("ps", "rz", "rh", "sum", "cand", "diff", "zdiff", "new"))
        snT_ps, snT_out, qk_ps, qk_out, v4_ps, v4_out = (
            sem(n) for n in ("snT_ps", "snT_out", "qk_ps", "qk_out", "v4_ps", "v4_out"))
        c_ps, c_max, c_sub, c_exp, c_sum, c_rc, c_out, cT_ps, cT_out, cm_ps, y_out = (
            sem(f"c_{n}") for n in ("ps", "max", "sub", "exp", "sum", "recip", "att", "attT_ps", "attT", "comm", "y"))
        y_st, y_ag, y_sd, y_rs, y_n, yT_ps, yT_out, sv_ps, sv_out, svo_ps, svo_out, alT_ps, alT_out = (
            sem(f"y_{n}") for n in ("stats", "aggr", "sd", "recip", "normed", "T_ps", "T_out", "sv_ps", "sv",
                                    "svo_ps", "svo", "alphaT_ps", "alphaT"))

        passed = {nc.sync: sem("sp_passed"), nc.gpsimd: sem("pool_passed")}

        block = ctx.enter_context(nc.Block())

        def wait(eng, s, value):
            if not (isinstance(value, int) and value <= 0):
                eng.wait_ge(s, value)

        def wait_alone(eng, s, value):
            wait(eng, s, value)
            if not isinstance(value, int):
                eng.sem_inc(passed[eng], 1)

        @block.sync
        def _(sp):
            sp.dma_start(x_sb[:, :, :], a["x"].rearrange("b (q p) d -> p (b q) d", p=P)).then_inc(x_in, 16)
            sp.dma_start(wq[:, :, :], a["L0_xattn_Wq"].rearrange("(c p) n -> p c n", p=P)).then_inc(w_in, 16)
            for w, name, row in ((wk, "L0_xattn_Wk", "L0_xattn_bk"), (wv, "L0_xattn_Wv", "L0_xattn_bv")):
                sp.dma_start(w[:, 0, :], a[name][0:P, :]).then_inc(w_in, 16)
                sp.dma_start(w[0:C2, 1, :], a[name][P:C, :]).then_inc(w_in, 16)
                sp.dma_start(w[C2:C2 + 1, 1, :], a[row].rearrange("(o n) -> o n", o=1)).then_inc(w_in, 16)
            with nc.allow_non_contiguous_dma("256 biases onto partitions"):
                sp.dma_start(bq[:, :], a["L0_xattn_bq"].rearrange("(g p) -> p g", p=P)).then_inc(bq_in, 16)

            for name, row in bias.items():
                sp.dma_start(row, a[name].rearrange("(o n) -> o n", o=1)).then_inc(rows_in, 16)
            for n in range(2):
                sp.dma_start(slots[n * SL:(n + 1) * SL, :], a["L0_ffn_slot_init"]).then_inc(small_in, 16)
                sp.dma_start(slotT[:, :, n * SL:(n + 1) * SL],
                             a["ffn_slotT"].rearrange("(c p) s -> p c s", p=P)).then_inc(small_in, 16)
            sp.dma_start(tau[:, 0:1], a["L0_ffn_tau"].rearrange("(o n) -> o n", o=1).to_broadcast([P, 1])).then_inc(small_in, 16)
            with nc.allow_non_contiguous_dma("short vectors onto partitions"):
                for n, name in enumerate(("L0_attn_kln_g", "L0_attn_kln_b", "L0_attn_qln_g", "L0_attn_qln_b")):
                    sp.dma_start(gb16[:, n:n + 1], a[name].rearrange("(p o) -> p o", o=1)).then_inc(small_in, 16)
                for n, name in enumerate(("L0_ffn_ln_g", "L0_ffn_ln_b", "L0_ffn_bvp")):
                    sp.dma_start(colv[:, n, :], a[name].rearrange("(c p) -> p c", p=P)).then_inc(small_in, 16)

            def load_ctx(dst, slot, done, c):
                src = a["ctxT"][bass.ds(c, 1), :, :].rearrange("o c t -> (o c) t")
                sp.dma_start(dst[:, slot, 0, :], src[0:P, :]).then_inc(done, 16)
                sp.dma_start(dst[0:C2, slot, 1, :], src[P:C, :]).then_inc(done, 16)

            def write_k(c):
                wait_alone(sp, k_3, c + 1)
                for g in range(2):
                    sp.dma_start(kscr[g * P:(g + 1) * P, :, bass.ds(c * CH, CH)],
                                 kparts[:, g, :, :]).then_inc(kscr_w, 16)

            def load_stacks(b, h, slot):
                done = stacks_in[slot]
                rows, cols = bass.ds(h * DH, DH), bass.ds(b * S, S)
                sp.dma_start(kst[0:48, slot, :], kscr[rows, :, cols].rearrange("d r t -> (d r) t")).then_inc(done, 16)
                for n, r in enumerate((0, 1, 0)):
                    sp.dma_start(kst[48 + 16 * n:64 + 16 * n, slot, :],
                                 kscr[rows, r:r + 1, cols].rearrange("d r t -> (d r) t")).then_inc(done, 16)
                cols = bass.ds(b * T, T)
                sp.dma_start(qst[0:48, slot, :], qscr1[rows, :, cols].rearrange("d r t -> (d r) t")).then_inc(done, 16)
                for n, scr in enumerate((qscr2, qscr2, qscr3)):
                    sp.dma_start(qst[48 + 16 * n:64 + 16 * n, slot, :], scr[rows, cols]).then_inc(done, 16)

            load_ctx(ctxk, 0, ctxk_in[0], 0)
            load_ctx(ctxk, 1, ctxk_in[1], 1)
            sp.wait_ge(q_1, 1)
            for g in range(2):
                for r in range(3):
                    sp.dma_start(qscr1[g * P:(g + 1) * P, r, :], q1[:, g, :]).then_inc(qscr_w, 16)
            sp.wait_ge(q_2, 1)
            for g in range(2):
                sp.dma_start(qscr2[g * P:(g + 1) * P, :], q2[:, g, :]).then_inc(qscr_w, 16)
            sp.wait_ge(q_3, 1)
            for g in range(2):
                sp.dma_start(qscr3[g * P:(g + 1) * P, :], q3[:, g, :]).then_inc(qscr_w, 16)

            def early_job(c, slot):
                write_k(c)
                wait_alone(sp, k_ps, c + 1)
                wait_alone(sp, v_ps, c + 1)
                load_ctx(ctxk, slot, ctxk_in[slot], c + 2)
                wait_alone(sp, kscr_w, 32 * c + 32)

            with sp.Fori(0, VLEAD // 2, 1) as n:
                early_job(2 * n, 0)
                early_job(2 * n + 1, 1)
            for c in range(VLEAD, KLEAD):
                write_k(c)
                wait_alone(sp, k_ps, c + 1)
                load_ctx(ctxk, c % 2, ctxk_in[c % 2], c + 2)
                wait_alone(sp, kscr_w, 32 * c + 32)
            load_ctx(ctxv, 0, ctxv_in[0], VLEAD)
            load_ctx(ctxv, 1, ctxv_in[1], VLEAD + 1)
            sp.wait_ge(qscr_w, 160)
            load_stacks(0, 0, 0)
            load_stacks(0, 1, 1)

            def head(it, u, k_job, v_job, ahead):
                i = it * 4 + u
                if k_job:
                    write_k(i + KLEAD)
                    wait_alone(sp, k_ps, i + KLEAD + 1)
                    if k_job != "last" or u < 2:
                        load_ctx(ctxk, u % 2, ctxk_in[u % 2], i + KLEAD + 2)
                    wait_alone(sp, kscr_w, 32 * (i + KLEAD + 1))
                if v_job:
                    wait_alone(sp, v_ps, i + VLEAD + 1)
                    if v_job != "last" or u < 2:
                        load_ctx(ctxv, u % 2, ctxv_in[u % 2], i + VLEAD + 2)
                if ahead:
                    j = it * 4 + u + 2
                    wait_alone(sp, st_ps, ST * (i - 1))
                    if isinstance(it, int):
                        load_stacks(j // H, j % H, j % 4)
                    else:
                        load_stacks(j // H, j % H, (u + 2) % 4)

            for u in range(4):
                head(0, u, True, True, True)
            with sp.Fori(1, 10, 1) as it:
                for u in range(4):
                    head(it, u, True, True, True)
            for u in range(4):
                head(10, u, "last", True, True)
            for u in range(4):
                head(11, u, False, "last", True)
            for u in range(4):
                head(12, u, False, False, True)
            sp.wait_ge(vh_ready, 3 * H + 1)
            for name, dst in wt.items():
                sp.dma_start(dst, a[name].rearrange("(c p) n -> p c n", p=P)).then_inc(late_in, 16)
            with sp.Fori(13, 15, 1) as it:
                for u in range(4):
                    head(it, u, False, False, True)
            for u in range(2):
                head(15, u, False, False, True)
            for n in range(4):
                sp.wait_ge(x_new, 8 + n + 1)
                sp.dma_start(out[n].rearrange("(q p) d -> p q d", p=P), x_sb[:, 2 * n:2 * n + 2, :]).then_inc(stored, 16)
            sp.wait_ge(stored, 16 * 4)

        @block.gpsimd
        def _(pool):
            pool.memset(ident[:, :], 0.0).then_inc(consts, 1)
            pool.memset(identb[:, :], 0.0).then_inc(consts, 1)
            pool.memset(gsum[:, :], 0.0).then_inc(consts, 1)
            pool.memset(vh[:, :, :, :], 0.0).then_inc(consts, 1)
            pool.memset(negclip[:, :], -CLIP).then_inc(consts, 1)
            pool.memset(epsc[:, :], EPS).then_inc(consts, 1)
            pool.wait_ge(consts, 6)
            for m in (ident, identb):
                pool.affine_select(out=m[:, :], in_=m[:, :], compare_op=ALU.not_equal, fill=1.0, base=0,
                                   pattern=[[-1, P]], channel_multiplier=1).then_inc(consts, 1)
            for g in range(4):
                pool.wait_ge(consts, 8 + g)
                pool.affine_select(out=gsum[:, :], in_=gsum[:, :], compare_op=ALU.not_equal, fill=1.0,
                                   base=-32 * g, pattern=[[-1, DH + 1]], channel_multiplier=1).then_inc(consts, 1)
            pool.memset(vh[:, :, :, DH:DH + 1], 1.0).then_inc(consts, 1)
            pool.memset(ones[:, :], 1.0).then_inc(rest_set, 1)
            pool.memset(onescol[:, :], 1.0).then_inc(rest_set, 1)
            pool.memset(spread[:, :, :], 0.0).then_inc(rest_set, 1)
            pool.memset(causal[:, :, :], 0.0).then_inc(rest_set, 1)
            pool.wait_ge(rest_set, 4)
            for n, (rep, width, base) in enumerate(((8, DH, 0), (4, 2 * DH, 0), (4, 2 * DH, DH))):
                pool.affine_select(out=spread[:, n, :].rearrange("d (r c) -> d r c", r=rep),
                                   in_=spread[:, n, :].rearrange("d (r c) -> d r c", r=rep),
                                   compare_op=ALU.not_equal, fill=1.0, base=base, pattern=[[0, rep], [-1, width]],
                                   channel_multiplier=1).then_inc(rest_set, 1)
            pool.affine_select(out=causal[:, 1, :], in_=causal[:, 1, :], compare_op=ALU.is_ge, fill=-1e30,
                               base=0, pattern=[[-1, P]], channel_multiplier=1).then_inc(rest_set, 1)

            def k_split(c):
                wait_alone(pool, k_r, c + 1)
                pool.tensor_copy(kparts[:, :, 1, :], kres[:, :, :]).then_inc(k_2, 1)
                wait_alone(pool, k_2, c + 1)
                pool.tensor_tensor(kparts[:, :, 2, :], kres[:, :, :], kparts[:, :, 1, :],
                                   ALU.subtract).then_inc(k_3, 1)

            def copy_vh(slot, half, h, i):
                pool.tensor_copy(vh[:, slot, :, 0:DH],
                                 v_sb[:, bass.ds(half * 32, 32), bass.ds(h * DH, DH)]).then_inc(vh_ready, 1)

            pool.wait_ge(x_in, 16)
            k_split(0)
            with pool.Fori(1, KLEAD, 1) as c:
                k_split(c)
            pool.wait_ge(v_out, VLEAD)
            pool.wait_ge(consts, 13)
            copy_vh(0, 0, 0, 0)

            def head(it, u, k_job, v_job, ahead):
                i = it * 4 + u
                if k_job:
                    k_split(i + KLEAD)
                wait_alone(pool, flag_set, i + 1)
                clipping = pool.value_load(flag[96:97, 0:1])
                with pool.If(clipping != 0):
                    with pool.Fori(0, ST // 8, 1) as half:
                        for s in range(8):
                            n = i * ST + half * 8 + s
                            p = prob[:, s, :].rearrange("p (n q) -> p n q", n=2)
                            bound = low[:, :].unsqueeze(1).to_broadcast([P, 2, T])
                            wait_alone(pool, exp_done, n + 1)
                            pool.tensor_scalar(p, p, 1.0, None, ALU.min).then_inc(clip_step, 1)
                            wait_alone(pool, low_set, i + 1)
                            wait_alone(pool, clip_step, 3 * n + 1)
                            pool.tensor_tensor(p, p, bound, ALU.subtract).then_inc(clip_step, 1)
                            wait_alone(pool, clip_step, 3 * n + 2)
                            pool.tensor_scalar(p, p, 0.0, None, ALU.max).then_inc(clip_step, 1)
                            wait_alone(pool, clip_step, 3 * n + 3)
                            pool.tensor_tensor(p, p, bound, ALU.add).then_inc(clip_done, 1)
                with pool.Else():
                    pool.sem_inc(clip_step, 3 * ST)
                    pool.sem_inc(clip_done, ST)
                if ahead:
                    wait_alone(pool, v_out, i + VLEAD + 1 if v_job else NCH)
                    wait_alone(pool, pv_done, 8 * i)
                    copy_vh((u + 1) % 2, ((i + 1) // H) % 2, (i + 1) % H, i + 1)

            for u in range(4):
                head(0, u, True, True, True)
            with pool.Fori(1, 11, 1) as it:
                for u in range(4):
                    head(it, u, True, True, True)
            for u in range(4):
                head(11, u, False, True, True)
            with pool.Fori(12, 15, 1) as it:
                for u in range(4):
                    head(it, u, False, False, True)
            for u in range(4):
                head(15, u, False, False, u < 3)

        @block.scalar
        def _(act):
            def norm_sd(k):
                act.wait_ge(ln_ag, NT * (k + 1))
                act.activation(rstd[:, :, 0], mv[:, :, 1], ACT.Sqrt, bias=epsc[:, :]).then_inc(ln_sq, 1)

            def turned(k):
                for n in range(2):
                    act.wait_ge(xnT_ps, 4 * k + n + 1)
                    act.activation(xnT[:, 0, n * 512:(n + 1) * 512], st[n][:, :], ACT.Copy).then_inc(xnT_act, 1)

            act.wait_ge(consts, 13)
            norm_sd(0)
            turned(0)
            act.wait_ge(q_full, 4)
            act.activation(q1, q_sb, ACT.Copy).then_inc(q_1, 1)

            def k_first(c):
                wait(act, k_ps, c + 1)
                wait(act, kscr_w, 32 * c)
                act.activation(kparts[:, :, 0, :], kps[:, :].rearrange("p (g t) -> p g t", g=2),
                               ACT.Copy).then_inc(k_1, 1)

            def v_copy(bank, c):
                wait(act, v_ps, c + 1)
                act.activation(v_sb[:, bass.ds((c * 2) % 64, 2), :].rearrange("p n d -> p (n d)"),
                               bank[:, :], ACT.Copy).then_inc(v_out, 1)

            k_first(0)
            v_copy(mxb[1], 0)
            with act.Fori(1, VLEAD, 1) as c:
                k_first(c)
                v_copy(mxb[1], c)
            for c in range(VLEAD, KLEAD):
                k_first(c)

            def head(it, u, k_job, v_job):
                i = it * 4 + u
                if k_job:
                    k_first(i + KLEAD)
                if v_job:
                    v_copy(mxb[1], i + VLEAD)
                wait(act, low_ps, i + 1)
                wait(act, clip_done, ST * i)
                act.activation(low[:, :], misc[:, 0:T], ACT.Exp, bias=negclip[:, :]).then_inc(low_set, 1)
                for s in range(ST):
                    wait(act, st_ps, i * ST + s + 1)
                    if s % 2 == 0:
                        wait(act, pv_done, i * 8 + s // 2 - 3)
                    act.activation(prob[:, s % 8, :], st[s % 3][:, :], ACT.Exp).then_inc(exp_done, 1)

            for u in range(4):
                head(0, u, True, True)
            with act.Fori(1, 11, 1) as it:
                for u in range(4):
                    head(it, u, True, True)
            for u in range(4):
                head(11, u, False, True)
            with act.Fori(12, 16, 1) as it:
                for u in range(4):
                    head(it, u, False, False)

            act.wait_ge(head_out, NH)
            turned(1)
            norm_sd(1)
            turned(2)
            for n in range(4):
                act.wait_ge(v2_ps, n + 1)
                act.activation(v2[:, 2 * n:2 * n + 2, :].rearrange("p t d -> p (t d)"),
                               (mxb[1], acc, misc, kps)[n][:, :], ACT.Copy).then_inc(v2_out, 1)
            for t in range(NT):
                act.wait_ge(kq_c, t + 1)
                if t >= 4:
                    act.wait_ge(kq_var, t - 3)
                act.activation(sq[:, t % 4, :, :], kqc[:, t, :, :], ACT.Square).then_inc(kq_sq, 1)
            act.wait_ge(kq_var, NT)
            act.activation(hsd[:, :, :], hvar[:, :, :], ACT.Sqrt, bias=epsc[:, :], scale=1.0 / DH).then_inc(kq_sd, 1)
            act.wait_ge(gb_out, 1)
            for m in range(4):
                act.wait_ge(kqT_ps, 2 * m + 2)
                for e in range(2):
                    act.activation((qeT, qoT)[e][:, :, m * T:(m + 1) * T],
                                   (st[2], mxb[0])[m % 2][:, :].rearrange("p (g t) -> p g t", g=2), ACT.Identity,
                                   bias=gbp[:, 1 + e, 1:2], scale=gbp[:, 1 + e, 0:1]).then_inc(qT_out, 1)
            for n in range(64):
                u, j = n // 4, n % 4
                b, qt, g = u // 4, (u // 2) % 2, u % 2
                w = P * (qt + 1)
                act.wait_ge(a_max, n + 1)
                if n >= 8:
                    act.wait_ge(pT_ps, n - 7)
                for e in range(2):
                    h = 8 * g + 2 * j + e
                    act.activation(prob[:, n % 8, e * w:(e + 1) * w], (mxb[1], acc, misc, kps)[j][:, e * w:(e + 1) * w],
                                   ACT.Exp, bias=amax[:, 2 * b + qt, h:h + 1],
                                   accum_out=asum[:, 2 * b + qt, h:h + 1]).then_inc(a_exp, 1)
            turned(3)
            norm_sd(2)
            turned(4)

            act.wait_ge(cv_out, 1)
            for n in range(2):
                act.wait_ge(h_ps, n + 1)
                act.activation(hT[:, n * 512:(n + 1) * 512], (mxb[1], acc)[n][:, :], ACT.Gelu,
                               bias=cvec[:, :]).then_inc(h_out, 1)
            act.wait_ge(l_sub, 1)
            act.activation(lexp, lsub, ACT.Exp).then_inc(l_exp, 1)
            for n in range(2):
                act.wait_ge(alT_ps, n + 1)
                act.activation(alphaT[:, 4 * n:4 * n + 4, :].rearrange("p t q -> p (t q)"),
                               (mxb[1], acc)[n][0:SL, :], ACT.Copy).then_inc(alT_out, 1)
            for r in range(2):
                act.wait_ge(g_ps, r + 1)
                act.activation(rz[:, r, :], (mxb[0], kps)[r][:, :], ACT.Sigmoid).then_inc(g_rz, 1)
            for r in range(2):
                act.wait_ge(g_sum, r + 1)
                act.activation(cand[:, r, :], snew[:, r, :], ACT.Tanh).then_inc(g_n, 1)
            for n in range(2):
                act.wait_ge(v4_ps, n + 1)
                act.activation(v4[:, 2 * n:2 * n + 2, :].rearrange("p b d -> p (b d)"),
                               (mxb[1], acc)[n][0:SL, :], ACT.Copy).then_inc(v4_out, 1)
            act.wait_ge(c_sub, 1)
            act.activation(att, att, ACT.Exp).then_inc(c_exp, 1)
            act.wait_ge(y_ag, 2)
            act.activation(rstd[:, 0:2, 0], mv[:, 0:2, 1], ACT.Sqrt, bias=epsc[:, :]).then_inc(y_sd, 1)
            for n in range(2):
                act.wait_ge(svo_ps, n + 1)
                act.activation(svo[:, 2 * n:2 * n + 2, :].rearrange("p b d -> p (b d)"),
                               (mxb[1], acc)[n][0:SL, :], ACT.Copy).then_inc(svo_out, 1)

        @block.vector
        def _(dve):
            dve.memset(ctxk[C2:C2 + 1, :, 1, :], 1.0).then_inc(rows_set, 1)
            dve.memset(ctxv[C2:C2 + 1, :, 1, :], 1.0).then_inc(rows_set, 1)
            dve.memset(shrow[:, :], 0.0).then_inc(rows_set, 1)
            dve.wait_ge(rows_set, 3)
            dve.memset(shrow[96:99, :], 1.0).then_inc(rows_set, 1)
            dve.wait_ge(x_in, 16)
            def norm(k):
                for j in range(NT):
                    if k > 0 and j % 2 == 0:
                        dve.wait_ge(x_new, 4 * (k - 1) + j // 2 + 1)
                    dve.bn_stats(stats[:, j, :], x_sb[:, j, :]).then_inc(ln_st, 1)
                for j in range(NT):
                    dve.wait_ge(ln_st, NT * k + j + 1)
                    dve.bn_aggr(mv[:, j, :], stats[:, j, :]).then_inc(ln_ag, 1)
                dve.wait_ge(ln_sq, k + 1)
                dve.reciprocal(rstd[:, :, 1], rstd[:, :, 0]).then_inc(ln_rc, 1)
                dve.wait_ge(ln_rc, k + 1)
                for j in range(NT):
                    dve.tensor_scalar(xn[:, j, :], x_sb[:, j, :], mv[:, j, 0:1], rstd[:, j, 1:2],
                                      ALU.subtract, ALU.mult).then_inc(ln_xn, 1)

            def turned(k):
                for n in range(2):
                    dve.wait_ge(xnT_ps, 4 * k + n + 3)
                    dve.tensor_copy(xnT[:, 1, n * 512:(n + 1) * 512], (st[2], mxb[0])[n][:, :]).then_inc(xnT_dve, 1)

            norm(0)
            turned(0)
            dve.wait_ge(bq_in, 16)
            for n in range(4):
                g, half = n // 2, n % 2
                dve.wait_ge(q_ps, n + 1)
                dve.tensor_scalar(q_sb[:, g, half * 512:(half + 1) * 512], (mxb[1], acc, misc, kps)[n][:, :],
                                  bq[:, g:g + 1], DH ** -0.5, ALU.add, ALU.mult).then_inc(q_full, 1)
            dve.wait_ge(q_1, 1)
            dve.wait_ge(q_full, 4)
            dve.tensor_tensor(qres, q_sb, q1, ALU.subtract).then_inc(q_r1, 1)
            dve.wait_ge(q_r1, 1)
            dve.tensor_copy(q2, qres).then_inc(q_2, 1)
            dve.wait_ge(q_2, 1)
            dve.tensor_tensor(q3, qres, q2, ALU.subtract).then_inc(q_3, 1)

            def k_rest(c):
                wait(dve, k_1, c + 1)
                wait(dve, k_3, c)
                dve.tensor_tensor(kres[:, :, :].rearrange("p g t -> p (g t)").rearrange("p (g t) -> p g t", g=2),
                                  kps[:, :].rearrange("p (g t) -> p g t", g=2), kparts[:, :, 0, :],
                                  ALU.subtract).then_inc(k_r, 1)

            def reduce_step(j, s):
                wait(dve, max_ps, j * ST + s + 1)
                dve.reduce_max(mxp[:, s // 8, s % 8:s % 8 + 1], mxb[s % 2][:, :], AX.X).then_inc(max_red, 1)

            k_rest(0)
            with dve.Fori(1, KLEAD, 1) as c:
                k_rest(c)
            dve.wait_ge(qscr_w, 160)
            dve.memset(kst[96:99, :, :], 1.0).then_inc(ones_set, 1)
            for s in range(ST):
                reduce_step(0, s)

            def normalise(i):
                wait(dve, fin_ps, i + 1)
                done = misc[:, 0:64].rearrange("p (q d) -> p q d", q=2)
                dve.reciprocal(rcp[:, :], done[:, :, DH]).then_inc(fin_rcp, 1)
                wait(dve, fin_rcp, i + 1)
                dve.tensor_tensor(o_sb[:, bass.ds(i // H, 1), :, bass.ds(i % H * DH, DH)]
                                  .rearrange("p o q d -> p (o q) d"), done[:, :, 0:DH],
                                  rcp[:, :].unsqueeze(2).to_broadcast([P, QT, DH]), ALU.mult).then_inc(head_out, 1)

            def save_acc(i):
                wait(dve, pv_done, 8 * (i + 1))
                wait(dve, fin_ps, i)
                dve.tensor_copy(accs[:, :], acc[:, 0:T]).then_inc(acc_out, 1)

            def head(it, u, k_job, ahead):
                i = it * 4 + u
                wait(dve, max_red, (i + 1) * ST)
                dve.reduce_max(rowmax[:, :], mxp[:, :, :], AX.X).then_inc(m_row, 1)
                wait(dve, m_row, i + 1)
                dve.tensor_scalar(shift[:, :], rowmax[:, :], CLIP, -CLIP, ALU.min, ALU.max).then_inc(m_clip, 1)
                wait(dve, m_clip, i + 1)
                wait(dve, shift_ps, i)
                dve.tensor_scalar(sparts[:, :, 0], shift[:, :], -1.0, None, ALU.mult).then_inc(m_1, 1)
                wait(dve, m_1, i + 1)
                dve.scalar_tensor_tensor(sres[:, :], shift[:, :], -1.0, sparts[:, :, 0],
                                         ALU.mult, ALU.subtract).then_inc(m_res, 1)
                wait(dve, m_res, i + 1)
                dve.tensor_copy(sparts[:, :, 1], sres[:, :]).then_inc(m_2, 1)
                wait(dve, m_2, i + 1)
                dve.tensor_tensor(sparts[:, :, 2], sres[:, :], sparts[:, :, 1], ALU.subtract).then_inc(m_3, 1)
                wait(dve, shift_ps, i + 1)
                dve.tensor_copy(qst[96:99, u, :], misc[96:99, 0:T]).then_inc(shift_set, 1)
                dve.tensor_reduce(flagf[96:97, :], misc[96:97, 0:T], AX.X, ALU.max,
                                  apply_absolute_value=True).then_inc(flag_abs, 1)
                wait(dve, flag_abs, i + 1)
                wait(dve, clip_done, ST * i)
                dve.tensor_scalar(flag[96:97, :], flagf[96:97, :], NEAR, None, ALU.is_gt).then_inc(flag_set, 1)
                if not (isinstance(it, int) and i == 0):
                    save_acc(i - 1)
                if k_job:
                    k_rest(i + KLEAD)
                for s in range(ST):
                    if ahead:
                        reduce_step(i + 1, s)
                    if s == 7 and not (isinstance(it, int) and i == 0):
                        normalise(i - 1)

            for u in range(4):
                head(0, u, True, True)
            with dve.Fori(1, 11, 1) as it:
                for u in range(4):
                    head(it, u, True, True)
            with dve.Fori(11, 15, 1) as it:
                for u in range(4):
                    head(it, u, False, True)
            for u in range(4):
                head(15, u, False, u < 3)
            save_acc(NH - 1)
            normalise(NH - 1)

            def add_out(k, banks):
                for n in range(4):
                    dve.wait_ge(out_ps, 4 * k + n + 1)
                    xs = x_sb[:, 2 * n:2 * n + 2, :].rearrange("p t d -> p (t d)")
                    dve.tensor_tensor(xs, xs, banks[n][:, :], ALU.add).then_inc(x_new, 1)

            four = (mxb[1], acc, misc, kps)
            turned(1)
            add_out(0, four)
            norm(1)
            dve.wait_ge(gb_ps, 1)
            dve.tensor_scalar(gbp[:, :, :].rearrange("p n k -> p (n k)"), misc[:, 0:6], D ** -0.25, None,
                              ALU.mult).then_inc(gb_out, 1)
            turned(2)
            ring = (st[0], st[1], st[2], mxb[0])
            for t in range(NT):
                kq = ring[t % 4][:, :].rearrange("p (h d) -> p h d", d=DH)
                dve.wait_ge(kq_ps, t + 1)
                dve.reduce_sum(hsum[:, t, :], kq, AX.X).then_inc(kq_sum, 1)
                dve.wait_ge(kq_sum, t + 1)
                dve.scalar_tensor_tensor(kqc[:, t, :, :], hsum[:, t, :].unsqueeze(2).to_broadcast([P, 2 * H, DH]),
                                         -1.0 / DH, kq, ALU.mult, ALU.add).then_inc(kq_c, 1)
            for t in range(NT):
                dve.wait_ge(kq_sq, t + 1)
                dve.reduce_sum(hvar[:, t, :], sq[:, t % 4, :, :], AX.X).then_inc(kq_var, 1)
            dve.wait_ge(kq_sd, 1)
            dve.reciprocal(hrs[:, :, :], hsd[:, :, :]).then_inc(kq_rs, 1)
            dve.wait_ge(kq_rs, 1)
            for t in range(NT):
                dve.tensor_tensor(kqc[:, t, :, :], kqc[:, t, :, :],
                                  hrs[:, t, :].unsqueeze(2).to_broadcast([P, 2 * H, DH]), ALU.mult).then_inc(kq_n, 1)
            dve.wait_ge(gb_out, 1)
            for m in range(4):
                dve.wait_ge(kqT_ps, 2 * m + 1)
                dve.tensor_scalar(kT[:, :, m * T:(m + 1) * T], ring[m % 2][:, :].rearrange("p (g t) -> p g t", g=2),
                                  gbp[:, 0, 0:1], gbp[:, 0, 1:2], ALU.mult, ALU.add).then_inc(kT_out, 1)

            def a_maxima(n):
                u, j = n // 4, n % 4
                b, qt, g = u // 4, (u // 2) % 2, u % 2
                w = P * (qt + 1)
                h = 8 * g + 2 * j
                dve.wait_ge(a_ps, n + 1)
                dve.tensor_reduce(amax[:, 2 * b + qt, h:h + 2], four[j][:, 0:2 * w].rearrange("p (e k) -> p e k", e=2),
                                  AX.X, ALU.max, negate=True).then_inc(a_max, 1)

            def a_turned(n):
                qt = (n // 8) % 2
                w = 2 * P * (qt + 1)
                dve.wait_ge(pT_ps, n + 1)
                if n >= 4:
                    dve.wait_ge(o2_ps, n - 3)
                dve.tensor_copy(probT[:, n % 4, 0:w], st[n % 2][:, 0:w]).then_inc(pT_out, 1)

            def a_norm(t):
                dve.wait_ge(o2_ps, 8 * t + 8)
                dve.wait_ge(a_exp, 16 * t + 16)
                dve.reciprocal(arcp[:, t, :], asum[:, t, :]).then_inc(o2_rc, 1)
                dve.wait_ge(o2_rc, t + 1)
                dve.tensor_tensor(xn[:, t, :].rearrange("p (h d) -> p h d", d=DH),
                                  (st[2], mxb[0])[t % 2][:, 0:D].rearrange("p (h d) -> p h d", d=DH),
                                  arcp[:, t, :].unsqueeze(2).to_broadcast([P, H, DH]), ALU.mult).then_inc(o2_out, 1)

            for n in range(4):
                a_maxima(n)
            for n in range(64):
                a_turned(n)
                if n + 4 < 64:
                    a_maxima(n + 4)
                if n % 8 == 2 and n > 8:
                    a_norm(n // 8 - 1)
            a_norm(7)
            turned(3)
            add_out(1, four)
            norm(2)

            dve.reduce_sum(smean[:, 0, :], slotT[:, :, 0:SL], AX.X).then_inc(sm_a, 1)
            dve.wait_ge(sm_a, 1)
            dve.tensor_scalar(smean[:, 1, :], smean[:, 0, :], 1.0 / SL, None, ALU.mult).then_inc(sm_out, 1)
            dve.scalar_tensor_tensor(tau[:, 1:2], tau[:, 0:1], -1.0, tau[:, 0:1], ALU.mult, ALU.max).then_inc(tau_a, 1)
            dve.wait_ge(tau_a, 1)
            dve.tensor_scalar(tau[:, 2:3], tau[:, 1:2], 0.1, None, ALU.add).then_inc(tau_a, 1)
            dve.wait_ge(tau_a, 2)
            dve.reciprocal(tau[:, 3:4], tau[:, 2:3]).then_inc(tau_out, 1)
            dve.wait_ge(cv_ps, 1)
            dve.tensor_copy(cvec[:, :], kps[:, 0:1]).then_inc(cv_out, 1)
            turned(4)
            dve.wait_ge(lg_ps, 1)
            dve.wait_ge(tau_out, 1)
            dve.tensor_scalar(lg, misc[:, :].rearrange("p (t s) -> p t s", t=NT), tau[:, 3:4], None,
                              ALU.mult).then_inc(lg_out, 1)
            dve.wait_ge(lg_out, 1)
            for t in range(NT):
                dve.max(top8[:, t, :], lg[:, t, :]).then_inc(l_top, 1)
            for t in range(NT):
                dve.wait_ge(l_top, t + 1)
                dve.match_replace(lrep[:, t, :], top8[:, t, :], lg[:, t, :], -3e38).then_inc(l_rep, 1)
            dve.tensor_tensor(lsub, lg, top8[:, :, 0:1].to_broadcast([P, NT, SL]), ALU.subtract).then_inc(l_sub, 1)
            dve.wait_ge(l_rep, NT)
            dve.tensor_tensor(lmask, lg, lrep, ALU.not_equal).then_inc(l_mask, 1)
            dve.wait_ge(l_mask, 1)
            dve.wait_ge(l_exp, 1)
            dve.tensor_tensor(lexp, lexp, lmask, ALU.mult).then_inc(l_al, 1)
            dve.wait_ge(l_al, 1)
            dve.reduce_sum(lsum[:, :, 0], lexp, AX.X).then_inc(l_sum, 1)
            dve.wait_ge(l_sum, 1)
            dve.reciprocal(lsum[:, :, 1], lsum[:, :, 0]).then_inc(l_rc, 1)
            dve.wait_ge(l_rc, 1)
            dve.tensor_tensor(alpha, lexp, lsum[:, :, 1:2].to_broadcast([P, NT, SL]), ALU.mult).then_inc(l_out, 1)
            for r in range(2):
                dve.wait_ge(si_ps, r + 1)
                dve.tensor_scalar(den[:, r, 0:1], st[r][:, D:D + 1], 1e-8, None, ALU.add).then_inc(si_den, 1)
                dve.wait_ge(si_den, r + 1)
                dve.reciprocal(den[:, r, 1:2], den[:, r, 0:1]).then_inc(si_rc, 1)
                dve.wait_ge(si_rc, r + 1)
                dve.tensor_scalar(si[:, r, :], st[r][:, 0:D], den[:, r, 1:2], None, ALU.mult).then_inc(si_out, 1)
            dve.wait_ge(siT_ps, 1)
            dve.tensor_copy(siT.rearrange("p c s -> p (c s)"), st[2][:, :]).then_inc(siT_out, 1)
            for r in range(2):
                nb = (misc, st[0])[r]
                dve.wait_ge(g_rz, r + 1)
                dve.tensor_tensor(cand[:, r, :], rz[:, r, 0:D], nb[:, D:2 * D], ALU.mult).then_inc(g_rh, 1)
                dve.wait_ge(g_rh, r + 1)
                dve.tensor_tensor(snew[:, r, :], cand[:, r, :], nb[:, 0:D], ALU.add).then_inc(g_sum, 1)
            for r in range(2):
                dve.wait_ge(g_n, r + 1)
                dve.tensor_tensor(y[:, r, :], slots[:, :], cand[:, r, :], ALU.subtract).then_inc(g_d, 1)
                dve.wait_ge(g_d, r + 1)
                dve.tensor_tensor(y[:, r, :], y[:, r, :], rz[:, r, D:2 * D], ALU.mult).then_inc(g_zd, 1)
                dve.wait_ge(g_zd, r + 1)
                dve.tensor_tensor(snew[:, r, :], cand[:, r, :], y[:, r, :], ALU.add).then_inc(g_new, 1)
            dve.wait_ge(snT_ps, 1)
            dve.tensor_copy(snT.rearrange("p c s -> p (c s)"), st[1][:, :]).then_inc(snT_out, 1)
            dve.wait_ge(qk_ps, 1)
            dve.tensor_scalar(qkT[:, 0, :], st[2][0:SL, 0:T], QS ** -0.5, None, ALU.mult).then_inc(qk_out, 1)
            dve.tensor_copy(qkT[:, 1, :], st[2][0:SL, T:2 * T]).then_inc(qk_out, 1)
            dve.wait_ge(c_ps, 1)
            sc = mxb[0][:, 0:2 * SL].rearrange("p (r s) -> p r s", r=2)
            dve.reduce_max(smx[:, :, 0], sc, AX.X).then_inc(c_max, 1)
            dve.wait_ge(c_max, 1)
            dve.tensor_tensor(att, sc, smx[:, :, 0:1].to_broadcast([P, 2, SL]), ALU.subtract).then_inc(c_sub, 1)
            dve.wait_ge(c_exp, 1)
            dve.reduce_sum(smx[:, :, 1], att, AX.X).then_inc(c_sum, 1)
            dve.wait_ge(c_sum, 1)
            dve.reciprocal(smx[:, :, 2], smx[:, :, 1]).then_inc(c_rc, 1)
            dve.wait_ge(c_rc, 1)
            dve.tensor_tensor(att, att, smx[:, :, 2:3].to_broadcast([P, 2, SL]), ALU.mult).then_inc(c_out, 1)
            dve.wait_ge(cT_ps, 1)
            dve.tensor_copy(attT.rearrange("p r s -> p (r s)"), misc[0:SL, 0:2 * P]).then_inc(cT_out, 1)
            dve.wait_ge(cm_ps, 1)
            dve.wait_ge(g_new, 2)
            dve.tensor_tensor(y, snew, kps[:, :].rearrange("p (r d) -> p r d", r=2), ALU.add).then_inc(y_out, 1)
            dve.wait_ge(y_out, 1)
            for r in range(2):
                dve.bn_stats(stats[:, r, :], y[:, r, :]).then_inc(y_st, 1)
                dve.wait_ge(y_st, r + 1)
                dve.bn_aggr(mv[:, r, :], stats[:, r, :]).then_inc(y_ag, 1)
            dve.wait_ge(y_sd, 1)
            dve.reciprocal(rstd[:, 0:2, 1], rstd[:, 0:2, 0]).then_inc(y_rs, 1)
            dve.wait_ge(y_rs, 1)
            for r in range(2):
                dve.tensor_scalar(y[:, r, :], y[:, r, :], mv[:, r, 0:1], rstd[:, r, 1:2],
                                  ALU.subtract, ALU.mult).then_inc(y_n, 1)
            dve.wait_ge(yT_ps, 1)
            for c in range(2):
                dve.tensor_scalar(yT[:, c, :], st[0][:, c * T:(c + 1) * T], colv[:, 0, c:c + 1], colv[:, 1, c:c + 1],
                                  ALU.mult, ALU.add).then_inc(yT_out, 1)
            dve.wait_ge(sv_ps, 1)
            for m in range(2):
                dve.tensor_scalar(svT[:, m, :], st[1][:, m * T:(m + 1) * T], colv[:, 2, m:m + 1], None,
                                  ALU.add).then_inc(sv_out, 1)
            add_out(2, (st[2], mxb[0], misc, kps))

        @block.tensor
        def _(pe):
            def turn(k, src, ready, per):
                for n in range(4):
                    c, half = n // 2, n % 2
                    bank = (st[0], st[1], st[2], mxb[0])[n]
                    for j in range(4):
                        t = half * 4 + j
                        if c == 0:
                            pe.wait_ge(ready, per(t))
                        tr = pe.transpose(bank[:, j * P:(j + 1) * P], src(t, c), ident[:, :])
                    tr.then_inc(xnT_ps, 1)

            def normed(t, c):
                return xn[:, t, c * P:(c + 1) * P]

            turn(0, normed, ln_xn, lambda t: t + 1)
            pe.wait_ge(xnT_act, 2)
            pe.wait_ge(xnT_dve, 2)
            pe.wait_ge(w_in, 16 * 7)
            for n in range(4):
                g, half = n // 2, n % 2
                for c in range(2):
                    mm = pe.matmul((mxb[1], acc, misc, kps)[n][:, :], wq[:, c, g * P:(g + 1) * P],
                                   xnT[:, c, half * 512:(half + 1) * 512], start=(c == 0), stop=(c == 1))
                mm.then_inc(q_ps, 1)

            def project_k(slot, c):
                for g in range(2):
                    for n in range(2):
                        rows = P if n == 0 else C2 + 1
                        mm = pe.matmul(kps[:, g * CH:(g + 1) * CH], wk[0:rows, n, g * P:(g + 1) * P],
                                       ctxk[0:rows, slot, n, :], start=(n == 0), stop=(n == 1))
                mm.then_inc(k_ps, 1)

            def project_v(bank, src, slot):
                for t in range(2):
                    for n in range(2):
                        rows = P if n == 0 else C2 + 1
                        mm = pe.matmul(bank[:, t * D:(t + 1) * D], src[0:rows, slot, n, t * P:(t + 1) * P],
                                       wv[0:rows, n, :], start=(n == 0), stop=(n == 1))
                mm.then_inc(v_ps, 1)

            def max_step(j, slot, s):
                qt, n = s // 8, s % 8
                pe.matmul(mxb[s % 2][:, :], qst[0:96, slot, qt * P:(qt + 1) * P],
                          kst[0:96, slot, n * 512:(n + 1) * 512], start=True, stop=True).then_inc(max_ps, 1)

            pe.wait_ge(q_full, 4)

            def early_job(c, half, slot):
                wait(pe, ctxk_in[slot], 32 * half + 32)
                wait(pe, k_r, c)
                project_k(slot, c)
                wait(pe, v_out, c)
                project_v(mxb[1], ctxk, slot)

            early_job(0, 0, 0)
            early_job(1, 0, 1)
            with pe.Fori(1, VLEAD // 2, 1) as n:
                early_job(2 * n, n, 0)
                early_job(2 * n + 1, n, 1)
            for c in range(VLEAD, KLEAD):
                pe.wait_ge(ctxk_in[c % 2], 32 * (c // 2) + 32)
                pe.wait_ge(k_r, c)
                project_k(c % 2, c)
            pe.wait_ge(stacks_in[0], 128)
            pe.wait_ge(v_out, VLEAD)
            for s in range(ST):
                wait(pe, max_red, s - 1)
                max_step(0, 0, s)

            def pv_group(i, par, g):
                wait(pe, exp_done, i * ST + 2 * g + 2)
                wait(pe, clip_done, i * ST + 2 * g + 2)
                for r in range(4):
                    n = 4 * g + r
                    mm = pe.matmul(acc[32 * r:32 * r + 32, 0:T], vh[:, par, n, :],
                                   prob[:, (n // 2) % 8, (n % 2) * T:(n % 2 + 1) * T],
                                   start=(g == 0), stop=(g == 7), skip_group_check=True)
                mm.then_inc(pv_done, 1)

            def finish(i):
                wait(pe, acc_out, i + 1)
                for qt in range(QT):
                    mm = pe.matmul(misc[:, qt * 32:qt * 32 + DH + 1], accs[:, qt * P:(qt + 1) * P], gsum[:, :],
                                   start=True, stop=True)
                mm.then_inc(fin_ps, 1)

            def head(it, u, k_job, v_job, ahead):
                i = it * 4 + u
                first = isinstance(it, int) and i == 0
                if not first:
                    pv_group(i - 1, (u + 1) % 2, 7)
                if k_job:
                    wait(pe, ctxk_in[u % 2], 32 * (it * 2 + u // 2 + KLEAD // 2 + 1))
                    wait(pe, k_r, i + KLEAD)
                    project_k(u % 2, i + KLEAD)
                wait(pe, m_3, i + 1)
                wait(pe, head_out, i - 1)
                for qt in range(QT):
                    mm = pe.matmul(misc[96:99, qt * P:(qt + 1) * P], sparts[:, qt, :], identb[:, :],
                                   start=True, stop=True)
                mm.then_inc(shift_ps, 1)
                if v_job:
                    wait(pe, ctxv_in[u % 2], 32 * (it * 2 + u // 2 + 1))
                    wait(pe, max_red, (i + 1) * ST)
                    project_v(mxb[1], ctxv, u % 2)
                wait(pe, shift_set, i + 1)
                wait(pe, flag_abs, i + 1)
                pe.matmul(misc[:, 0:T], shrow[0:99, :], qst[0:99, u, :], start=True, stop=True).then_inc(low_ps, 1)
                if first:
                    pe.wait_ge(ones_set, 1)
                for s in range(ST):
                    wait(pe, exp_done, i * ST + (s - 2 if s >= 3 else 0))
                    for n in range(2):
                        mm = pe.matmul(st[s % 3][:, n * T:(n + 1) * T],
                                       kst[0:99, u, (2 * s + n) * P:(2 * s + n + 1) * P], qst[0:99, u, :],
                                       start=True, stop=True)
                    mm.then_inc(st_ps, 1)
                    if ahead:
                        if s == 0:
                            wait(pe, stacks_in[(u + 1) % 4], 128 * (it + (u + 1) // 4 + 1))
                            wait(pe, max_red, (i + 1) * ST - 1)
                        elif s == 1:
                            wait(pe, max_red, (i + 1) * ST)
                            if v_job:
                                wait(pe, v_out, i + VLEAD + 1)
                        else:
                            wait(pe, max_red, (i + 1) * ST + s - 1)
                        max_step(i + 1, (u + 1) % 4, s)
                    if s % 2 == 1 and s >= 3:
                        if s == 3:
                            wait(pe, vh_ready, i + 1)
                            wait(pe, acc_out, i)
                        pv_group(i, u % 2, (s - 3) // 2)
                    if s == 4 and not first:
                        wait(pe, low_set, i + 1)
                        finish(i - 1)

            for u in range(4):
                head(0, u, True, True, True)
            with pe.Fori(1, 11, 1) as it:
                for u in range(4):
                    head(it, u, True, True, True)
            for u in range(4):
                head(11, u, False, True, True)
            with pe.Fori(12, 15, 1) as it:
                for u in range(4):
                    head(it, u, False, False, True)
            for u in range(4):
                head(15, u, False, False, u < 3)
            pv_group(NH - 1, 1, 7)
            finish(NH - 1)

            four = (mxb[1], acc, misc, kps)

            pe.wait_ge(late_in, 16 * len(wt))
            pe.wait_ge(rows_in, 16 * len(bias))
            pe.wait_ge(rest_set, 8)
            pe.wait_ge(small_in, 16 * 12)
            turn(1, lambda t, c: o_sb[:, t // 2, t % 2, c * P:(c + 1) * P], head_out, lambda t: NH)
            pe.wait_ge(xnT_act, 4)
            pe.wait_ge(xnT_dve, 4)
            for n in range(4):
                for j in range(2):
                    t = 2 * n + j
                    to = four[n][:, j * D:(j + 1) * D]
                    pe.matmul(to, ones[0:1, 0:P], bias["L0_xattn_bo"], start=True, stop=False)
                    for c in range(2):
                        mm = pe.matmul(to, xnT[:, c, t * P:(t + 1) * P], wt["L0_xattn_Wo"][:, c, :],
                                       start=False, stop=(c == 1))
                mm.then_inc(out_ps, 1)

            pe.wait_ge(x_new, 4)
            pe.matmul(misc[:, 0:2], spread[:, 0, :], gb16[:, 0:2], start=True, stop=True)
            for n in range(1, 3):
                mm = pe.matmul(misc[:, 2 * n:2 * n + 2], spread[:, n, :], gb16[:, 2:4], start=True, stop=True)
            mm.then_inc(gb_ps, 1)
            turn(2, normed, ln_xn, lambda t: NT + t + 1)
            pe.wait_ge(xnT_act, 6)
            pe.wait_ge(xnT_dve, 6)
            ring = (st[0], st[1], st[2], mxb[0])
            pe.wait_ge(gb_out, 1)
            for t in range(NT):
                if t >= 4:
                    pe.wait_ge(kq_c, t - 3)
                for c in range(2):
                    mm = pe.matmul(ring[t % 4][:, :], xnT[:, c, t * P:(t + 1) * P], wt["attn_WkqT"][:, c, :],
                                   start=(c == 0), stop=(c == 1))
                mm.then_inc(kq_ps, 1)
                for c in range(2):
                    mm = pe.matmul(four[t // 2][:, (t % 2) * D:(t % 2 + 1) * D], xnT[:, c, t * P:(t + 1) * P],
                                   wt["attn_WvT"][:, c, :], start=(c == 0), stop=(c == 1))
                if t % 2:
                    mm.then_inc(v2_ps, 1)
            pe.wait_ge(kq_c, NT)
            for m in range(4):
                for which in range(2):
                    bank = ring[which * 2 + m % 2]
                    if m >= 2:
                        pe.wait_ge(qT_out if which else kT_out, 2 * (m - 1) if which else m - 1)
                    for g in range(2):
                        for j in range(2):
                            t = 2 * m + j
                            pe.wait_ge(kq_n, t + 1)
                            tr = pe.transpose(bank[:, (g * 2 + j) * P:(g * 2 + j + 1) * P],
                                              kqc[:, t, which * H + 8 * g:which * H + 8 * g + 8, :], ident[:, :])
                    tr.then_inc(kqT_ps, 1)

            def a_scores(n):
                u, j = n // 4, n % 4
                b, qt, g = u // 4, (u // 2) % 2, u % 2
                w = P * (qt + 1)
                tok = b * T + qt * P
                if n >= 4:
                    pe.wait_ge(a_exp, 2 * (n - 4) + 2)
                for e in range(2):
                    to = four[j][:, e * w:(e + 1) * w]
                    pe.matmul(to, identb[:, :], causal[:, 1 - qt:2, :], start=True, stop=False)
                    mm = pe.matmul(to, (qeT, qoT)[e][32 * j:32 * j + 32, g, tok:tok + P],
                                   kT[32 * j:32 * j + 32, g, b * T:b * T + w], start=False, stop=True)
                mm.then_inc(a_ps, 1)

            def a_turn(n):
                u, j = n // 4, n % 4
                qt = (u // 2) % 2
                w = P * (qt + 1)
                if n >= 2:
                    pe.wait_ge(pT_out, n - 1)
                pe.wait_ge(a_exp, 2 * n + 2)
                for e in range(2):
                    for kt in range(qt + 1):
                        s = (e * (qt + 1) + kt) * P
                        tr = pe.transpose(st[n % 2][:, s:s + P], prob[:, n % 8, e * w + kt * P:e * w + (kt + 1) * P],
                                          ident[:, :])
                tr.then_inc(pT_ps, 1)

            def a_values(n):
                u, j = n // 4, n % 4
                b, qt, g = u // 4, (u // 2) % 2, u % 2
                t = b * 2 + qt
                pe.wait_ge(pT_out, n + 1)
                if n % 8 == 0 and n >= 16:
                    pe.wait_ge(o2_out, t - 1)
                for e in range(2):
                    h = 8 * g + 2 * j + e
                    for kt in range(qt + 1):
                        s = (e * (qt + 1) + kt) * P
                        mm = pe.matmul((st[2], mxb[0])[t % 2][:, h * DH:(h + 1) * DH],
                                       probT[:, n % 4, s:s + P], v2[:, 2 * b + kt, h * DH:(h + 1) * DH],
                                       start=(kt == 0), stop=(kt == qt))
                mm.then_inc(o2_ps, 1)

            pe.wait_ge(kT_out, 4)
            pe.wait_ge(qT_out, 8)
            pe.wait_ge(v2_out, 4)
            for n in range(4):
                a_scores(n)
            for n in range(64):
                a_turn(n)
                if n + 4 < 64:
                    a_scores(n + 4)
                if n >= 1:
                    a_values(n - 1)
            a_values(63)
            turn(3, normed, o2_out, lambda t: t + 1)
            pe.wait_ge(xnT_act, 8)
            pe.wait_ge(xnT_dve, 8)
            for n in range(4):
                for j in range(2):
                    t = 2 * n + j
                    to = four[n][:, j * D:(j + 1) * D]
                    pe.matmul(to, ones[0:1, 0:P], bias["L0_attn_bo"], start=True, stop=False)
                    for c in range(2):
                        mm = pe.matmul(to, xnT[:, c, t * P:(t + 1) * P], wt["attn_WoT"][:, c, :],
                                       start=False, stop=(c == 1))
                mm.then_inc(out_ps, 1)

            pe.wait_ge(sm_out, 1)
            pe.wait_ge(x_new, 8)
            for c in range(2):
                pe.matmul(kps[:, 0:1], wt["L0_ffn_w1"][:, 2 + c, :], smean[:, 1, c:c + 1], start=(c == 0), stop=False)
            pe.matmul(kps[:, 0:1], bias["L0_ffn_b1"], ones[0:1, 0:1], start=False, stop=True).then_inc(cv_ps, 1)
            turn(4, normed, ln_xn, lambda t: 2 * NT + t + 1)
            pe.wait_ge(xnT_act, 10)
            pe.wait_ge(xnT_dve, 10)
            for n in range(2):
                for c in range(2):
                    mm = pe.matmul(four[n][:, :], wt["L0_ffn_w1"][:, c, :], xnT[:, c, n * 512:(n + 1) * 512],
                                   start=(c == 0), stop=(c == 1))
                mm.then_inc(h_ps, 1)
            for t in range(NT):
                pe.wait_ge(h_out, t // 4 + 1)
                to = misc[:, t * SL:(t + 1) * SL]
                pe.matmul(to, ones[0:1, 0:P], bias["L0_ffn_b2"], start=True, stop=False)
                mm = pe.matmul(to, hT[:, t * P:(t + 1) * P], wt["L0_ffn_w2"][:, 0, :], start=False, stop=True)
            mm.then_inc(lg_ps, 1)
            pe.wait_ge(l_out, 1)
            for b in range(B):
                rows = slice((b % 2) * SL, (b % 2 + 1) * SL)
                for q in range(2):
                    pe.matmul(st[b // 2][rows, 0:D], alpha[:, 2 * b + q, :], xn[:, 2 * b + q, :],
                              start=(q == 0), stop=(q == 1))
                for q in range(2):
                    mm = pe.matmul(st[b // 2][rows, D:D + 1], alpha[:, 2 * b + q, :], onescol[:, :],
                                   start=(q == 0), stop=(q == 1))
                if b % 2:
                    mm.then_inc(si_ps, 1)
            for t in range(NT):
                tr = pe.transpose(four[t // 4][0:SL, (t % 4) * P:(t % 4 + 1) * P], alpha[:, t, :], ident[:, :])
                if t % 4 == 3:
                    tr.then_inc(alT_ps, 1)
            pe.wait_ge(si_out, 2)
            for c in range(2):
                for r in range(2):
                    tr = pe.transpose(st[2][:, (c * 2 + r) * P:(c * 2 + r + 1) * P], si[:, r, c * P:(c + 1) * P],
                                      ident[:, :])
            tr.then_inc(siT_ps, 1)
            pe.wait_ge(siT_out, 1)
            pe.wait_ge(lg_out, 1)
            pe.wait_ge(si_out, 2)
            wih, whh = wt["ffn_WihT"], wt["ffn_WhhT"]
            for r in range(2):
                rzb, nb = ((mxb[0], misc), (kps, st[0]))[r]
                for n, (w, lhs) in enumerate(((wih, siT[:, :, r * P:(r + 1) * P]), (whh, slotT))):
                    row = bias[("L0_ffn_bih", "L0_ffn_bhh")[n]]
                    for c in range(2):
                        pe.matmul(rzb[:, :], lhs[:, c, :], w[:, c, 0:2 * D], start=(n == 0 and c == 0), stop=False)
                    pe.matmul(rzb[:, :], ones[0:1, 0:P], row[:, 0:2 * D], start=False, stop=(n == 1))
                for n, (w, lhs) in enumerate(((wih, siT[:, :, r * P:(r + 1) * P]), (whh, slotT))):
                    row = bias[("L0_ffn_bih", "L0_ffn_bhh")[n]]
                    to = nb[:, n * D:(n + 1) * D]
                    for c in range(2):
                        pe.matmul(to, lhs[:, c, :], w[:, c, 2 * D:3 * D], start=(c == 0), stop=False)
                    mm = pe.matmul(to, ones[0:1, 0:P], row[:, 2 * D:3 * D], start=False, stop=True)
                mm.then_inc(g_ps, 1)
            for c in range(2):
                for r in range(2):
                    pe.wait_ge(g_new, r + 1)
                    tr = pe.transpose(st[1][:, (c * 2 + r) * P:(c * 2 + r + 1) * P], snew[:, r, c * P:(c + 1) * P],
                                      ident[:, :])
            tr.then_inc(snT_ps, 1)
            pe.wait_ge(snT_out, 1)
            for n, (w, row) in enumerate((("L0_ffn_wq", "L0_ffn_bq"), ("L0_ffn_wk", "L0_ffn_bk"))):
                to = st[2][0:SL, n * T:(n + 1) * T]
                for c in range(2):
                    pe.matmul(to, wt[w][:, c, :], snT[:, c, :], start=(c == 0), stop=False)
                mm = pe.matmul(to, bias[row], ones[0:1, 0:T], start=False, stop=True)
            mm.then_inc(qk_ps, 1)
            pe.wait_ge(alT_out, 2)
            for b in range(B):
                to = (mxb[1], acc)[b // 2][0:SL, (b % 2) * D:(b % 2 + 1) * D]
                for c in range(2):
                    pe.matmul(to, snT[:, c, b * SL:(b + 1) * SL], wt["L0_ffn_wv"][:, c, :], start=(c == 0), stop=False)
                mm = pe.matmul(to, ones[0:1, 0:SL], bias["L0_ffn_bv"], start=False, stop=True)
                if b % 2:
                    mm.then_inc(v4_ps, 1)
            pe.wait_ge(qk_out, 2)
            for b in range(B):
                mm = pe.matmul(mxb[0][(b % 2) * SL:(b % 2 + 1) * SL, (b // 2) * SL:(b // 2 + 1) * SL],
                               qkT[:, 0, b * SL:(b + 1) * SL], qkT[:, 1, b * SL:(b + 1) * SL], start=True, stop=True)
            mm.then_inc(c_ps, 1)
            pe.wait_ge(c_out, 1)
            for r in range(2):
                tr = pe.transpose(misc[0:SL, r * P:(r + 1) * P], att[:, r, :], ident[:, :])
            tr.then_inc(cT_ps, 1)
            pe.wait_ge(cT_out, 1)
            pe.wait_ge(v4_out, 2)
            for b in range(B):
                mm = pe.matmul(kps[(b % 2) * SL:(b % 2 + 1) * SL, (b // 2) * D:(b // 2 + 1) * D],
                               attT[:, b // 2, (b % 2) * SL:(b % 2 + 1) * SL], v4[:, b, :], start=True, stop=True)
            mm.then_inc(cm_ps, 1)
            pe.wait_ge(y_n, 2)
            for c in range(2):
                for r in range(2):
                    tr = pe.transpose(st[0][:, (c * 2 + r) * P:(c * 2 + r + 1) * P], y[:, r, c * P:(c + 1) * P],
                                      ident[:, :])
            tr.then_inc(yT_ps, 1)
            pe.wait_ge(yT_out, 2)
            for m in range(2):
                for c in range(2):
                    mm = pe.matmul(st[1][:, m * T:(m + 1) * T], wt["L0_ffn_wvp"][:, c, m * P:(m + 1) * P],
                                   yT[:, c, :], start=(c == 0), stop=(c == 1))
            mm.then_inc(sv_ps, 1)
            pe.wait_ge(sv_out, 2)
            for b in range(B):
                to = (mxb[1], acc)[b // 2][0:SL, (b % 2) * D:(b % 2 + 1) * D]
                for m in range(2):
                    mm = pe.matmul(to, svT[:, m, b * SL:(b + 1) * SL], wt["L0_ffn_wo"][:, m, :],
                                   start=(m == 0), stop=(m == 1))
                if b % 2:
                    mm.then_inc(svo_ps, 1)
            last = (st[2], mxb[0], misc, kps)
            pe.wait_ge(y_out, 1)
            for n in range(4):
                pe.wait_ge(svo_out, n // 2 + 1)
                for j in range(2):
                    t = 2 * n + j
                    to = last[n][:, j * D:(j + 1) * D]
                    pe.matmul(to, ones[0:1, 0:P], bias["L0_ffn_bo"], start=True, stop=False)
                    mm = pe.matmul(to, alphaT[:, t, :], svo[:, n, :], start=False, stop=True)
                mm.then_inc(out_ps, 1)


def kernel(**inputs):
    import numpy as np
    import concourse.bacc as bacc
    from concourse.bass_utils import run_bass_kernel_spmd as run

    arrays = {k: np.ascontiguousarray(v) for k, v in inputs.items() if k != "ctx_768"}
    ctx = np.ascontiguousarray(inputs["ctx_768"]).reshape(NCH, CH, C)
    arrays["ctxT"] = np.ascontiguousarray(ctx.transpose(0, 2, 1))
    for name, key in (("attn_WvT", "L0_attn_Wv"), ("attn_WoT", "L0_attn_Wo"), ("ffn_WihT", "L0_ffn_Wih"),
                      ("ffn_WhhT", "L0_ffn_Whh"), ("ffn_slotT", "L0_ffn_slot_init")):
        arrays[name] = np.ascontiguousarray(arrays[key].T)
    arrays["attn_WkqT"] = np.ascontiguousarray(
        np.concatenate([arrays["L0_attn_Wk"], arrays["L0_attn_Wq"]], axis=0).T)
    for key in ("L0_attn_Wv", "L0_attn_Wo", "L0_attn_Wk", "L0_attn_Wq", "L0_ffn_Wih", "L0_ffn_Whh"):
        del arrays[key]
    nc = bacc.Bacc("TRN2", target_bir_lowering=False, num_devices=1)
    aps = {k: nc.dram_tensor("in_" + k, v.shape, mybir.dt.from_np(v.dtype), kind="ExternalInput").ap()
           for k, v in arrays.items()}
    out = nc.dram_tensor("out", (B, T, D), F32, kind="ExternalOutput").ap()
    build(nc, aps, out)
    r = run(nc, [{"in_" + k: v for k, v in arrays.items()}], core_ids=[0])
    return r.results[0]["out"]
```

```python
from contextlib import ExitStack

import concourse.bass as bass
from concourse import mybir

ALU = mybir.AluOpType
ACT = mybir.ActivationFunctionType
F32 = mybir.dt.float32
BF16 = mybir.dt.bfloat16
I32 = mybir.dt.int32
AX = mybir.AxisListType

P = 128
B, T, D = 4, 256, 256
S, C = 4096, 192
H = 16
DH = D // H
NT = B * T // P
QT = T // P
NH = B * H
C2 = C - P
CH = 256
NCH = B * S // CH
KLEAD, VLEAD = 20, 17
ST = 16
CLIP = 10000.0
EPS = 1e-5
SL = 64
FH = 128
QS = D // 4
NEAR = 9800.0


def build(nc, a, out):
    with ExitStack() as ctx:
        def sb(name, shape, dt=F32):
            return ctx.enter_context(nc.sbuf_tensor(name, shape, dt))

        def psum(name):
            return ctx.enter_context(nc.psum_tensor(name, [P, 512], F32))

        def sem(name):
            return ctx.enter_context(nc.semaphore(name))

        st = [psum(f"st{n}") for n in range(3)]
        mxb = [psum(f"mx{n}") for n in range(2)]
        acc = psum("acc")
        misc = psum("misc")
        kps = psum("kps")

        x_sb = sb("x_sb", [P, NT, D])
        xn = sb("xn", [P, NT, D])
        xnT = sb("xnT", [P, 2, B * T])
        o_sb = sb("o_sb", [P, B, QT, D])
        v_sb = sb("v_sb", [P, 64, D])
        kst = sb("kst", [P, 4, S], BF16)
        qst = sb("qst", [P, 4, T], BF16)
        prob = sb("prob", [P, 8, 512])
        vh = sb("vh", [P, 2, 32, 32])
        ctx4 = sb("ctx4", [P, 4, 2, CH])
        wk = sb("wk", [P, 2, D])
        wv = sb("wv", [P, 2, D])
        wq = sb("wq", [P, 2, D])
        bq = sb("bq", [P, 2])
        kparts = sb("kparts", [P, 2, 2, 3, CH], BF16)
        kres = sb("kres", [P, 2, 2, CH])
        low = sb("low", [P, T])
        accs = sb("accs", [P, T])
        mxp = sb("mxp", [P, 2, QT, 8])
        rowmax = sb("rowmax", [P, QT])
        shift = sb("shift", [P, QT])
        sres = sb("sres", [P, QT])
        sparts = sb("sparts", [P, QT, 3], BF16)
        flagf = sb("flagf", [P, 1])
        flag = sb("flag", [P, 1], I32)
        rcp = sb("rcp", [P, QT])
        stats = sb("stats", [P, NT, 6])
        mv = sb("mv", [P, NT, 2])
        rstd = sb("rstd", [P, NT, 2])
        ident = sb("ident", [P, P])
        identb = sb("identb", [P, P], BF16)
        gsum = sb("gsum", [P, DH + 1])
        shrow = sb("shrow", [P, P], BF16)
        negclip = sb("negclip", [P, 1])
        epsc = sb("epsc", [P, 1])

        ones = sb("ones", [1, 512])
        onescol = sb("onescol", [P, 1])
        brow = sb("brow", [1, 2880])
        slotT = sb("slotT", [P, 2, 2 * SL])
        slots = sb("slots", [P, D])
        colv = sb("colv", [P, 3, 2])
        tau = sb("tau", [P, 4])
        gb16 = sb("gb16", [DH, 4])
        spread = sb("spread", [DH, 3, P])
        gbp = sb("gbp", [P, 3, 2])
        causal = sb("causal", [P, 2, P], BF16)
        bias = {}
        at = 0
        for name, n in (("L0_xattn_bo", D), ("L0_attn_bo", D), ("L0_ffn_bih", 3 * D), ("L0_ffn_bhh", 3 * D),
                        ("L0_ffn_b1", FH), ("L0_ffn_b2", SL), ("L0_ffn_bq", QS), ("L0_ffn_bk", QS),
                        ("L0_ffn_bv", D), ("L0_ffn_bo", D)):
            bias[name] = brow[0:1, at:at + n]
            at += n

        late = v_sb[:, 0:32, :].rearrange("p t d -> p (t d)")
        wt = {}
        at = 0
        for name, c, n in (("L0_xattn_Wo", 2, D), ("attn_WkqT", 2, 2 * D), ("attn_WvT", 2, D), ("attn_WoT", 2, D),
                           ("L0_ffn_w1", 4, FH), ("L0_ffn_w2", 1, SL), ("ffn_WihT", 2, 3 * D),
                           ("ffn_WhhT", 2, 3 * D), ("L0_ffn_wq", 2, QS), ("L0_ffn_wk", 2, QS),
                           ("L0_ffn_wv", 2, D), ("L0_ffn_wvp", 2, D), ("L0_ffn_wo", 2, D)):
            wt[name] = late[:, at:at + c * n].rearrange("p (c n) -> p c n", c=c)
            at += c * n
        assert at <= 32 * D
        free_v = v_sb[:, 32:64, :].rearrange("p t d -> p (t d)")
        v2 = free_v[:, 0:2048].rearrange("p (t d) -> p t d", t=NT)
        kqc = free_v[:, 2048:6144].rearrange("p (t h d) -> p t h d", t=NT, d=DH)
        probT = free_v[:, 6144:8192].rearrange("p (n q) -> p n q", n=4)
        free_k = kst[:, :, :].rearrange("p a s -> p (a s)").bitcast(F32)
        kT = free_k[:, 0:2048].rearrange("p (g t) -> p g t", g=2)
        qeT = free_k[:, 2048:4096].rearrange("p (g t) -> p g t", g=2)
        qoT = free_k[:, 4096:6144].rearrange("p (g t) -> p g t", g=2)
        sq = free_k[:, 6144:8192].rearrange("p (t h d) -> p t h d", t=4, d=DH)
        hsum = sb("hsum", [P, NT, 2 * H])
        hvar = sb("hvar", [P, NT, 2 * H])
        hsd = sb("hsd", [P, NT, 2 * H])
        hrs = sb("hrs", [P, NT, 2 * H])
        amax = sb("amax", [P, NT, H])
        asum = sb("asum", [P, NT, H])
        arcp = sb("arcp", [P, NT, H])
        hT = kqc.rearrange("p t h d -> p (t h d)")[:, 0:1024]
        lg = kqc.rearrange("p t h d -> p (t h d)")[:, 1024:1536].rearrange("p (t s) -> p t s", t=NT)
        lrep = kqc.rearrange("p t h d -> p (t h d)")[:, 1536:2048].rearrange("p (t s) -> p t s", t=NT)
        lmask = kqc.rearrange("p t h d -> p (t h d)")[:, 2048:2560].rearrange("p (t s) -> p t s", t=NT)
        lsub = kqc.rearrange("p t h d -> p (t h d)")[:, 2560:3072].rearrange("p (t s) -> p t s", t=NT)
        alpha = kqc.rearrange("p t h d -> p (t h d)")[:, 3072:3584].rearrange("p (t s) -> p t s", t=NT)
        lexp = kqc.rearrange("p t h d -> p (t h d)")[:, 3584:4096].rearrange("p (t s) -> p t s", t=NT)
        si = v2.rearrange("p t d -> p (t d)")[:, 0:512].rearrange("p (r d) -> p r d", r=2)
        siT = v2.rearrange("p t d -> p (t d)")[:, 512:1024].rearrange("p (c s) -> p c s", c=2)
        rz = v2.rearrange("p t d -> p (t d)")[:, 1024:2048].rearrange("p (r d) -> p r d", r=2)
        pT = probT.rearrange("p n q -> p (n q)")
        cand = pT[:, 0:512].rearrange("p (r d) -> p r d", r=2)
        snew = pT[:, 512:1024].rearrange("p (r d) -> p r d", r=2)
        snT = pT[:, 1024:1536].rearrange("p (c s) -> p c s", c=2)
        yT = pT[:, 1536:2048].rearrange("p (c s) -> p c s", c=2)
        fk = kT.rearrange("p g t -> p (g t)")
        qkT = fk[0:SL, 0:512].rearrange("p (n s) -> p n s", n=2)
        v4 = fk[0:SL, 512:1536].rearrange("p (b d) -> p b d", b=B)
        att = fk[:, 1536:1664].rearrange("p (r s) -> p r s", r=2)
        attT = fk[0:SL, 1664:1920].rearrange("p (r s) -> p r s", r=2)
        fq = qeT.rearrange("p g t -> p (g t)")
        y = fq[:, 0:512].rearrange("p (r d) -> p r d", r=2)
        svT = fq[:, 512:1024].rearrange("p (c s) -> p c s", c=2)
        svo = fq[0:SL, 1024:2048].rearrange("p (b d) -> p b d", b=B)
        alphaT = qoT.rearrange("p g t -> p (g t)")[0:SL, 0:1024].rearrange("p (t q) -> p t q", t=NT)
        cvec = sb("cvec", [P, 1])
        smean = sb("smean", [P, 2, 2])
        top8 = sb("top8", [P, NT, 8])
        lsum = sb("lsum", [P, NT, 2])
        den = sb("den", [P, 2, 3])
        smx = sb("smx", [P, 2, 4])

        qw = v_sb[:, 32:64, :].rearrange("p t d -> p (t d)")
        q_sb = qw[:, 0:2048].rearrange("p (g t) -> p g t", g=2)
        qres = qw[:, 2048:4096].rearrange("p (g t) -> p g t", g=2)
        q1 = qw[:, 4096:5120].bitcast(BF16).rearrange("p (g t) -> p g t", g=2)
        q2 = qw[:, 5120:6144].bitcast(BF16).rearrange("p (g t) -> p g t", g=2)
        q3 = qw[:, 6144:7168].bitcast(BF16).rearrange("p (g t) -> p g t", g=2)

        kscr = nc.dram_tensor("kscr", [D, 3, B * S], BF16, kind="Internal").ap()
        qscr1 = nc.dram_tensor("qscr1", [D, 3, B * T], BF16, kind="Internal").ap()
        qscr2 = nc.dram_tensor("qscr2", [D, B * T], BF16, kind="Internal").ap()
        qscr3 = nc.dram_tensor("qscr3", [D, B * T], BF16, kind="Internal").ap()

        x_in, w_in, wq_in = sem("x_in"), sem("w_in"), sem("wq_in")
        consts, rest_set = sem("consts"), sem("rest_set")
        ln_st, ln_ag, ln_sq, ln_rc, ln_xn = (sem(f"ln_{n}") for n in ("stats", "aggr", "sqrt", "recip", "out"))
        xnT_ps, xnT_act, xnT_dve = sem("xnT_ps"), sem("xnT_act"), sem("xnT_dve")
        q_ps, q_full, q_1, q_r1, q_2, q_3 = (sem(f"q_{n}") for n in ("ps", "full", "1", "r1", "2", "3"))
        qscr_w = sem("qscr_written")
        rows_set, ones_set = sem("rows_set"), sem("ones_set")
        ctx_in = [sem(f"ctx_in{n}") for n in range(4)]
        k_ps, k_1, k_r, k_2, k_3 = (sem(f"k_{n}") for n in ("ps", "1", "res", "2", "3"))
        kscr_w = [sem(f"k_written{n}") for n in range(2)]
        v_ps, v_out = sem("v_ps"), sem("v_out")
        stacks_in = [sem(f"stacks_in{n}") for n in range(4)]
        vh_ready = sem("vh_ready")
        max_ps, max_red = sem("max_ps"), sem("max_red")
        m_row, m_clip, m_1, m_res, m_2, m_3 = (sem(f"m_{n}") for n in ("row", "clip", "1", "res", "2", "3"))
        shift_ps, shift_set, flag_abs, flag_set = (sem(n) for n in ("shift_ps", "shift_set", "flag_abs", "flag_set"))
        low_ps, low_set = sem("low_ps"), sem("low_set")
        st_ps, exp_done, clip_step, clip_done = (sem(n) for n in ("st_ps", "exp_done", "clip_step", "clip_done"))
        pv_done, acc_out, fin_ps, fin_rcp, head_out = (
            sem(n) for n in ("pv_done", "acc_out", "fin_ps", "fin_rcp", "head_out"))
        stored = sem("stored")
        rows_in, late_in, small_in = sem("rows_in"), sem("late_in"), sem("small_in")
        gb_ps, gb_out = sem("gb_ps"), sem("gb_out")
        out_ps, x_new = sem("out_ps"), sem("x_new")
        kq_ps, kq_sum, kq_c, kq_sq, kq_var, kq_sd, kq_rs, kq_n = (
            sem(f"kq_{n}") for n in ("ps", "sum", "centred", "square", "var", "sd", "rs", "normed"))
        v2_ps, v2_out = sem("v2_ps"), sem("v2_out")
        kqT_ps, kT_out, qT_out = sem("kqT_ps"), sem("kT_out"), sem("qT_out")
        a_ps, a_max, a_exp, pT_ps, pT_out, o2_ps, o2_rc, o2_out = (
            sem(f"a_{n}") for n in ("ps", "max", "exp", "pT_ps", "pT_out", "o_ps", "o_recip", "o_out"))
        sm_out, cv_ps, cv_out, tau_a, tau_out = (
            sem(n) for n in ("sm_out", "cv_ps", "cv_out", "tau_abs", "tau_out"))
        h_ps, h_out, lg_ps, lg_out, l_top, l_rep, l_mask, l_sub, l_exp, l_al, l_sum, l_rc, l_out = (
            sem(f"l_{n}") for n in ("h_ps", "h", "ps", "logits", "top", "replaced", "mask", "sub", "exp", "masked",
                                    "sum", "recip", "alpha"))
        si_ps, si_den, si_rc, si_out, siT_ps, siT_out = (
            sem(f"si_{n}") for n in ("ps", "den", "recip", "out", "T_ps", "T_out"))
        g_ps, g_rz, g_rh, g_sum, g_n, g_d, g_zd, g_new = (
            sem(f"g_{n}") for n in ("ps", "rz", "rh", "sum", "cand", "diff", "zdiff", "new"))
        snT_ps, snT_out, qk_ps, qk_out, v4_ps, v4_out = (
            sem(n) for n in ("snT_ps", "snT_out", "qk_ps", "qk_out", "v4_ps", "v4_out"))
        c_ps, c_max, c_sub, c_exp, c_sum, c_rc, c_out, cT_ps, cT_out, cm_ps, y_out = (
            sem(f"c_{n}") for n in ("ps", "max", "sub", "exp", "sum", "recip", "att", "attT_ps", "attT", "comm", "y"))
        y_st, y_ag, y_sd, y_rs, y_n, yT_ps, yT_out, sv_ps, sv_out, svo_ps, svo_out, alT_ps, alT_out = (
            sem(f"y_{n}") for n in ("stats", "aggr", "sd", "recip", "normed", "T_ps", "T_out", "sv_ps", "sv",
                                    "svo_ps", "svo", "alphaT_ps", "alphaT"))

        bank_of = [s % 3 for s in range(15)] + [1]

        passed = {nc.sync: sem("sp_passed"), nc.gpsimd: sem("pool_passed")}

        block = ctx.enter_context(nc.Block())

        def wait(eng, s, value):
            if not (isinstance(value, int) and value <= 0):
                eng.wait_ge(s, value)

        def wait_alone(eng, s, value):
            wait(eng, s, value)
            if not isinstance(value, int):
                eng.sem_inc(passed[eng], 1)

        @block.sync
        def _(sp):
            def load_ctx(slot, c):
                src = a["ctxT"][bass.ds(c, 1), :, :].rearrange("o c t -> (o c) t")
                sp.dma_start(ctx4[:, slot, 0, :], src[0:P, :]).then_inc(ctx_in[slot], 16)
                sp.dma_start(ctx4[0:C2, slot, 1, :], src[P:C, :]).then_inc(ctx_in[slot], 16)

            for w, name, row in ((wk, "L0_xattn_Wk", "L0_xattn_bk"), (wv, "L0_xattn_Wv", "L0_xattn_bv")):
                sp.dma_start(w[:, 0, :], a[name][0:P, :]).then_inc(w_in, 16)
                sp.dma_start(w[0:C2, 1, :], a[name][P:C, :]).then_inc(w_in, 16)
                sp.dma_start(w[C2:C2 + 1, 1, :], a[row].rearrange("(o n) -> o n", o=1)).then_inc(w_in, 16)
                if w is wk:
                    load_ctx(0, 0)
                    sp.dma_start(x_sb[:, :, :], a["x"].rearrange("b (q p) d -> p (b q) d", p=P)).then_inc(x_in, 16)
            load_ctx(1, 1)
            sp.dma_start(wq[:, :, :], a["L0_xattn_Wq"].rearrange("(c p) n -> p c n", p=P)).then_inc(wq_in, 16)
            load_ctx(2, 2)
            load_ctx(3, 3)
            with nc.allow_non_contiguous_dma("256 biases onto partitions"):
                sp.dma_start(bq[:, :], a["L0_xattn_bq"].rearrange("(g p) -> p g", p=P)).then_inc(wq_in, 16)
            sp.wait_ge(ones_set, 1)
            for n in range(1, 4):
                sp.dma_start(kst[96:99, n, :], kst[96:99, 0, :]).then_inc(ones_set, 16)

            def write_k(par, c):
                wait_alone(sp, k_3, c + 1)
                for g in range(2):
                    sp.dma_start(kscr[g * P:(g + 1) * P, :, bass.ds(c * CH, CH)],
                                 kparts[:, par, g, :, :]).then_inc(kscr_w[par], 16)

            def load_stacks(b, h, slot):
                done = stacks_in[slot]
                rows, cols = bass.ds(h * DH, DH), bass.ds(b * S, S)
                sp.dma_start(kst[0:48, slot, :], kscr[rows, :, cols].rearrange("d r t -> (d r) t")).then_inc(done, 16)
                for n, r in enumerate((0, 1, 0)):
                    sp.dma_start(kst[48 + 16 * n:64 + 16 * n, slot, :],
                                 kscr[rows, r:r + 1, cols].rearrange("d r t -> (d r) t")).then_inc(done, 16)
                cols = bass.ds(b * T, T)
                sp.dma_start(qst[0:48, slot, :], qscr1[rows, :, cols].rearrange("d r t -> (d r) t")).then_inc(done, 16)
                for n, scr in enumerate((qscr2, qscr2, qscr3)):
                    sp.dma_start(qst[48 + 16 * n:64 + 16 * n, slot, :], scr[rows, cols]).then_inc(done, 16)

            def early_job(c, slot):
                wait_alone(sp, v_ps, c + 1)
                load_ctx(slot, c + 4)
                write_k(slot % 2, c)

            for c in range(4):
                early_job(c, c)
            sp.wait_ge(q_1, 1)
            for g in range(2):
                for r in range(3):
                    sp.dma_start(qscr1[g * P:(g + 1) * P, r, :], q1[:, g, :]).then_inc(qscr_w, 16)
            sp.wait_ge(q_2, 1)
            for g in range(2):
                sp.dma_start(qscr2[g * P:(g + 1) * P, :], q2[:, g, :]).then_inc(qscr_w, 16)
            sp.wait_ge(q_3, 1)
            for g in range(2):
                sp.dma_start(qscr3[g * P:(g + 1) * P, :], q3[:, g, :]).then_inc(qscr_w, 16)
            with sp.Fori(1, 4, 1) as n:
                for c in range(4):
                    early_job(4 * n + c, c)
            sp.wait_ge(qscr_w, 160)
            for n in range(2):
                sp.wait_ge(kscr_w[n], 32 * 8)
            load_stacks(0, 0, 0)
            load_stacks(0, 1, 1)
            sp.wait_ge(v_ps, 17)
            load_ctx(0, KLEAD)
            write_k(0, 16)
            sp.wait_ge(k_ps, 18)
            load_ctx(1, KLEAD + 1)
            write_k(1, 17)
            sp.wait_ge(k_ps, 19)
            load_ctx(2, VLEAD + 1)
            write_k(0, 18)
            sp.wait_ge(k_ps, 20)
            load_ctx(3, VLEAD)
            write_k(1, 19)
            load_stacks(0, 2, 2)

            def head(it, u, k_job, v_job, k_load, v_load, ahead):
                i = it * 4 + u
                if ahead:
                    j = i + 3
                    wait_alone(sp, st_ps, ST * i)
                    wait_alone(sp, kscr_w[0], 32 * (it * 2 + 10 + u // 2) if k_job else 16 * NCH)
                    wait_alone(sp, kscr_w[1], 32 * (it * 2 + 9 + u % 2 + u // 2) if k_job else 16 * NCH)
                    load_stacks(j // H, j % H, (u + 3) % 4)
                if k_job:
                    wait_alone(sp, k_ps, i + KLEAD + 1)
                    if k_load:
                        load_ctx(u % 2, i + KLEAD + 2)
                    write_k(u % 2, i + KLEAD)
                if v_load:
                    wait_alone(sp, v_ps, i + VLEAD + 1)
                    load_ctx(2 + (u + 1) % 2, i + VLEAD + 2)

            for u in range(4):
                head(0, u, True, True, True, True, True)
            for name, row in bias.items():
                sp.dma_start(row, a[name].rearrange("(o n) -> o n", o=1)).then_inc(rows_in, 16)
            for n in range(2):
                sp.dma_start(slots[n * SL:(n + 1) * SL, :], a["L0_ffn_slot_init"]).then_inc(small_in, 16)
                sp.dma_start(slotT[:, :, n * SL:(n + 1) * SL],
                             a["ffn_slotT"].rearrange("(c p) s -> p c s", p=P)).then_inc(small_in, 16)
            sp.dma_start(tau[:, 0:1], a["L0_ffn_tau"].rearrange("(o n) -> o n", o=1).to_broadcast([P, 1])).then_inc(small_in, 16)
            with nc.allow_non_contiguous_dma("short vectors onto partitions"):
                for n, name in enumerate(("L0_attn_kln_g", "L0_attn_kln_b", "L0_attn_qln_g", "L0_attn_qln_b")):
                    sp.dma_start(gb16[:, n:n + 1], a[name].rearrange("(p o) -> p o", o=1)).then_inc(small_in, 16)
                for n, name in enumerate(("L0_ffn_ln_g", "L0_ffn_ln_b", "L0_ffn_bvp")):
                    sp.dma_start(colv[:, n, :], a[name].rearrange("(c p) -> p c", p=P)).then_inc(small_in, 16)
            with sp.Fori(1, 10, 1) as it:
                for u in range(4):
                    head(it, u, True, True, True, True, True)
            for u in range(4):
                head(10, u, True, True, u < 2, True, True)
            for u in range(4):
                head(11, u, False, u < 3, False, u < 1, True)
            for u in range(4):
                head(12, u, False, False, False, False, True)
            sp.wait_ge(vh_ready, 3 * H + 1)
            for name, dst in wt.items():
                sp.dma_start(dst, a[name].rearrange("(c p) n -> p c n", p=P)).then_inc(late_in, 16)
            with sp.Fori(13, 15, 1) as it:
                for u in range(4):
                    head(it, u, False, False, False, False, True)
            head(15, 0, False, False, False, False, True)
            for n in range(4):
                sp.wait_ge(x_new, 8 + n + 1)
                sp.dma_start(out[n].rearrange("(q p) d -> p q d", p=P), x_sb[:, 2 * n:2 * n + 2, :]).then_inc(stored, 16)
            sp.wait_ge(stored, 16 * 4)

        @block.gpsimd
        def _(pool):
            pool.memset(ident[:, :], 0.0).then_inc(consts, 1)
            pool.memset(identb[:, :], 0.0).then_inc(consts, 1)
            pool.memset(gsum[:, :], 0.0).then_inc(consts, 1)
            pool.memset(negclip[:, :], -CLIP).then_inc(consts, 1)
            pool.memset(epsc[:, :], EPS).then_inc(consts, 1)
            pool.wait_ge(consts, 5)
            for m in (ident, identb):
                pool.affine_select(out=m[:, :], in_=m[:, :], compare_op=ALU.not_equal, fill=1.0, base=0,
                                   pattern=[[-1, P]], channel_multiplier=1).then_inc(consts, 1)
            for g in range(4):
                pool.wait_ge(consts, 7 + g)
                pool.affine_select(out=gsum[:, :], in_=gsum[:, :], compare_op=ALU.not_equal, fill=1.0,
                                   base=-32 * g, pattern=[[-1, DH + 1]], channel_multiplier=1).then_inc(consts, 1)
            pool.memset(ones[:, :], 1.0).then_inc(rest_set, 1)
            pool.memset(onescol[:, :], 1.0).then_inc(rest_set, 1)
            pool.memset(spread[:, :, :], 0.0).then_inc(rest_set, 1)
            pool.memset(causal[:, :, :], 0.0).then_inc(rest_set, 1)
            pool.wait_ge(rest_set, 4)
            for n, (rep, width, base) in enumerate(((8, DH, 0), (4, 2 * DH, 0), (4, 2 * DH, DH))):
                pool.affine_select(out=spread[:, n, :].rearrange("d (r c) -> d r c", r=rep),
                                   in_=spread[:, n, :].rearrange("d (r c) -> d r c", r=rep),
                                   compare_op=ALU.not_equal, fill=1.0, base=base, pattern=[[0, rep], [-1, width]],
                                   channel_multiplier=1).then_inc(rest_set, 1)
            pool.affine_select(out=causal[:, 1, :], in_=causal[:, 1, :], compare_op=ALU.is_ge, fill=-1e30,
                               base=0, pattern=[[-1, P]], channel_multiplier=1).then_inc(rest_set, 1)

            pool.memset(vh[:, :, :, :], 0.0).then_inc(rest_set, 1)
            pool.wait_ge(rest_set, 9)
            pool.memset(vh[:, :, :, DH:DH + 1], 1.0).then_inc(rest_set, 1)

            def k_second(c, par):
                wait_alone(pool, k_r, c + 1)
                pool.tensor_copy(kparts[:, par, :, 1, :], kres[:, par, :, :]).then_inc(k_2, 1)

            def k_third(c, par):
                wait_alone(pool, k_2, c + 1)
                pool.tensor_tensor(kparts[:, par, :, 2, :], kres[:, par, :, :], kparts[:, par, :, 1, :],
                                   ALU.subtract).then_inc(k_3, 1)

            def copy_vh(slot, half, h, i):
                pool.tensor_copy(vh[:, slot, :, 0:DH],
                                 v_sb[:, bass.ds(half * 32, 32), bass.ds(h * DH, DH)]).then_inc(vh_ready, 1)

            with pool.Fori(0, KLEAD // 2, 1) as n:
                k_third(2 * n, 0)
                k_third(2 * n + 1, 1)
            pool.wait_ge(v_out, VLEAD)
            pool.wait_ge(rest_set, 10)
            copy_vh(0, 0, 0, 0)

            def head(it, u, k_job, v_job, ahead):
                i = it * 4 + u
                wait_alone(pool, flag_set, i + 1)
                clipping = pool.value_load(flag[96:97, 0:1])
                with pool.If(clipping != 0):
                    with pool.Fori(0, ST // 8, 1) as half:
                        for s in range(8):
                            n = i * ST + half * 8 + s
                            p = prob[:, s, :].rearrange("p (n q) -> p n q", n=2)
                            bound = low[:, :].unsqueeze(1).to_broadcast([P, 2, T])
                            wait_alone(pool, exp_done, n + 1)
                            pool.tensor_scalar(p, p, 1.0, None, ALU.min).then_inc(clip_step, 1)
                            wait_alone(pool, low_set, i + 1)
                            wait_alone(pool, clip_step, 3 * n + 1)
                            pool.tensor_tensor(p, p, bound, ALU.subtract).then_inc(clip_step, 1)
                            wait_alone(pool, clip_step, 3 * n + 2)
                            pool.tensor_scalar(p, p, 0.0, None, ALU.max).then_inc(clip_step, 1)
                            wait_alone(pool, clip_step, 3 * n + 3)
                            pool.tensor_tensor(p, p, bound, ALU.add).then_inc(clip_done, 1)
                with pool.Else():
                    pool.sem_inc(clip_step, 3 * ST)
                    pool.sem_inc(clip_done, ST)
                if ahead:
                    wait_alone(pool, v_out, i + VLEAD if v_job else NCH)
                    wait_alone(pool, pv_done, 8 * i)
                    copy_vh((u + 1) % 2, ((i + 1) // H) % 2, (i + 1) % H, i + 1)
                if k_job:
                    k_second(i + KLEAD, u % 2)
                    k_third(i + KLEAD, u % 2)

            for u in range(4):
                head(0, u, True, True, True)
            with pool.Fori(1, 11, 1) as it:
                for u in range(4):
                    head(it, u, True, True, True)
            for u in range(4):
                head(11, u, False, True, True)
            with pool.Fori(12, 15, 1) as it:
                for u in range(4):
                    head(it, u, False, False, True)
            for u in range(4):
                head(15, u, False, False, u < 3)

        @block.scalar
        def _(act):
            def norm_sd(k):
                act.wait_ge(ln_ag, NT * (k + 1))
                act.activation(rstd[:, :, 0], mv[:, :, 1], ACT.Sqrt, bias=epsc[:, :]).then_inc(ln_sq, 1)

            def turned(k):
                for n in range(2):
                    act.wait_ge(xnT_ps, 4 * k + n + 1)
                    act.activation(xnT[:, 0, n * 512:(n + 1) * 512], st[n][:, :], ACT.Copy).then_inc(xnT_act, 1)

            def k_first(c, par, before):
                wait(act, k_ps, c + 1)
                wait(act, kscr_w[par], 32 * before)
                act.activation(kparts[:, par, :, 0, :], kps[:, :].rearrange("p (g t) -> p g t", g=2),
                               ACT.Copy).then_inc(k_1, 1)

            def v_copy(bank, c):
                wait(act, v_ps, c + 1)
                act.activation(v_sb[:, bass.ds((c * 2) % 64, 2), :].rearrange("p n d -> p (n d)"),
                               bank[:, :], ACT.Copy).then_inc(v_out, 1)

            k_first(0, 0, 0)
            v_copy(mxb[1], 0)
            act.wait_ge(consts, 11)
            norm_sd(0)
            k_first(1, 1, 0)
            v_copy(mxb[1], 1)
            turned(0)
            act.wait_ge(q_full, 4)
            act.activation(q1, q_sb, ACT.Copy).then_inc(q_1, 1)
            for c in range(2, 4):
                k_first(c, c % 2, c // 2)
                v_copy(mxb[1], c)
            with act.Fori(1, 4, 1) as n:
                for u in range(4):
                    k_first(n * 4 + u, u % 2, n * 2 + u // 2)
                    v_copy(mxb[1], n * 4 + u)
            k_first(16, 0, 8)
            act.wait_ge(qscr_w, 160)
            v_copy(mxb[1], 16)
            for c in range(17, KLEAD):
                k_first(c, c % 2, c // 2)

            def head(it, u, k_job, v_job):
                i = it * 4 + u
                for s in range(ST):
                    wait(act, st_ps, i * ST + s + 1)
                    if s % 2 == 0:
                        wait(act, pv_done, i * 8 + s // 2 - 3)
                    act.activation(prob[:, s % 8, :], st[bank_of[s]][:, :], ACT.Exp).then_inc(exp_done, 1)
                    if s == 1:
                        wait(act, low_ps, i + 1)
                        wait(act, clip_done, ST * i)
                        act.activation(low[:, :], misc[:, 0:T], ACT.Exp, bias=negclip[:, :]).then_inc(low_set, 1)
                    if s == 5 and k_job:
                        k_first(i + KLEAD, u % 2, it * 2 + u // 2 + KLEAD // 2)
                    if s == 13 and v_job:
                        wait(act, vh_ready, i + 1)
                        v_copy(kps, i + VLEAD)

            for u in range(4):
                head(0, u, True, True)
            with act.Fori(1, 11, 1) as it:
                for u in range(4):
                    head(it, u, True, True)
            for u in range(4):
                head(11, u, False, u < 3)
            with act.Fori(12, 16, 1) as it:
                for u in range(4):
                    head(it, u, False, False)

            act.wait_ge(head_out, NH)
            turned(1)
            norm_sd(1)
            turned(2)
            for n in range(4):
                act.wait_ge(v2_ps, n + 1)
                act.activation(v2[:, 2 * n:2 * n + 2, :].rearrange("p t d -> p (t d)"),
                               (mxb[1], acc, misc, kps)[n][:, :], ACT.Copy).then_inc(v2_out, 1)
            for t in range(NT):
                act.wait_ge(kq_c, t + 1)
                if t >= 4:
                    act.wait_ge(kq_var, t - 3)
                act.activation(sq[:, t % 4, :, :], kqc[:, t, :, :], ACT.Square).then_inc(kq_sq, 1)
            act.wait_ge(kq_var, NT)
            act.activation(hsd[:, :, :], hvar[:, :, :], ACT.Sqrt, bias=epsc[:, :], scale=1.0 / DH).then_inc(kq_sd, 1)
            act.wait_ge(gb_out, 1)
            for m in range(4):
                act.wait_ge(kqT_ps, 2 * m + 2)
                for e in range(2):
                    act.activation((qeT, qoT)[e][:, :, m * T:(m + 1) * T],
                                   (st[2], mxb[0])[m % 2][:, :].rearrange("p (g t) -> p g t", g=2), ACT.Identity,
                                   bias=gbp[:, 1 + e, 1:2], scale=gbp[:, 1 + e, 0:1]).then_inc(qT_out, 1)
            for n in range(64):
                u, j = n // 4, n % 4
                b, qt, g = u // 4, (u // 2) % 2, u % 2
                w = P * (qt + 1)
                act.wait_ge(a_max, n + 1)
                if n >= 8:
                    act.wait_ge(pT_ps, n - 7)
                for e in range(2):
                    h = 8 * g + 2 * j + e
                    act.activation(prob[:, n % 8, e * w:(e + 1) * w], (mxb[1], acc, misc, kps)[j][:, e * w:(e + 1) * w],
                                   ACT.Exp, bias=amax[:, 2 * b + qt, h:h + 1],
                                   accum_out=asum[:, 2 * b + qt, h:h + 1]).then_inc(a_exp, 1)
            turned(3)
            norm_sd(2)
            turned(4)

            act.wait_ge(cv_out, 1)
            for n in range(2):
                act.wait_ge(h_ps, n + 1)
                act.activation(hT[:, n * 512:(n + 1) * 512], (mxb[1], acc)[n][:, :], ACT.Gelu,
                               bias=cvec[:, :]).then_inc(h_out, 1)
            act.wait_ge(l_sub, 1)
            act.activation(lexp, lsub, ACT.Exp).then_inc(l_exp, 1)
            for n in range(2):
                act.wait_ge(alT_ps, n + 1)
                act.activation(alphaT[:, 4 * n:4 * n + 4, :].rearrange("p t q -> p (t q)"),
                               (mxb[1], acc)[n][0:SL, :], ACT.Copy).then_inc(alT_out, 1)
            for r in range(2):
                act.wait_ge(g_ps, r + 1)
                act.activation(rz[:, r, :], (mxb[0], kps)[r][:, :], ACT.Sigmoid).then_inc(g_rz, 1)
            for r in range(2):
                act.wait_ge(g_sum, r + 1)
                act.activation(cand[:, r, :], snew[:, r, :], ACT.Tanh).then_inc(g_n, 1)
            for n in range(2):
                act.wait_ge(v4_ps, n + 1)
                act.activation(v4[:, 2 * n:2 * n + 2, :].rearrange("p b d -> p (b d)"),
                               (mxb[1], acc)[n][0:SL, :], ACT.Copy).then_inc(v4_out, 1)
            act.wait_ge(c_sub, 1)
            act.activation(att, att, ACT.Exp).then_inc(c_exp, 1)
            act.wait_ge(y_ag, 2)
            act.activation(rstd[:, 0:2, 0], mv[:, 0:2, 1], ACT.Sqrt, bias=epsc[:, :]).then_inc(y_sd, 1)
            for n in range(2):
                act.wait_ge(svo_ps, n + 1)
                act.activation(svo[:, 2 * n:2 * n + 2, :].rearrange("p b d -> p (b d)"),
                               (mxb[1], acc)[n][0:SL, :], ACT.Copy).then_inc(svo_out, 1)

        @block.vector
        def _(dve):
            dve.memset(ctx4[C2:C2 + 1, :, 1, :], 1.0).then_inc(rows_set, 1)
            dve.memset(shrow[:, :], 0.0).then_inc(rows_set, 1)
            dve.wait_ge(rows_set, 2)
            dve.memset(shrow[96:99, :], 1.0).then_inc(rows_set, 1)
            dve.memset(kst[96:99, 0, :], 1.0).then_inc(ones_set, 1)

            def k_rest(c, par):
                wait(dve, k_1, c + 1)
                wait(dve, k_3, c - 1)
                dve.tensor_tensor(kres[:, par, :, :], kps[:, :].rearrange("p (g t) -> p g t", g=2),
                                  kparts[:, par, :, 0, :], ALU.subtract).then_inc(k_r, 1)

            def norm(k):
                for j in range(NT):
                    if k > 0 and j % 2 == 0:
                        dve.wait_ge(x_new, 4 * (k - 1) + j // 2 + 1)
                    dve.bn_stats(stats[:, j, :], x_sb[:, j, :]).then_inc(ln_st, 1)
                for j in range(NT):
                    dve.wait_ge(ln_st, NT * k + j + 1)
                    dve.bn_aggr(mv[:, j, :], stats[:, j, :]).then_inc(ln_ag, 1)
                dve.wait_ge(ln_sq, k + 1)
                dve.reciprocal(rstd[:, :, 1], rstd[:, :, 0]).then_inc(ln_rc, 1)
                dve.wait_ge(ln_rc, k + 1)
                for j in range(NT):
                    dve.tensor_scalar(xn[:, j, :], x_sb[:, j, :], mv[:, j, 0:1], rstd[:, j, 1:2],
                                      ALU.subtract, ALU.mult).then_inc(ln_xn, 1)

            def turned(k):
                for n in range(2):
                    dve.wait_ge(xnT_ps, 4 * k + n + 3)
                    dve.tensor_copy(xnT[:, 1, n * 512:(n + 1) * 512], (st[2], mxb[0])[n][:, :]).then_inc(xnT_dve, 1)

            def early_rest(c, par):
                k_rest(c, par)
                wait(dve, k_r, c + 1)
                dve.tensor_copy(kparts[:, par, :, 1, :], kres[:, par, :, :]).then_inc(k_2, 1)

            dve.wait_ge(x_in, 16)
            early_rest(0, 0)
            norm(0)
            early_rest(1, 1)
            turned(0)
            dve.wait_ge(wq_in, 32)
            for n in range(4):
                g, half = n // 2, n % 2
                dve.wait_ge(q_ps, n + 1)
                dve.tensor_scalar(q_sb[:, g, half * 512:(half + 1) * 512], (st[0], st[1], st[2], mxb[0])[n][:, :],
                                  bq[:, g:g + 1], DH ** -0.5, ALU.add, ALU.mult).then_inc(q_full, 1)
            dve.wait_ge(q_1, 1)
            dve.wait_ge(q_full, 4)
            dve.tensor_tensor(qres, q_sb, q1, ALU.subtract).then_inc(q_r1, 1)
            early_rest(2, 0)
            dve.wait_ge(q_r1, 1)
            dve.tensor_copy(q2, qres).then_inc(q_2, 1)
            early_rest(3, 1)
            dve.wait_ge(q_2, 1)
            dve.tensor_tensor(q3, qres, q2, ALU.subtract).then_inc(q_3, 1)

            with dve.Fori(2, KLEAD // 2, 1) as n:
                early_rest(2 * n, 0)
                early_rest(2 * n + 1, 1)

            def reduce_step(j, par, s):
                if s == 0:
                    wait(dve, m_row, j - 1)
                wait(dve, max_ps, j * ST + s + 1)
                dve.reduce_max(mxp[:, par, s // 8, s % 8:s % 8 + 1], mxb[s % 2][:, :], AX.X).then_inc(max_red, 1)

            def shift_step(j, slot, n):
                if n == 0:
                    wait(dve, max_red, (j + 1) * ST)
                    dve.reduce_max(rowmax[:, :], mxp[:, slot % 2, :, :], AX.X).then_inc(m_row, 1)
                elif n == 1:
                    wait(dve, m_row, j + 1)
                    dve.tensor_scalar(shift[:, :], rowmax[:, :], CLIP, -CLIP, ALU.min, ALU.max).then_inc(m_clip, 1)
                elif n == 2:
                    wait(dve, m_clip, j + 1)
                    wait(dve, shift_ps, j)
                    dve.tensor_scalar(sparts[:, :, 0], shift[:, :], -1.0, None, ALU.mult).then_inc(m_1, 1)
                elif n == 3:
                    wait(dve, m_1, j + 1)
                    dve.scalar_tensor_tensor(sres[:, :], shift[:, :], -1.0, sparts[:, :, 0],
                                             ALU.mult, ALU.subtract).then_inc(m_res, 1)
                elif n == 4:
                    wait(dve, m_res, j + 1)
                    dve.tensor_copy(sparts[:, :, 1], sres[:, :]).then_inc(m_2, 1)
                elif n == 5:
                    wait(dve, m_2, j + 1)
                    dve.tensor_tensor(sparts[:, :, 2], sres[:, :], sparts[:, :, 1], ALU.subtract).then_inc(m_3, 1)
                elif n == 6:
                    wait(dve, shift_ps, j + 1)
                    dve.tensor_copy(qst[96:99, slot, :], misc[96:99, 0:T]).then_inc(shift_set, 1)
                elif n == 7:
                    wait(dve, flag_set, j)
                    dve.tensor_reduce(flagf[96:97, :], misc[96:97, 0:T], AX.X, ALU.max,
                                      apply_absolute_value=True).then_inc(flag_abs, 1)

            def max_step(it, u, s, near, far):
                i = it * 4 + u
                if s < 8 and near:
                    reduce_step(i + 1, (u + 1) % 2, s + 8)
                elif s >= 8 and far:
                    reduce_step(i + 2, u % 2, s - 8)
                if s >= 8 and near:
                    shift_step(i + 1, (u + 1) % 4, s - 8)

            for s in range(8):
                reduce_step(0, 0, s)
            for s in range(ST):
                max_step(-1, 3, s, True, True)

            def take_sums(i):
                wait(dve, fin_ps, i + 1)
                dve.reciprocal(rcp[:, :], done[:, :, DH]).then_inc(fin_rcp, 1)

            def normalise(i):
                wait(dve, fin_rcp, i + 1)
                dve.tensor_tensor(o_sb[:, bass.ds(i // H, 1), :, bass.ds(i % H * DH, DH)]
                                  .rearrange("p o q d -> p (o q) d"), done[:, :, 0:DH],
                                  rcp[:, :].unsqueeze(2).to_broadcast([P, QT, DH]), ALU.mult).then_inc(head_out, 1)

            done = misc[:, 0:64].rearrange("p (q d) -> p q d", q=2)

            def save_acc(i):
                wait(dve, pv_done, 8 * (i + 1))
                wait(dve, fin_ps, i)
                dve.tensor_copy(accs[:, :], acc[:, 0:T]).then_inc(acc_out, 1)

            def head(it, u, k_job, near, far):
                i = it * 4 + u
                first = isinstance(it, int) and i == 0
                wait(dve, flag_abs, i + 1)
                wait(dve, clip_done, ST * i)
                dve.tensor_scalar(flag[96:97, :], flagf[96:97, :], NEAR, None, ALU.is_gt).then_inc(flag_set, 1)
                for s in range(ST):
                    max_step(it, u, s, near, far)
                    if s == 2 and not first:
                        save_acc(i - 1)
                    if s == 6 and k_job:
                        k_rest(i + KLEAD, u % 2)
                    if s == 9 and not first:
                        take_sums(i - 1)
                    if s == 11 and not first:
                        normalise(i - 1)

            for u in range(4):
                head(0, u, True, True, True)
            with dve.Fori(1, 11, 1) as it:
                for u in range(4):
                    head(it, u, True, True, True)
            with dve.Fori(11, 15, 1) as it:
                for u in range(4):
                    head(it, u, False, True, True)
            for u in range(4):
                head(15, u, False, u < 3, u < 2)
            save_acc(NH - 1)
            take_sums(NH - 1)
            normalise(NH - 1)

            def add_out(k, banks):
                for n in range(4):
                    dve.wait_ge(out_ps, 4 * k + n + 1)
                    xs = x_sb[:, 2 * n:2 * n + 2, :].rearrange("p t d -> p (t d)")
                    dve.tensor_tensor(xs, xs, banks[n][:, :], ALU.add).then_inc(x_new, 1)

            four = (mxb[1], acc, misc, kps)
            turned(1)
            add_out(0, four)
            norm(1)
            dve.wait_ge(gb_ps, 1)
            dve.tensor_scalar(gbp[:, :, :].rearrange("p n k -> p (n k)"), misc[:, 0:6], D ** -0.25, None,
                              ALU.mult).then_inc(gb_out, 1)
            turned(2)
            ring = (st[0], st[1], st[2], mxb[0])
            for t in range(NT):
                kq = ring[t % 4][:, :].rearrange("p (h d) -> p h d", d=DH)
                dve.wait_ge(kq_ps, t + 1)
                dve.reduce_sum(hsum[:, t, :], kq, AX.X).then_inc(kq_sum, 1)
                dve.wait_ge(kq_sum, t + 1)
                dve.scalar_tensor_tensor(kqc[:, t, :, :], hsum[:, t, :].unsqueeze(2).to_broadcast([P, 2 * H, DH]),
                                         -1.0 / DH, kq, ALU.mult, ALU.add).then_inc(kq_c, 1)
            for t in range(NT):
                dve.wait_ge(kq_sq, t + 1)
                dve.reduce_sum(hvar[:, t, :], sq[:, t % 4, :, :], AX.X).then_inc(kq_var, 1)
            dve.wait_ge(kq_sd, 1)
            dve.reciprocal(hrs[:, :, :], hsd[:, :, :]).then_inc(kq_rs, 1)
            dve.wait_ge(kq_rs, 1)
            for t in range(NT):
                dve.tensor_tensor(kqc[:, t, :, :], kqc[:, t, :, :],
                                  hrs[:, t, :].unsqueeze(2).to_broadcast([P, 2 * H, DH]), ALU.mult).then_inc(kq_n, 1)
            dve.wait_ge(gb_out, 1)
            for m in range(4):
                dve.wait_ge(kqT_ps, 2 * m + 1)
                dve.tensor_scalar(kT[:, :, m * T:(m + 1) * T], ring[m % 2][:, :].rearrange("p (g t) -> p g t", g=2),
                                  gbp[:, 0, 0:1], gbp[:, 0, 1:2], ALU.mult, ALU.add).then_inc(kT_out, 1)

            def a_maxima(n):
                u, j = n // 4, n % 4
                b, qt, g = u // 4, (u // 2) % 2, u % 2
                w = P * (qt + 1)
                h = 8 * g + 2 * j
                dve.wait_ge(a_ps, n + 1)
                dve.tensor_reduce(amax[:, 2 * b + qt, h:h + 2], four[j][:, 0:2 * w].rearrange("p (e k) -> p e k", e=2),
                                  AX.X, ALU.max, negate=True).then_inc(a_max, 1)

            def a_turned(n):
                qt = (n // 8) % 2
                w = 2 * P * (qt + 1)
                dve.wait_ge(pT_ps, n + 1)
                if n >= 4:
                    dve.wait_ge(o2_ps, n - 3)
                dve.tensor_copy(probT[:, n % 4, 0:w], st[n % 2][:, 0:w]).then_inc(pT_out, 1)

            def a_norm(t):
                dve.wait_ge(o2_ps, 8 * t + 8)
                dve.wait_ge(a_exp, 16 * t + 16)
                dve.reciprocal(arcp[:, t, :], asum[:, t, :]).then_inc(o2_rc, 1)
                dve.wait_ge(o2_rc, t + 1)
                dve.tensor_tensor(xn[:, t, :].rearrange("p (h d) -> p h d", d=DH),
                                  (st[2], mxb[0])[t % 2][:, 0:D].rearrange("p (h d) -> p h d", d=DH),
                                  arcp[:, t, :].unsqueeze(2).to_broadcast([P, H, DH]), ALU.mult).then_inc(o2_out, 1)

            for n in range(4):
                a_maxima(n)
            for n in range(64):
                a_turned(n)
                if n + 4 < 64:
                    a_maxima(n + 4)
                if n % 8 == 2 and n > 8:
                    a_norm(n // 8 - 1)
            a_norm(7)
            turned(3)
            add_out(1, four)
            norm(2)

            dve.reduce_sum(smean[:, 0, :], slotT[:, :, 0:SL], AX.X).then_inc(sm_out, 1)
            dve.wait_ge(sm_out, 1)
            dve.tensor_scalar(smean[:, 1, :], smean[:, 0, :], 1.0 / SL, None, ALU.mult).then_inc(sm_out, 1)
            dve.scalar_tensor_tensor(tau[:, 1:2], tau[:, 0:1], -1.0, tau[:, 0:1], ALU.mult, ALU.max).then_inc(tau_a, 1)
            dve.wait_ge(tau_a, 1)
            dve.tensor_scalar(tau[:, 2:3], tau[:, 1:2], 0.1, None, ALU.add).then_inc(tau_a, 1)
            dve.wait_ge(tau_a, 2)
            dve.reciprocal(tau[:, 3:4], tau[:, 2:3]).then_inc(tau_out, 1)
            dve.wait_ge(cv_ps, 1)
            dve.tensor_copy(cvec[:, :], kps[:, 0:1]).then_inc(cv_out, 1)
            turned(4)
            dve.wait_ge(lg_ps, 1)
            dve.wait_ge(tau_out, 1)
            dve.tensor_scalar(lg, misc[:, :].rearrange("p (t s) -> p t s", t=NT), tau[:, 3:4], None,
                              ALU.mult).then_inc(lg_out, 1)
            dve.wait_ge(lg_out, 1)
            for t in range(NT):
                dve.max(top8[:, t, :], lg[:, t, :]).then_inc(l_top, 1)
            for t in range(NT):
                dve.wait_ge(l_top, t + 1)
                dve.match_replace(lrep[:, t, :], top8[:, t, :], lg[:, t, :], -3e38).then_inc(l_rep, 1)
            dve.tensor_tensor(lsub, lg, top8[:, :, 0:1].to_broadcast([P, NT, SL]), ALU.subtract).then_inc(l_sub, 1)
            dve.wait_ge(l_rep, NT)
            dve.tensor_tensor(lmask, lg, lrep, ALU.not_equal).then_inc(l_mask, 1)
            dve.wait_ge(l_mask, 1)
            dve.wait_ge(l_exp, 1)
            dve.tensor_tensor(lexp, lexp, lmask, ALU.mult).then_inc(l_al, 1)
            dve.wait_ge(l_al, 1)
            dve.reduce_sum(lsum[:, :, 0], lexp, AX.X).then_inc(l_sum, 1)
            dve.wait_ge(l_sum, 1)
            dve.reciprocal(lsum[:, :, 1], lsum[:, :, 0]).then_inc(l_rc, 1)
            dve.wait_ge(l_rc, 1)
            dve.tensor_tensor(alpha, lexp, lsum[:, :, 1:2].to_broadcast([P, NT, SL]), ALU.mult).then_inc(l_out, 1)
            for r in range(2):
                dve.wait_ge(si_ps, r + 1)
                dve.tensor_scalar(den[:, r, 0:1], st[r][:, D:D + 1], 1e-8, None, ALU.add).then_inc(si_den, 1)
                dve.wait_ge(si_den, r + 1)
                dve.reciprocal(den[:, r, 1:2], den[:, r, 0:1]).then_inc(si_rc, 1)
                dve.wait_ge(si_rc, r + 1)
                dve.tensor_scalar(si[:, r, :], st[r][:, 0:D], den[:, r, 1:2], None, ALU.mult).then_inc(si_out, 1)
            dve.wait_ge(siT_ps, 1)
            dve.tensor_copy(siT.rearrange("p c s -> p (c s)"), st[2][:, :]).then_inc(siT_out, 1)
            for r in range(2):
                nb = (misc, st[0])[r]
                dve.wait_ge(g_rz, r + 1)
                dve.tensor_tensor(cand[:, r, :], rz[:, r, 0:D], nb[:, D:2 * D], ALU.mult).then_inc(g_rh, 1)
                dve.wait_ge(g_rh, r + 1)
                dve.tensor_tensor(snew[:, r, :], cand[:, r, :], nb[:, 0:D], ALU.add).then_inc(g_sum, 1)
            for r in range(2):
                dve.wait_ge(g_n, r + 1)
                dve.tensor_tensor(y[:, r, :], slots[:, :], cand[:, r, :], ALU.subtract).then_inc(g_d, 1)
                dve.wait_ge(g_d, r + 1)
                dve.tensor_tensor(y[:, r, :], y[:, r, :], rz[:, r, D:2 * D], ALU.mult).then_inc(g_zd, 1)
                dve.wait_ge(g_zd, r + 1)
                dve.tensor_tensor(snew[:, r, :], cand[:, r, :], y[:, r, :], ALU.add).then_inc(g_new, 1)
            dve.wait_ge(snT_ps, 1)
            dve.tensor_copy(snT.rearrange("p c s -> p (c s)"), st[1][:, :]).then_inc(snT_out, 1)
            dve.wait_ge(qk_ps, 1)
            dve.tensor_scalar(qkT[:, 0, :], st[2][0:SL, 0:T], QS ** -0.5, None, ALU.mult).then_inc(qk_out, 1)
            dve.tensor_copy(qkT[:, 1, :], st[2][0:SL, T:2 * T]).then_inc(qk_out, 1)
            dve.wait_ge(c_ps, 1)
            sc = mxb[0][:, 0:2 * SL].rearrange("p (r s) -> p r s", r=2)
            dve.reduce_max(smx[:, :, 0], sc, AX.X).then_inc(c_max, 1)
            dve.wait_ge(c_max, 1)
            dve.tensor_tensor(att, sc, smx[:, :, 0:1].to_broadcast([P, 2, SL]), ALU.subtract).then_inc(c_sub, 1)
            dve.wait_ge(c_exp, 1)
            dve.reduce_sum(smx[:, :, 1], att, AX.X).then_inc(c_sum, 1)
            dve.wait_ge(c_sum, 1)
            dve.reciprocal(smx[:, :, 2], smx[:, :, 1]).then_inc(c_rc, 1)
            dve.wait_ge(c_rc, 1)
            dve.tensor_tensor(att, att, smx[:, :, 2:3].to_broadcast([P, 2, SL]), ALU.mult).then_inc(c_out, 1)
            dve.wait_ge(cT_ps, 1)
            dve.tensor_copy(attT.rearrange("p r s -> p (r s)"), misc[0:SL, 0:2 * P]).then_inc(cT_out, 1)
            dve.wait_ge(cm_ps, 1)
            dve.wait_ge(g_new, 2)
            dve.tensor_tensor(y, snew, kps[:, :].rearrange("p (r d) -> p r d", r=2), ALU.add).then_inc(y_out, 1)
            dve.wait_ge(y_out, 1)
            for r in range(2):
                dve.bn_stats(stats[:, r, :], y[:, r, :]).then_inc(y_st, 1)
                dve.wait_ge(y_st, r + 1)
                dve.bn_aggr(mv[:, r, :], stats[:, r, :]).then_inc(y_ag, 1)
            dve.wait_ge(y_sd, 1)
            dve.reciprocal(rstd[:, 0:2, 1], rstd[:, 0:2, 0]).then_inc(y_rs, 1)
            dve.wait_ge(y_rs, 1)
            for r in range(2):
                dve.tensor_scalar(y[:, r, :], y[:, r, :], mv[:, r, 0:1], rstd[:, r, 1:2],
                                  ALU.subtract, ALU.mult).then_inc(y_n, 1)
            dve.wait_ge(yT_ps, 1)
            for c in range(2):
                dve.tensor_scalar(yT[:, c, :], st[0][:, c * T:(c + 1) * T], colv[:, 0, c:c + 1], colv[:, 1, c:c + 1],
                                  ALU.mult, ALU.add).then_inc(yT_out, 1)
            dve.wait_ge(sv_ps, 1)
            for m in range(2):
                dve.tensor_scalar(svT[:, m, :], st[1][:, m * T:(m + 1) * T], colv[:, 2, m:m + 1], None,
                                  ALU.add).then_inc(sv_out, 1)
            add_out(2, (st[2], mxb[0], misc, kps))

        @block.tensor
        def _(pe):
            def turn(k, src, ready, per):
                for n in range(4):
                    c, half = n // 2, n % 2
                    bank = (st[0], st[1], st[2], mxb[0])[n]
                    for j in range(4):
                        t = half * 4 + j
                        if c == 0:
                            pe.wait_ge(ready, per(t))
                        tr = pe.transpose(bank[:, j * P:(j + 1) * P], src(t, c), ident[:, :])
                    tr.then_inc(xnT_ps, 1)

            def normed(t, c):
                return xn[:, t, c * P:(c + 1) * P]

            def project_k(slot, g):
                for n in range(2):
                    rows = P if n == 0 else C2 + 1
                    mm = pe.matmul(kps[:, g * CH:(g + 1) * CH], wk[0:rows, n, g * P:(g + 1) * P],
                                   ctx4[0:rows, slot, n, :], start=(n == 0), stop=(n == 1))
                if g == 1:
                    mm.then_inc(k_ps, 1)

            def project_v(bank, slot, t):
                for n in range(2):
                    rows = P if n == 0 else C2 + 1
                    mm = pe.matmul(bank[:, t * D:(t + 1) * D], ctx4[0:rows, slot, n, t * P:(t + 1) * P],
                                   wv[0:rows, n, :], start=(n == 0), stop=(n == 1))
                if t == 1:
                    mm.then_inc(v_ps, 1)

            def max_step(j, slot, s):
                qt, n = s // 8, s % 8
                wait(pe, max_red, j * ST + s - 1)
                pe.matmul(mxb[s % 2][:, :], qst[0:96, slot, qt * P:(qt + 1) * P],
                          kst[0:96, slot, n * 512:(n + 1) * 512], start=True, stop=True).then_inc(max_ps, 1)

            def max_ahead(it, u, s, near, far):
                i = it * 4 + u
                if s < 8 and near:
                    max_step(i + 1, (u + 1) % 4, s + 8)
                elif s >= 8 and far:
                    if s == 8:
                        wait(pe, stacks_in[(u + 2) % 4], 128 * (it + (u + 2) // 4 + 1))
                    max_step(i + 2, (u + 2) % 4, s - 8)
                if s == 14 and near:
                    wait(pe, m_3, i + 2)
                    wait(pe, head_out, i)
                    wait(pe, low_set, i + 1)
                    for qt in range(QT):
                        mm = pe.matmul(misc[96:99, qt * P:(qt + 1) * P], sparts[:, qt, :], identb[:, :],
                                       start=True, stop=True)
                    mm.then_inc(shift_ps, 1)

            def early_job(c, round_, slot):
                wait(pe, ctx_in[slot], 32 * round_ + 32)
                wait(pe, k_r, c)
                for g in range(2):
                    project_k(slot, g)
                wait(pe, v_out, c)
                for t in range(2):
                    project_v(mxb[1], slot, t)

            pe.wait_ge(rows_set, 3)
            pe.wait_ge(w_in, 16 * 6)
            early_job(0, 0, 0)
            early_job(1, 0, 1)
            pe.wait_ge(consts, 11)
            turn(0, normed, ln_xn, lambda t: t + 1)
            pe.wait_ge(xnT_act, 2)
            pe.wait_ge(xnT_dve, 2)
            pe.wait_ge(wq_in, 32)
            for n in range(4):
                g, half = n // 2, n % 2
                for c in range(2):
                    mm = pe.matmul((st[0], st[1], st[2], mxb[0])[n][:, :], wq[:, c, g * P:(g + 1) * P],
                                   xnT[:, c, half * 512:(half + 1) * 512], start=(c == 0), stop=(c == 1))
                mm.then_inc(q_ps, 1)
            early_job(2, 0, 2)
            early_job(3, 0, 3)
            with pe.Fori(1, 4, 1) as n:
                for u in range(4):
                    early_job(4 * n + u, n, u)
            early_job(16, 4, 0)
            for c in range(17, KLEAD):
                pe.wait_ge(ctx_in[c % 4], 32 * 5)
                pe.wait_ge(k_r, c)
                for g in range(2):
                    project_k(c % 4, g)
            pe.wait_ge(q_full, 4)
            pe.wait_ge(stacks_in[0], 128)
            pe.wait_ge(v_out, VLEAD)
            for s in range(8):
                max_step(0, 0, s)
            for s in range(ST):
                max_ahead(-1, 3, s, True, True)

            def pv_group(i, par, g):
                wait(pe, exp_done, i * ST + 2 * g + 2)
                wait(pe, clip_done, i * ST + 2 * g + 2)
                for r in range(4):
                    n = 4 * g + r
                    mm = pe.matmul(acc[32 * r:32 * r + 32, 0:T], vh[:, par, n, :],
                                   prob[:, (n // 2) % 8, (n % 2) * T:(n % 2 + 1) * T],
                                   start=(g == 0), stop=(g == 7), skip_group_check=True)
                mm.then_inc(pv_done, 1)

            def finish(i):
                wait(pe, acc_out, i + 1)
                for qt in range(QT):
                    mm = pe.matmul(misc[:, qt * 32:qt * 32 + DH + 1], accs[:, qt * P:(qt + 1) * P], gsum[:, :],
                                   start=True, stop=True)
                mm.then_inc(fin_ps, 1)

            def head(it, u, k_job, v_job, near, far):
                i = it * 4 + u
                first = isinstance(it, int) and i == 0
                for s in range(ST):
                    if s == 0:
                        wait(pe, shift_set, i + 1)
                        wait(pe, exp_done, i * ST - 3)
                    elif s == 1:
                        wait(pe, exp_done, i * ST)
                    elif s >= 3:
                        wait(pe, exp_done, i * ST + (s - 2 if s < 15 else 14))
                    for n in range(2):
                        mm = pe.matmul(st[bank_of[s]][:, n * T:(n + 1) * T],
                                       kst[0:99, u, (2 * s + n) * P:(2 * s + n + 1) * P], qst[0:99, u, :],
                                       start=True, stop=True)
                    mm.then_inc(st_ps, 1)
                    max_ahead(it, u, s, near, far)
                    if s == 0:
                        wait(pe, flag_abs, i + 1)
                        pe.matmul(misc[:, 0:T], shrow[0:99, :], qst[0:99, u, :],
                                  start=True, stop=True).then_inc(low_ps, 1)
                    if s == 1 and not first:
                        pv_group(i - 1, (u + 1) % 2, 7)
                    if s in (2, 4) and k_job:
                        if s == 2:
                            wait(pe, ctx_in[u % 2], 32 * (it * 2 + u // 2 + 6))
                            wait(pe, k_r, i + KLEAD)
                            wait(pe, v_out, i + VLEAD)
                        project_k(u % 2, (s - 2) // 2)
                    if s in (10, 12) and v_job:
                        if s == 10:
                            wait(pe, ctx_in[2 + (u + 1) % 2], 32 * (it * 2 + u // 2 + 6))
                            wait(pe, k_r, i + KLEAD + 1 if k_job else NCH)
                            wait(pe, v_out, i + VLEAD)
                        project_v(kps, 2 + (u + 1) % 2, (s - 10) // 2)
                    if s % 2 == 1 and s >= 3:
                        if s == 3:
                            wait(pe, vh_ready, i + 1)
                            wait(pe, acc_out, i)
                        pv_group(i, u % 2, (s - 3) // 2)
                    if s == 6 and not first:
                        wait(pe, low_set, i + 1)
                        finish(i - 1)

            pe.wait_ge(ones_set, 1 + 16 * 3)
            for u in range(4):
                head(0, u, True, True, True, True)
            with pe.Fori(1, 11, 1) as it:
                for u in range(4):
                    head(it, u, True, True, True, True)
            for u in range(4):
                head(11, u, False, u < 3, True, True)
            with pe.Fori(12, 15, 1) as it:
                for u in range(4):
                    head(it, u, False, False, True, True)
            for u in range(4):
                head(15, u, False, False, u < 3, u < 2)
            pv_group(NH - 1, 1, 7)
            finish(NH - 1)

            four = (mxb[1], acc, misc, kps)

            pe.wait_ge(late_in, 16 * len(wt))
            pe.wait_ge(rows_in, 16 * len(bias))
            pe.wait_ge(rest_set, 10)
            pe.wait_ge(small_in, 16 * 12)
            turn(1, lambda t, c: o_sb[:, t // 2, t % 2, c * P:(c + 1) * P], head_out, lambda t: NH)
            pe.wait_ge(xnT_act, 4)
            pe.wait_ge(xnT_dve, 4)
            for n in range(4):
                for j in range(2):
                    t = 2 * n + j
                    to = four[n][:, j * D:(j + 1) * D]
                    pe.matmul(to, ones[0:1, 0:P], bias["L0_xattn_bo"], start=True, stop=False)
                    for c in range(2):
                        mm = pe.matmul(to, xnT[:, c, t * P:(t + 1) * P], wt["L0_xattn_Wo"][:, c, :],
                                       start=False, stop=(c == 1))
                mm.then_inc(out_ps, 1)

            pe.wait_ge(x_new, 4)
            pe.matmul(misc[:, 0:2], spread[:, 0, :], gb16[:, 0:2], start=True, stop=True)
            for n in range(1, 3):
                mm = pe.matmul(misc[:, 2 * n:2 * n + 2], spread[:, n, :], gb16[:, 2:4], start=True, stop=True)
            mm.then_inc(gb_ps, 1)
            turn(2, normed, ln_xn, lambda t: NT + t + 1)
            pe.wait_ge(xnT_act, 6)
            pe.wait_ge(xnT_dve, 6)
            ring = (st[0], st[1], st[2], mxb[0])
            pe.wait_ge(gb_out, 1)
            for t in range(NT):
                if t >= 4:
                    pe.wait_ge(kq_c, t - 3)
                for c in range(2):
                    mm = pe.matmul(ring[t % 4][:, :], xnT[:, c, t * P:(t + 1) * P], wt["attn_WkqT"][:, c, :],
                                   start=(c == 0), stop=(c == 1))
                mm.then_inc(kq_ps, 1)
                for c in range(2):
                    mm = pe.matmul(four[t // 2][:, (t % 2) * D:(t % 2 + 1) * D], xnT[:, c, t * P:(t + 1) * P],
                                   wt["attn_WvT"][:, c, :], start=(c == 0), stop=(c == 1))
                if t % 2:
                    mm.then_inc(v2_ps, 1)
            pe.wait_ge(kq_c, NT)
            for m in range(4):
                for which in range(2):
                    bank = ring[which * 2 + m % 2]
                    if m >= 2:
                        pe.wait_ge(qT_out if which else kT_out, 2 * (m - 1) if which else m - 1)
                    for g in range(2):
                        for j in range(2):
                            t = 2 * m + j
                            pe.wait_ge(kq_n, t + 1)
                            tr = pe.transpose(bank[:, (g * 2 + j) * P:(g * 2 + j + 1) * P],
                                              kqc[:, t, which * H + 8 * g:which * H + 8 * g + 8, :], ident[:, :])
                    tr.then_inc(kqT_ps, 1)

            def a_scores(n):
                u, j = n // 4, n % 4
                b, qt, g = u // 4, (u // 2) % 2, u % 2
                w = P * (qt + 1)
                tok = b * T + qt * P
                if n >= 4:
                    pe.wait_ge(a_exp, 2 * (n - 4) + 2)
                for e in range(2):
                    to = four[j][:, e * w:(e + 1) * w]
                    pe.matmul(to, identb[:, :], causal[:, 1 - qt:2, :], start=True, stop=False)
                    mm = pe.matmul(to, (qeT, qoT)[e][32 * j:32 * j + 32, g, tok:tok + P],
                                   kT[32 * j:32 * j + 32, g, b * T:b * T + w], start=False, stop=True)
                mm.then_inc(a_ps, 1)

            def a_turn(n):
                u, j = n // 4, n % 4
                qt = (u // 2) % 2
                w = P * (qt + 1)
                if n >= 2:
                    pe.wait_ge(pT_out, n - 1)
                pe.wait_ge(a_exp, 2 * n + 2)
                for e in range(2):
                    for kt in range(qt + 1):
                        s = (e * (qt + 1) + kt) * P
                        tr = pe.transpose(st[n % 2][:, s:s + P], prob[:, n % 8, e * w + kt * P:e * w + (kt + 1) * P],
                                          ident[:, :])
                tr.then_inc(pT_ps, 1)

            def a_values(n):
                u, j = n // 4, n % 4
                b, qt, g = u // 4, (u // 2) % 2, u % 2
                t = b * 2 + qt
                pe.wait_ge(pT_out, n + 1)
                if n % 8 == 0 and n >= 16:
                    pe.wait_ge(o2_out, t - 1)
                for e in range(2):
                    h = 8 * g + 2 * j + e
                    for kt in range(qt + 1):
                        s = (e * (qt + 1) + kt) * P
                        mm = pe.matmul((st[2], mxb[0])[t % 2][:, h * DH:(h + 1) * DH],
                                       probT[:, n % 4, s:s + P], v2[:, 2 * b + kt, h * DH:(h + 1) * DH],
                                       start=(kt == 0), stop=(kt == qt))
                mm.then_inc(o2_ps, 1)

            pe.wait_ge(kT_out, 4)
            pe.wait_ge(qT_out, 8)
            pe.wait_ge(v2_out, 4)
            for n in range(4):
                a_scores(n)
            for n in range(64):
                a_turn(n)
                if n + 4 < 64:
                    a_scores(n + 4)
                if n >= 1:
                    a_values(n - 1)
            a_values(63)
            turn(3, normed, o2_out, lambda t: t + 1)
            pe.wait_ge(xnT_act, 8)
            pe.wait_ge(xnT_dve, 8)
            for n in range(4):
                for j in range(2):
                    t = 2 * n + j
                    to = four[n][:, j * D:(j + 1) * D]
                    pe.matmul(to, ones[0:1, 0:P], bias["L0_attn_bo"], start=True, stop=False)
                    for c in range(2):
                        mm = pe.matmul(to, xnT[:, c, t * P:(t + 1) * P], wt["attn_WoT"][:, c, :],
                                       start=False, stop=(c == 1))
                mm.then_inc(out_ps, 1)

            pe.wait_ge(sm_out, 2)
            pe.wait_ge(x_new, 8)
            for c in range(2):
                pe.matmul(kps[:, 0:1], wt["L0_ffn_w1"][:, 2 + c, :], smean[:, 1, c:c + 1], start=(c == 0), stop=False)
            pe.matmul(kps[:, 0:1], bias["L0_ffn_b1"], ones[0:1, 0:1], start=False, stop=True).then_inc(cv_ps, 1)
            turn(4, normed, ln_xn, lambda t: 2 * NT + t + 1)
            pe.wait_ge(xnT_act, 10)
            pe.wait_ge(xnT_dve, 10)
            for n in range(2):
                for c in range(2):
                    mm = pe.matmul(four[n][:, :], wt["L0_ffn_w1"][:, c, :], xnT[:, c, n * 512:(n + 1) * 512],
                                   start=(c == 0), stop=(c == 1))
                mm.then_inc(h_ps, 1)
            for t in range(NT):
                pe.wait_ge(h_out, t // 4 + 1)
                to = misc[:, t * SL:(t + 1) * SL]
                pe.matmul(to, ones[0:1, 0:P], bias["L0_ffn_b2"], start=True, stop=False)
                mm = pe.matmul(to, hT[:, t * P:(t + 1) * P], wt["L0_ffn_w2"][:, 0, :], start=False, stop=True)
            mm.then_inc(lg_ps, 1)
            pe.wait_ge(l_out, 1)
            for b in range(B):
                rows = slice((b % 2) * SL, (b % 2 + 1) * SL)
                for q in range(2):
                    pe.matmul(st[b // 2][rows, 0:D], alpha[:, 2 * b + q, :], xn[:, 2 * b + q, :],
                              start=(q == 0), stop=(q == 1))
                for q in range(2):
                    mm = pe.matmul(st[b // 2][rows, D:D + 1], alpha[:, 2 * b + q, :], onescol[:, :],
                                   start=(q == 0), stop=(q == 1))
                if b % 2:
                    mm.then_inc(si_ps, 1)
            for t in range(NT):
                tr = pe.transpose(four[t // 4][0:SL, (t % 4) * P:(t % 4 + 1) * P], alpha[:, t, :], ident[:, :])
                if t % 4 == 3:
                    tr.then_inc(alT_ps, 1)
            pe.wait_ge(si_out, 2)
            for c in range(2):
                for r in range(2):
                    tr = pe.transpose(st[2][:, (c * 2 + r) * P:(c * 2 + r + 1) * P], si[:, r, c * P:(c + 1) * P],
                                      ident[:, :])
            tr.then_inc(siT_ps, 1)
            pe.wait_ge(siT_out, 1)
            pe.wait_ge(lg_out, 1)
            pe.wait_ge(si_out, 2)
            wih, whh = wt["ffn_WihT"], wt["ffn_WhhT"]
            for r in range(2):
                rzb, nb = ((mxb[0], misc), (kps, st[0]))[r]
                for n, (w, lhs) in enumerate(((wih, siT[:, :, r * P:(r + 1) * P]), (whh, slotT))):
                    row = bias[("L0_ffn_bih", "L0_ffn_bhh")[n]]
                    for c in range(2):
                        pe.matmul(rzb[:, :], lhs[:, c, :], w[:, c, 0:2 * D], start=(n == 0 and c == 0), stop=False)
                    pe.matmul(rzb[:, :], ones[0:1, 0:P], row[:, 0:2 * D], start=False, stop=(n == 1))
                for n, (w, lhs) in enumerate(((wih, siT[:, :, r * P:(r + 1) * P]), (whh, slotT))):
                    row = bias[("L0_ffn_bih", "L0_ffn_bhh")[n]]
                    to = nb[:, n * D:(n + 1) * D]
                    for c in range(2):
                        pe.matmul(to, lhs[:, c, :], w[:, c, 2 * D:3 * D], start=(c == 0), stop=False)
                    mm = pe.matmul(to, ones[0:1, 0:P], row[:, 2 * D:3 * D], start=False, stop=True)
                mm.then_inc(g_ps, 1)
            for c in range(2):
                for r in range(2):
                    pe.wait_ge(g_new, r + 1)
                    tr = pe.transpose(st[1][:, (c * 2 + r) * P:(c * 2 + r + 1) * P], snew[:, r, c * P:(c + 1) * P],
                                      ident[:, :])
            tr.then_inc(snT_ps, 1)
            pe.wait_ge(snT_out, 1)
            for n, (w, row) in enumerate((("L0_ffn_wq", "L0_ffn_bq"), ("L0_ffn_wk", "L0_ffn_bk"))):
                to = st[2][0:SL, n * T:(n + 1) * T]
                for c in range(2):
                    pe.matmul(to, wt[w][:, c, :], snT[:, c, :], start=(c == 0), stop=False)
                mm = pe.matmul(to, bias[row], ones[0:1, 0:T], start=False, stop=True)
            mm.then_inc(qk_ps, 1)
            pe.wait_ge(alT_out, 2)
            for b in range(B):
                to = (mxb[1], acc)[b // 2][0:SL, (b % 2) * D:(b % 2 + 1) * D]
                for c in range(2):
                    pe.matmul(to, snT[:, c, b * SL:(b + 1) * SL], wt["L0_ffn_wv"][:, c, :], start=(c == 0), stop=False)
                mm = pe.matmul(to, ones[0:1, 0:SL], bias["L0_ffn_bv"], start=False, stop=True)
                if b % 2:
                    mm.then_inc(v4_ps, 1)
            pe.wait_ge(qk_out, 2)
            for b in range(B):
                mm = pe.matmul(mxb[0][(b % 2) * SL:(b % 2 + 1) * SL, (b // 2) * SL:(b // 2 + 1) * SL],
                               qkT[:, 0, b * SL:(b + 1) * SL], qkT[:, 1, b * SL:(b + 1) * SL], start=True, stop=True)
            mm.then_inc(c_ps, 1)
            pe.wait_ge(c_out, 1)
            for r in range(2):
                tr = pe.transpose(misc[0:SL, r * P:(r + 1) * P], att[:, r, :], ident[:, :])
            tr.then_inc(cT_ps, 1)
            pe.wait_ge(cT_out, 1)
            pe.wait_ge(v4_out, 2)
            for b in range(B):
                mm = pe.matmul(kps[(b % 2) * SL:(b % 2 + 1) * SL, (b // 2) * D:(b // 2 + 1) * D],
                               attT[:, b // 2, (b % 2) * SL:(b % 2 + 1) * SL], v4[:, b, :], start=True, stop=True)
            mm.then_inc(cm_ps, 1)
            pe.wait_ge(y_n, 2)
            for c in range(2):
                for r in range(2):
                    tr = pe.transpose(st[0][:, (c * 2 + r) * P:(c * 2 + r + 1) * P], y[:, r, c * P:(c + 1) * P],
                                      ident[:, :])
            tr.then_inc(yT_ps, 1)
            pe.wait_ge(yT_out, 2)
            for m in range(2):
                for c in range(2):
                    mm = pe.matmul(st[1][:, m * T:(m + 1) * T], wt["L0_ffn_wvp"][:, c, m * P:(m + 1) * P],
                                   yT[:, c, :], start=(c == 0), stop=(c == 1))
            mm.then_inc(sv_ps, 1)
            pe.wait_ge(sv_out, 2)
            for b in range(B):
                to = (mxb[1], acc)[b // 2][0:SL, (b % 2) * D:(b % 2 + 1) * D]
                for m in range(2):
                    mm = pe.matmul(to, svT[:, m, b * SL:(b + 1) * SL], wt["L0_ffn_wo"][:, m, :],
                                   start=(m == 0), stop=(m == 1))
                if b % 2:
                    mm.then_inc(svo_ps, 1)
            last = (st[2], mxb[0], misc, kps)
            pe.wait_ge(y_out, 1)
            for n in range(4):
                pe.wait_ge(svo_out, n // 2 + 1)
                for j in range(2):
                    t = 2 * n + j
                    to = last[n][:, j * D:(j + 1) * D]
                    pe.matmul(to, ones[0:1, 0:P], bias["L0_ffn_bo"], start=True, stop=False)
                    mm = pe.matmul(to, alphaT[:, t, :], svo[:, n, :], start=False, stop=True)
                mm.then_inc(out_ps, 1)


def kernel(**inputs):
    import numpy as np
    import concourse.bacc as bacc
    from concourse.bass_utils import run_bass_kernel_spmd as run

    arrays = {k: np.ascontiguousarray(v) for k, v in inputs.items() if k != "ctx_768"}
    ctx = np.ascontiguousarray(inputs["ctx_768"]).reshape(NCH, CH, C)
    arrays["ctxT"] = np.ascontiguousarray(ctx.transpose(0, 2, 1))
    for name, key in (("attn_WvT", "L0_attn_Wv"), ("attn_WoT", "L0_attn_Wo"), ("ffn_WihT", "L0_ffn_Wih"),
                      ("ffn_WhhT", "L0_ffn_Whh"), ("ffn_slotT", "L0_ffn_slot_init")):
        arrays[name] = np.ascontiguousarray(arrays[key].T)
    arrays["attn_WkqT"] = np.ascontiguousarray(
        np.concatenate([arrays["L0_attn_Wk"], arrays["L0_attn_Wq"]], axis=0).T)
    for key in ("L0_attn_Wv", "L0_attn_Wo", "L0_attn_Wk", "L0_attn_Wq", "L0_ffn_Wih", "L0_ffn_Whh"):
        del arrays[key]
    nc = bacc.Bacc("TRN2", target_bir_lowering=False, num_devices=1)
    aps = {k: nc.dram_tensor("in_" + k, v.shape, mybir.dt.from_np(v.dtype), kind="ExternalInput").ap()
           for k, v in arrays.items()}
    out = nc.dram_tensor("out", (B, T, D), F32, kind="ExternalOutput").ap()
    build(nc, aps, out)
    r = run(nc, [{"in_" + k: v for k, v in arrays.items()}], core_ids=[0])
    return r.results[0]["out"]
```

```python
from contextlib import ExitStack

import concourse.bass as bass
from concourse import mybir

ALU = mybir.AluOpType
ACT = mybir.ActivationFunctionType
F32 = mybir.dt.float32
BF16 = mybir.dt.bfloat16
I32 = mybir.dt.int32
AX = mybir.AxisListType

P = 128
B, T, D = 4, 256, 256
S, C = 4096, 192
H = 16
DH = D // H
NT = B * T // P
QT = T // P
NH = B * H
C2 = C - P
CH = 256
NCH = B * S // CH
KLEAD, VLEAD = 20, 17
ST = 16
CLIP = 10000.0
EPS = 1e-5
SL = 64
FH = 128
QS = D // 4
NEAR = 9800.0


def build(nc, a, out):
    with ExitStack() as ctx:
        def sb(name, shape, dt=F32):
            return ctx.enter_context(nc.sbuf_tensor(name, shape, dt))

        def psum(name):
            return ctx.enter_context(nc.psum_tensor(name, [P, 512], F32))

        def sem(name):
            return ctx.enter_context(nc.semaphore(name))

        st = [psum(f"st{n}") for n in range(3)]
        mxb = [psum(f"mx{n}") for n in range(2)]
        acc = psum("acc")
        misc = psum("misc")
        kps = psum("kps")

        x_sb = sb("x_sb", [P, NT, D])
        xn = sb("xn", [P, NT, D])
        xnT = sb("xnT", [P, 2, B * T])
        o_sb = sb("o_sb", [P, B, QT, D])
        v_sb = sb("v_sb", [P, 64, D])
        kst = sb("kst", [P, 4, S], BF16)
        qst = sb("qst", [P, 4, T], BF16)
        prob = sb("prob", [P, 8, 512])
        vh = sb("vh", [P, 2, 32, 32])
        ctx4 = sb("ctx4", [P, 4, 2, CH])
        wk = sb("wk", [P, 2, D])
        wv = sb("wv", [P, 2, D])
        wq = sb("wq", [P, 2, D])
        bq = sb("bq", [P, 2])
        kparts = sb("kparts", [P, 2, 2, 3, CH], BF16)
        kres = sb("kres", [P, 2, 2, CH])
        low = sb("low", [P, T])
        accs = sb("accs", [P, T])
        mxp = sb("mxp", [P, 2, QT, 8])
        rowmax = sb("rowmax", [P, QT])
        shift = sb("shift", [P, QT])
        sres = sb("sres", [P, QT])
        sparts = sb("sparts", [P, QT, 3], BF16)
        flagf = sb("flagf", [P, 1])
        flag = sb("flag", [P, 1], I32)
        rcp = sb("rcp", [P, QT])
        stats = sb("stats", [P, NT, 6])
        mv = sb("mv", [P, NT, 2])
        rstd = sb("rstd", [P, NT, 2])
        ident = sb("ident", [P, P])
        identb = sb("identb", [P, P], BF16)
        gsum = sb("gsum", [P, DH + 1])
        shrow = sb("shrow", [P, P], BF16)
        negclip = sb("negclip", [P, 1])
        epsc = sb("epsc", [P, 1])

        ones = sb("ones", [1, 512])
        onescol = sb("onescol", [P, 1])
        brow = sb("brow", [1, 2368])
        slotT = sb("slotT", [P, 2, 2 * SL])
        slots = sb("slots", [P, D])
        colv = sb("colv", [P, 3, 2])
        tau = sb("tau", [P, 4])
        gb16 = sb("gb16", [DH, 4])
        spread = sb("spread", [DH, 3, P])
        gbp = sb("gbp", [P, 3, 2])
        causal = sb("causal", [P, P], BF16)
        bo = sb("bo", [P, 2, D])
        bias = {}
        at = 0
        for name, n in (("L0_ffn_bih", 3 * D), ("L0_ffn_bhh", 3 * D),
                        ("L0_ffn_b1", FH), ("L0_ffn_b2", SL), ("L0_ffn_bq", QS), ("L0_ffn_bk", QS),
                        ("L0_ffn_bv", D), ("L0_ffn_bo", D)):
            bias[name] = brow[0:1, at:at + n]
            at += n

        late = v_sb[:, 0:32, :].rearrange("p t d -> p (t d)")
        wt = {}
        at = 0
        for name, c, n in (("L0_xattn_Wo", 2, D), ("attn_WkqT", 2, 2 * D), ("attn_WvT", 2, D), ("attn_WoT", 2, D),
                           ("L0_ffn_w1", 4, FH), ("L0_ffn_w2", 1, SL), ("ffn_WihT", 2, 3 * D),
                           ("ffn_WhhT", 2, 3 * D), ("L0_ffn_wq", 2, QS), ("L0_ffn_wk", 2, QS),
                           ("L0_ffn_wv", 2, D), ("L0_ffn_wvp", 2, D), ("L0_ffn_wo", 2, D)):
            wt[name] = late[:, at:at + c * n].rearrange("p (c n) -> p c n", c=c)
            at += c * n
        assert at <= 32 * D
        free_v = v_sb[:, 32:64, :].rearrange("p t d -> p (t d)")
        v2e = free_v[:, 0:2048].rearrange("p (t d) -> p t d", t=NT)
        v2o = o_sb[:, :, :, :].rearrange("p b q d -> p (b q) d")
        kqc = free_v[:, 2048:6144].rearrange("p (t h d) -> p t h d", t=NT, d=DH)
        probT = (free_v[:, 6144:8192].rearrange("p (n q) -> p n q", n=4),
                 ctx4[:, :, :, :].rearrange("p n c t -> p n (c t)"))
        free_k = kst[:, :, :].rearrange("p a s -> p (a s)").bitcast(F32)
        kT = free_k[:, 0:2048].rearrange("p (g t) -> p g t", g=2)
        qeT = free_k[:, 2048:4096].rearrange("p (g t) -> p g t", g=2)
        qoT = free_k[:, 4096:6144].rearrange("p (g t) -> p g t", g=2)
        sq = free_k[:, 6144:8192].rearrange("p (t h d) -> p t h d", t=4, d=DH)
        hsum = sb("hsum", [P, NT, 2 * H])
        hvar = sb("hvar", [P, NT, 2 * H])
        hsd = sb("hsd", [P, NT, 2 * H])
        hrs = sb("hrs", [P, NT, 2 * H])
        amax = sb("amax", [P, NT, H])
        arcp = low[:, :].rearrange("p (n q) -> p n q", n=2)
        halfones = sb("halfones", [P, 2, 2 * DH])
        hT = kqc.rearrange("p t h d -> p (t h d)")[:, 0:1024]
        lg = kqc.rearrange("p t h d -> p (t h d)")[:, 1024:1536].rearrange("p (t s) -> p t s", t=NT)
        lrep = kqc.rearrange("p t h d -> p (t h d)")[:, 1536:2048].rearrange("p (t s) -> p t s", t=NT)
        lmask = kqc.rearrange("p t h d -> p (t h d)")[:, 2048:2560].rearrange("p (t s) -> p t s", t=NT)
        lsub = kqc.rearrange("p t h d -> p (t h d)")[:, 2560:3072].rearrange("p (t s) -> p t s", t=NT)
        alpha = kqc.rearrange("p t h d -> p (t h d)")[:, 3072:3584].rearrange("p (t s) -> p t s", t=NT)
        lexp = kqc.rearrange("p t h d -> p (t h d)")[:, 3584:4096].rearrange("p (t s) -> p t s", t=NT)
        si = v2e.rearrange("p t d -> p (t d)")[:, 0:512].rearrange("p (r d) -> p r d", r=2)
        siT = v2e.rearrange("p t d -> p (t d)")[:, 512:1024].rearrange("p (c s) -> p c s", c=2)
        rz = v2e.rearrange("p t d -> p (t d)")[:, 1024:2048].rearrange("p (r d) -> p r d", r=2)
        pT = probT[0].rearrange("p n q -> p (n q)")
        cand = pT[:, 0:512].rearrange("p (r d) -> p r d", r=2)
        snew = pT[:, 512:1024].rearrange("p (r d) -> p r d", r=2)
        snT = pT[:, 1024:1536].rearrange("p (c s) -> p c s", c=2)
        yT = pT[:, 1536:2048].rearrange("p (c s) -> p c s", c=2)
        fk = kT.rearrange("p g t -> p (g t)")
        qkT = fk[0:SL, 0:512].rearrange("p (n s) -> p n s", n=2)
        v4 = fk[0:SL, 512:1536].rearrange("p (b d) -> p b d", b=B)
        att = fk[:, 1536:1664].rearrange("p (r s) -> p r s", r=2)
        attT = fk[0:SL, 1664:1920].rearrange("p (r s) -> p r s", r=2)
        fq = qeT.rearrange("p g t -> p (g t)")
        y = fq[:, 0:512].rearrange("p (r d) -> p r d", r=2)
        svT = fq[:, 512:1024].rearrange("p (c s) -> p c s", c=2)
        svo = fq[0:SL, 1024:2048].rearrange("p (b d) -> p b d", b=B)
        alphaT = qoT.rearrange("p g t -> p (g t)")[0:SL, 0:1024].rearrange("p (t q) -> p t q", t=NT)
        cvec = sb("cvec", [P, 1])
        smean = sb("smean", [P, 2, 2])
        top8 = sb("top8", [P, NT, 8])
        lsum = sb("lsum", [P, NT, 2])
        den = sb("den", [P, 2, 3])
        smx = sb("smx", [P, 2, 4])

        qw = v_sb[:, 32:64, :].rearrange("p t d -> p (t d)")
        q_sb = qw[:, 0:2048].rearrange("p (g t) -> p g t", g=2)
        qres = qw[:, 2048:4096].rearrange("p (g t) -> p g t", g=2)
        q1 = qw[:, 4096:5120].bitcast(BF16).rearrange("p (g t) -> p g t", g=2)
        q2 = qw[:, 5120:6144].bitcast(BF16).rearrange("p (g t) -> p g t", g=2)
        q3 = qw[:, 6144:7168].bitcast(BF16).rearrange("p (g t) -> p g t", g=2)

        kscr = nc.dram_tensor("kscr", [D, 3, B * S], BF16, kind="Internal").ap()
        qscr1 = nc.dram_tensor("qscr1", [D, 3, B * T], BF16, kind="Internal").ap()
        qscr2 = nc.dram_tensor("qscr2", [D, B * T], BF16, kind="Internal").ap()
        qscr3 = nc.dram_tensor("qscr3", [D, B * T], BF16, kind="Internal").ap()

        x_in, w_in, wq_in, bo_in, x_bias = (sem(n) for n in ("x_in", "w_in", "wq_in", "bo_in", "x_bias"))
        consts, rest_set = sem("consts"), sem("rest_set")
        ln_st, ln_ag, ln_sq, ln_rc, ln_xn = (sem(f"ln_{n}") for n in ("stats", "aggr", "sqrt", "recip", "out"))
        xnT_ps, xnT_act, xnT_dve = sem("xnT_ps"), sem("xnT_act"), sem("xnT_dve")
        q_ps, q_full, q_1, q_r1, q_2, q_3 = (sem(f"q_{n}") for n in ("ps", "full", "1", "r1", "2", "3"))
        qscr_w = sem("qscr_written")
        rows_set, ones_set = sem("rows_set"), sem("ones_set")
        ctx_in = [sem(f"ctx_in{n}") for n in range(4)]
        k_ps, k_1, k_r, k_2, k_3 = (sem(f"k_{n}") for n in ("ps", "1", "res", "2", "3"))
        kscr_w = [sem(f"k_written{n}") for n in range(2)]
        v_ps, v_out = sem("v_ps"), sem("v_out")
        stacks_in = [sem(f"stacks_in{n}") for n in range(4)]
        vh_ready = sem("vh_ready")
        max_ps, max_red = sem("max_ps"), sem("max_red")
        m_row, m_clip, m_1, m_res, m_2, m_3 = (sem(f"m_{n}") for n in ("row", "clip", "1", "res", "2", "3"))
        shift_ps, shift_set, flag_abs, flag_set = (sem(n) for n in ("shift_ps", "shift_set", "flag_abs", "flag_set"))
        low_ps, low_set = sem("low_ps"), sem("low_set")
        st_ps, exp_done, clip_step, clip_done = (sem(n) for n in ("st_ps", "exp_done", "clip_step", "clip_done"))
        pv_done, acc_out, fin_ps, fin_rcp, head_out = (
            sem(n) for n in ("pv_done", "acc_out", "fin_ps", "fin_rcp", "head_out"))
        stored = sem("stored")
        rows_in, late_in, small_in = sem("rows_in"), sem("late_in"), sem("small_in")
        gb_ps, gb_out = sem("gb_ps"), sem("gb_out")
        out_ps, x_new = sem("out_ps"), sem("x_new")
        kq_ps, kq_sum, kq_c, kq_sq, kq_var, kq_sd, kq_rs, kq_n = (
            sem(f"kq_{n}") for n in ("ps", "sum", "centred", "square", "var", "sd", "rs", "normed"))
        v2_ps, v2_out = sem("v2_ps"), sem("v2_out")
        kqT_ps, kT_out, qT_out = sem("kqT_ps"), sem("kT_out"), sem("qT_out")
        v2_zero, a_ps, a_max, a_exp, pT_ps, pT_out, o2_ps, o2_rc, o2_out = (
            sem(f"a_{n}") for n in ("zero", "ps", "max", "exp", "pT_ps", "pT_out", "o_ps", "o_recip", "o_out"))
        sm_out, cv_ps, cv_out, tau_a, tau_out = (
            sem(n) for n in ("sm_out", "cv_ps", "cv_out", "tau_abs", "tau_out"))
        h_ps, h_out, lg_ps, lg_out, l_top, l_rep, l_mask, l_sub, l_exp, l_al, l_sum, l_out = (
            sem(f"l_{n}") for n in ("h_ps", "h", "ps", "logits", "top", "replaced", "mask", "sub", "exp", "masked",
                                    "sum", "alpha"))
        si_ps, si_den, si_rc, si_out, siT_ps, siT_out = (
            sem(f"si_{n}") for n in ("ps", "den", "recip", "out", "T_ps", "T_out"))
        g_ps, g_rz, g_rh, g_sum, g_n, g_d, g_zd, g_new = (
            sem(f"g_{n}") for n in ("ps", "rz", "rh", "sum", "cand", "diff", "zdiff", "new"))
        snT_ps, snT_out, qk_ps, qk_out, v4_ps, v4_out = (
            sem(n) for n in ("snT_ps", "snT_out", "qk_ps", "qk_out", "v4_ps", "v4_out"))
        c_ps, c_max, c_sub, c_exp, c_sum, c_out, cT_ps, cT_out, cm_ps, y_out = (
            sem(f"c_{n}") for n in ("ps", "max", "sub", "exp", "sum", "att", "attT_ps", "attT", "comm", "y"))
        y_st, y_ag, y_sd, y_rs, y_n, yT_ps, yT_out, sv_ps, sv_out, svo_ps, svo_out, alT_ps, alT_out = (
            sem(f"y_{n}") for n in ("stats", "aggr", "sd", "recip", "normed", "T_ps", "T_out", "sv_ps", "sv",
                                    "svo_ps", "svo", "alphaT_ps", "alphaT"))

        bank_of = [s % 3 for s in range(15)] + [1]

        passed = {nc.sync: sem("sp_passed"), nc.gpsimd: sem("pool_passed")}

        block = ctx.enter_context(nc.Block())

        def wait(eng, s, value):
            if not (isinstance(value, int) and value <= 0):
                eng.wait_ge(s, value)

        def wait_alone(eng, s, value):
            wait(eng, s, value)
            if not isinstance(value, int):
                eng.sem_inc(passed[eng], 1)

        @block.sync
        def _(sp):
            def load_ctx(slot, c):
                src = a["ctxT"][bass.ds(c, 1), :, :].rearrange("o c t -> (o c) t")
                sp.dma_start(ctx4[:, slot, 0, :], src[0:P, :]).then_inc(ctx_in[slot], 16)
                sp.dma_start(ctx4[0:C2, slot, 1, :], src[P:C, :]).then_inc(ctx_in[slot], 16)

            for w, name, row in ((wk, "L0_xattn_Wk", "L0_xattn_bk"), (wv, "L0_xattn_Wv", "L0_xattn_bv")):
                sp.dma_start(w[:, 0, :], a[name][0:P, :]).then_inc(w_in, 16)
                sp.dma_start(w[0:C2, 1, :], a[name][P:C, :]).then_inc(w_in, 16)
                sp.dma_start(w[C2:C2 + 1, 1, :], a[row].rearrange("(o n) -> o n", o=1)).then_inc(w_in, 16)
                if w is wk:
                    load_ctx(0, 0)
                    sp.dma_start(x_sb[:, :, :], a["x"].rearrange("b (q p) d -> p (b q) d", p=P)).then_inc(x_in, 16)
            load_ctx(1, 1)
            sp.dma_start(wq[:, :, :], a["L0_xattn_Wq"].rearrange("(c p) n -> p c n", p=P)).then_inc(wq_in, 16)
            load_ctx(2, 2)
            load_ctx(3, 3)
            with nc.allow_non_contiguous_dma("256 biases onto partitions"):
                sp.dma_start(bq[:, :], a["L0_xattn_bq"].rearrange("(g p) -> p g", p=P)).then_inc(wq_in, 16)
            for n, name in enumerate(("L0_xattn_bo", "L0_attn_bo")):
                sp.dma_start(bo[:, n, :], a[name].rearrange("(o n) -> o n", o=1).to_broadcast([P, D])).then_inc(bo_in, 16)
            sp.wait_ge(ones_set, 1)
            for n in range(1, 4):
                sp.dma_start(kst[96:99, n, :], kst[96:99, 0, :]).then_inc(ones_set, 16)

            def write_k(par, c):
                wait_alone(sp, k_3, c + 1)
                for g in range(2):
                    sp.dma_start(kscr[g * P:(g + 1) * P, :, bass.ds(c * CH, CH)],
                                 kparts[:, par, g, :, :]).then_inc(kscr_w[par], 16)

            def load_stacks(b, h, slot):
                done = stacks_in[slot]
                rows, cols = bass.ds(h * DH, DH), bass.ds(b * S, S)
                sp.dma_start(kst[0:48, slot, :], kscr[rows, :, cols].rearrange("d r t -> (d r) t")).then_inc(done, 16)
                for n, r in enumerate((0, 1, 0)):
                    sp.dma_start(kst[48 + 16 * n:64 + 16 * n, slot, :],
                                 kscr[rows, r:r + 1, cols].rearrange("d r t -> (d r) t")).then_inc(done, 16)
                cols = bass.ds(b * T, T)
                sp.dma_start(qst[0:48, slot, :], qscr1[rows, :, cols].rearrange("d r t -> (d r) t")).then_inc(done, 16)
                for n, scr in enumerate((qscr2, qscr2, qscr3)):
                    sp.dma_start(qst[48 + 16 * n:64 + 16 * n, slot, :], scr[rows, cols]).then_inc(done, 16)

            def early_job(c, slot):
                wait_alone(sp, v_ps, c + 1)
                load_ctx(slot, c + 4)
                write_k(slot % 2, c)

            for c in range(4):
                early_job(c, c)
            sp.wait_ge(q_1, 1)
            for g in range(2):
                for r in range(3):
                    sp.dma_start(qscr1[g * P:(g + 1) * P, r, :], q1[:, g, :]).then_inc(qscr_w, 16)
            sp.wait_ge(q_2, 1)
            for g in range(2):
                sp.dma_start(qscr2[g * P:(g + 1) * P, :], q2[:, g, :]).then_inc(qscr_w, 16)
            sp.wait_ge(q_3, 1)
            for g in range(2):
                sp.dma_start(qscr3[g * P:(g + 1) * P, :], q3[:, g, :]).then_inc(qscr_w, 16)
            with sp.Fori(1, 4, 1) as n:
                for c in range(4):
                    early_job(4 * n + c, c)
            sp.wait_ge(qscr_w, 160)
            for n in range(2):
                sp.wait_ge(kscr_w[n], 32 * 8)
            load_stacks(0, 0, 0)
            sp.wait_ge(v_ps, 17)
            load_ctx(0, KLEAD)
            write_k(0, 16)
            sp.wait_ge(k_ps, 18)
            load_ctx(1, KLEAD + 1)
            write_k(1, 17)
            load_stacks(0, 1, 1)
            sp.wait_ge(k_ps, 19)
            load_ctx(2, VLEAD + 1)
            write_k(0, 18)
            sp.wait_ge(k_ps, 20)
            load_ctx(3, VLEAD)
            write_k(1, 19)
            load_stacks(0, 2, 2)

            def head(it, u, k_job, v_job, k_load, v_load, ahead):
                i = it * 4 + u
                if ahead:
                    j = i + 3
                    wait_alone(sp, st_ps, ST * i)
                    wait_alone(sp, kscr_w[0], 32 * (it * 2 + 10 + u // 2) if k_job else 16 * NCH)
                    wait_alone(sp, kscr_w[1], 32 * (it * 2 + 9 + u % 2 + u // 2) if k_job else 16 * NCH)
                    load_stacks(j // H, j % H, (u + 3) % 4)
                if k_job:
                    wait_alone(sp, k_ps, i + KLEAD + 1)
                    if k_load:
                        load_ctx(u % 2, i + KLEAD + 2)
                    write_k(u % 2, i + KLEAD)
                if v_load:
                    wait_alone(sp, v_ps, i + VLEAD + 1)
                    load_ctx(2 + (u + 1) % 2, i + VLEAD + 2)

            for u in range(4):
                head(0, u, True, True, True, True, True)
            for name, row in bias.items():
                sp.dma_start(row, a[name].rearrange("(o n) -> o n", o=1)).then_inc(rows_in, 16)
            for n in range(2):
                sp.dma_start(slots[n * SL:(n + 1) * SL, :], a["L0_ffn_slot_init"]).then_inc(small_in, 16)
                sp.dma_start(slotT[:, :, n * SL:(n + 1) * SL],
                             a["ffn_slotT"].rearrange("(c p) s -> p c s", p=P)).then_inc(small_in, 16)
            sp.dma_start(tau[:, 0:1], a["L0_ffn_tau"].rearrange("(o n) -> o n", o=1).to_broadcast([P, 1])).then_inc(small_in, 16)
            with nc.allow_non_contiguous_dma("short vectors onto partitions"):
                for n, name in enumerate(("L0_attn_kln_g", "L0_attn_kln_b", "L0_attn_qln_g", "L0_attn_qln_b")):
                    sp.dma_start(gb16[:, n:n + 1], a[name].rearrange("(p o) -> p o", o=1)).then_inc(small_in, 16)
                for n, name in enumerate(("L0_ffn_ln_g", "L0_ffn_ln_b", "L0_ffn_bvp")):
                    sp.dma_start(colv[:, n, :], a[name].rearrange("(c p) -> p c", p=P)).then_inc(small_in, 16)
            with sp.Fori(1, 10, 1) as it:
                for u in range(4):
                    head(it, u, True, True, True, True, True)
            for u in range(4):
                head(10, u, True, True, u < 2, True, True)
            for u in range(4):
                head(11, u, False, u < 3, False, u < 1, True)
            for u in range(4):
                head(12, u, False, False, False, False, True)
            sp.wait_ge(vh_ready, 3 * H + 1)
            for name, dst in wt.items():
                sp.dma_start(dst, a[name].rearrange("(c p) n -> p c n", p=P)).then_inc(late_in, 16)
            with sp.Fori(13, 15, 1) as it:
                for u in range(4):
                    head(it, u, False, False, False, False, True)
            head(15, 0, False, False, False, False, True)
            for n in range(4):
                sp.wait_ge(x_new, 8 + n + 1)
                sp.dma_start(out[n].rearrange("(q p) d -> p q d", p=P), x_sb[:, 2 * n:2 * n + 2, :]).then_inc(stored, 16)
            sp.wait_ge(stored, 16 * 4)

        @block.gpsimd
        def _(pool):
            pool.memset(ident[:, :], 0.0).then_inc(consts, 1)
            pool.memset(identb[:, :], 0.0).then_inc(consts, 1)
            pool.memset(gsum[:, :], 0.0).then_inc(consts, 1)
            pool.memset(negclip[:, :], -CLIP).then_inc(consts, 1)
            pool.memset(epsc[:, :], EPS).then_inc(consts, 1)
            pool.wait_ge(consts, 5)
            for m in (ident, identb):
                pool.affine_select(out=m[:, :], in_=m[:, :], compare_op=ALU.not_equal, fill=1.0, base=0,
                                   pattern=[[-1, P]], channel_multiplier=1).then_inc(consts, 1)
            for g in range(4):
                pool.wait_ge(consts, 7 + g)
                pool.affine_select(out=gsum[:, :], in_=gsum[:, :], compare_op=ALU.not_equal, fill=1.0,
                                   base=-32 * g, pattern=[[-1, DH + 1]], channel_multiplier=1).then_inc(consts, 1)
            pool.memset(ones[:, :], 1.0).then_inc(rest_set, 1)
            pool.memset(onescol[:, :], 1.0).then_inc(rest_set, 1)
            pool.memset(spread[:, :, :], 0.0).then_inc(rest_set, 1)
            pool.memset(causal[:, :], 0.0).then_inc(rest_set, 1)
            pool.memset(halfones[:, :, :], 0.0).then_inc(rest_set, 1)
            pool.wait_ge(rest_set, 5)
            for e in range(2):
                pool.memset(halfones[:, e, e * DH:(e + 1) * DH], 1.0).then_inc(rest_set, 1)
            for n, (rep, width, base) in enumerate(((8, DH, 0), (4, 2 * DH, 0), (4, 2 * DH, DH))):
                pool.affine_select(out=spread[:, n, :].rearrange("d (r c) -> d r c", r=rep),
                                   in_=spread[:, n, :].rearrange("d (r c) -> d r c", r=rep),
                                   compare_op=ALU.not_equal, fill=1.0, base=base, pattern=[[0, rep], [-1, width]],
                                   channel_multiplier=1).then_inc(rest_set, 1)
            pool.affine_select(out=causal[:, :], in_=causal[:, :], compare_op=ALU.is_ge, fill=-1e30,
                               base=0, pattern=[[-1, P]], channel_multiplier=1).then_inc(rest_set, 1)

            pool.memset(vh[:, :, :, :], 0.0).then_inc(rest_set, 1)
            pool.wait_ge(rest_set, 12)
            pool.memset(vh[:, :, :, DH:DH + 1], 1.0).then_inc(rest_set, 1)

            def k_second(c, par):
                wait_alone(pool, k_r, c + 1)
                pool.tensor_copy(kparts[:, par, :, 1, :], kres[:, par, :, :]).then_inc(k_2, 1)

            def k_third(c, par):
                wait_alone(pool, k_2, c + 1)
                pool.tensor_tensor(kparts[:, par, :, 2, :], kres[:, par, :, :], kparts[:, par, :, 1, :],
                                   ALU.subtract).then_inc(k_3, 1)

            def add_bias(k):
                pool.wait_ge(ln_xn, NT * (k + 1))
                for n in range(4):
                    xs = x_sb[:, 2 * n:2 * n + 2, :]
                    pool.tensor_tensor(xs, xs, bo[:, k, :].unsqueeze(1).to_broadcast([P, 2, D]),
                                       ALU.add).then_inc(x_bias, 1)

            def copy_vh(slot, half, h, i):
                pool.tensor_copy(vh[:, slot, :, 0:DH],
                                 v_sb[:, bass.ds(half * 32, 32), bass.ds(h * DH, DH)]).then_inc(vh_ready, 1)

            with pool.Fori(0, KLEAD // 2, 1) as n:
                k_third(2 * n, 0)
                k_third(2 * n + 1, 1)
            pool.wait_ge(bo_in, 32)
            add_bias(0)
            pool.wait_ge(v_out, VLEAD)
            pool.wait_ge(rest_set, 13)
            copy_vh(0, 0, 0, 0)

            def head(it, u, k_job, v_job, ahead):
                i = it * 4 + u
                wait_alone(pool, flag_set, i + 1)
                clipping = pool.value_load(flag[96:97, 0:1])
                with pool.If(clipping != 0):
                    with pool.Fori(0, ST // 8, 1) as half:
                        for s in range(8):
                            n = i * ST + half * 8 + s
                            p = prob[:, s, :].rearrange("p (n q) -> p n q", n=2)
                            bound = low[:, :].unsqueeze(1).to_broadcast([P, 2, T])
                            wait_alone(pool, exp_done, n + 1)
                            pool.tensor_scalar(p, p, 1.0, None, ALU.min).then_inc(clip_step, 1)
                            wait_alone(pool, low_set, i + 1)
                            wait_alone(pool, clip_step, 3 * n + 1)
                            pool.tensor_tensor(p, p, bound, ALU.subtract).then_inc(clip_step, 1)
                            wait_alone(pool, clip_step, 3 * n + 2)
                            pool.tensor_scalar(p, p, 0.0, None, ALU.max).then_inc(clip_step, 1)
                            wait_alone(pool, clip_step, 3 * n + 3)
                            pool.tensor_tensor(p, p, bound, ALU.add).then_inc(clip_done, 1)
                with pool.Else():
                    pool.sem_inc(clip_step, 3 * ST)
                    pool.sem_inc(clip_done, ST)
                if ahead:
                    wait_alone(pool, v_out, i + VLEAD if v_job else NCH)
                    wait_alone(pool, pv_done, 8 * i)
                    copy_vh((u + 1) % 2, ((i + 1) // H) % 2, (i + 1) % H, i + 1)
                if k_job:
                    k_second(i + KLEAD, u % 2)
                    k_third(i + KLEAD, u % 2)

            for u in range(4):
                head(0, u, True, True, True)
            with pool.Fori(1, 11, 1) as it:
                for u in range(4):
                    head(it, u, True, True, True)
            for u in range(4):
                head(11, u, False, True, True)
            with pool.Fori(12, 15, 1) as it:
                for u in range(4):
                    head(it, u, False, False, True)
            for u in range(4):
                head(15, u, False, False, u < 3)
            pool.wait_ge(vh_ready, NH)
            pool.memset(v2e, 0.0).then_inc(v2_zero, 1)
            pool.wait_ge(xnT_ps, 8)
            pool.memset(v2o, 0.0).then_inc(v2_zero, 1)
            add_bias(1)

        @block.scalar
        def _(act):
            def norm_sd(k):
                act.wait_ge(ln_ag, NT * (k + 1))
                act.activation(rstd[:, :, 0], mv[:, :, 1], ACT.Sqrt, bias=epsc[:, :]).then_inc(ln_sq, 1)

            def turned(k):
                for n in range(2):
                    act.wait_ge(xnT_ps, 4 * k + n + 1)
                    act.activation(xnT[:, 0, n * 512:(n + 1) * 512], st[n][:, :], ACT.Copy).then_inc(xnT_act, 1)

            def k_first(c, par, before):
                wait(act, k_ps, c + 1)
                wait(act, kscr_w[par], 32 * before)
                act.activation(kparts[:, par, :, 0, :], kps[:, :].rearrange("p (g t) -> p g t", g=2),
                               ACT.Copy).then_inc(k_1, 1)

            def v_copy(bank, c):
                wait(act, v_ps, c + 1)
                act.activation(v_sb[:, bass.ds((c * 2) % 64, 2), :].rearrange("p n d -> p (n d)"),
                               bank[:, :], ACT.Copy).then_inc(v_out, 1)

            k_first(0, 0, 0)
            v_copy(mxb[1], 0)
            act.wait_ge(consts, 11)
            norm_sd(0)
            k_first(1, 1, 0)
            v_copy(mxb[1], 1)
            turned(0)
            act.wait_ge(q_full, 4)
            act.activation(q1, q_sb, ACT.Copy).then_inc(q_1, 1)
            for c in range(2, 4):
                k_first(c, c % 2, c // 2)
                v_copy(mxb[1], c)
            with act.Fori(1, 4, 1) as n:
                for u in range(4):
                    k_first(n * 4 + u, u % 2, n * 2 + u // 2)
                    v_copy(mxb[1], n * 4 + u)
            k_first(16, 0, 8)
            act.wait_ge(qscr_w, 160)
            v_copy(mxb[1], 16)
            for c in range(17, KLEAD):
                k_first(c, c % 2, c // 2)

            def head(it, u, k_job, v_job):
                i = it * 4 + u
                for s in range(ST):
                    wait(act, st_ps, i * ST + s + 1)
                    if s % 2 == 0:
                        wait(act, pv_done, i * 8 + s // 2 - 3)
                    act.activation(prob[:, s % 8, :], st[bank_of[s]][:, :], ACT.Exp).then_inc(exp_done, 1)
                    if s == 1:
                        wait(act, low_ps, i + 1)
                        wait(act, clip_done, ST * i)
                        act.activation(low[:, :], misc[:, 0:T], ACT.Exp, bias=negclip[:, :]).then_inc(low_set, 1)
                    if s == 5 and k_job:
                        k_first(i + KLEAD, u % 2, it * 2 + u // 2 + KLEAD // 2)
                    if s == 13 and v_job:
                        wait(act, vh_ready, i + 1)
                        v_copy(kps, i + VLEAD)

            for u in range(4):
                head(0, u, True, True)
            with act.Fori(1, 11, 1) as it:
                for u in range(4):
                    head(it, u, True, True)
            for u in range(4):
                head(11, u, False, u < 3)
            with act.Fori(12, 16, 1) as it:
                for u in range(4):
                    head(it, u, False, False)

            act.wait_ge(head_out, NH)
            turned(1)
            norm_sd(1)
            turned(2)
            for t in range(NT):
                act.wait_ge(kq_c, t + 1)
                if t >= 4:
                    act.wait_ge(kq_var, t - 3)
                act.activation(sq[:, t % 4, :, :], kqc[:, t, :, :], ACT.Square).then_inc(kq_sq, 1)
                if t % 2:
                    n = t // 2
                    act.wait_ge(v2_ps, n + 1)
                    act.wait_ge(v2_zero, 2)
                    for e, v2 in enumerate((v2e, v2o)):
                        act.activation(
                            v2[:, 2 * n:2 * n + 2, :].rearrange("p t (h e d) -> p t h e d", e=2, d=DH)[:, :, :, e, :],
                            (mxb[1], acc, misc, kps)[n][:, :].rearrange(
                                "p (t h e d) -> p t h e d", t=2, e=2, d=DH)[:, :, :, e, :],
                            ACT.Copy).then_inc(v2_out, 1)
                if t in (4, 7):
                    half = slice(4 * (t // 7), 4 * (t // 7) + 4)
                    act.wait_ge(kq_var, half.stop)
                    act.activation(hsd[:, half, :], hvar[:, half, :], ACT.Sqrt, bias=epsc[:, :],
                                   scale=1.0 / DH).then_inc(kq_sd, 1)
            act.wait_ge(gb_out, 1)
            for m in range(4):
                act.wait_ge(kqT_ps, 2 * m + 2)
                for e in range(2):
                    act.activation((qeT, qoT)[e][:, :, m * T:(m + 1) * T],
                                   (st[2], mxb[0])[m % 2][:, :].rearrange("p (g t) -> p g t", g=2), ACT.Identity,
                                   bias=gbp[:, 1 + e, 1:2], scale=gbp[:, 1 + e, 0:1]).then_inc(qT_out, 1)
            for n in range(64):
                u, j = n // 4, n % 4
                b, qt, g = u // 4, (u // 2) % 2, u % 2
                w = P * (qt + 1)
                act.wait_ge(a_max, n + 1)
                if n >= 8:
                    act.wait_ge(pT_ps, n - 7)
                for e in range(2):
                    h = 8 * g + 2 * j + e
                    act.activation(prob[:, n % 8, e * w:(e + 1) * w], (mxb[1], acc, misc, kps)[j][:, e * w:(e + 1) * w],
                                   ACT.Exp, bias=amax[:, 2 * b + qt, h:h + 1]).then_inc(a_exp, 1)
            norm_sd(2)
            turned(3)

            act.wait_ge(cv_out, 1)
            for n in range(2):
                act.wait_ge(h_ps, n + 1)
                act.activation(hT[:, n * 512:(n + 1) * 512], (mxb[1], acc)[n][:, :], ACT.Gelu,
                               bias=cvec[:, :]).then_inc(h_out, 1)
            act.wait_ge(l_sub, 1)
            act.activation(lexp, lsub, ACT.Exp).then_inc(l_exp, 1)
            for r in range(2):
                act.wait_ge(g_ps, r + 1)
                act.activation(rz[:, r, :], (mxb[0], misc)[r][:, :], ACT.Sigmoid).then_inc(g_rz, 1)
            for r in range(2):
                act.wait_ge(g_sum, r + 1)
                act.activation(cand[:, r, :], snew[:, r, :], ACT.Tanh).then_inc(g_n, 1)
            for n in range(2):
                act.wait_ge(alT_ps, n + 1)
                act.activation(alphaT[:, 4 * n:4 * n + 4, :].rearrange("p t q -> p (t q)"),
                               (acc, st[0])[n][0:SL, :], ACT.Copy).then_inc(alT_out, 1)
            for n in range(2):
                act.wait_ge(v4_ps, n + 1)
                act.activation(v4[:, 2 * n:2 * n + 2, :].rearrange("p b d -> p (b d)"),
                               (mxb[1], acc)[n][0:SL, :], ACT.Copy).then_inc(v4_out, 1)
            act.wait_ge(c_sub, 1)
            act.activation(att, att, ACT.Exp).then_inc(c_exp, 1)
            act.wait_ge(y_ag, 2)
            act.activation(rstd[:, 0:2, 0], mv[:, 0:2, 1], ACT.Sqrt, bias=epsc[:, :]).then_inc(y_sd, 1)
            for n in range(2):
                act.wait_ge(svo_ps, n + 1)
                act.activation(svo[:, 2 * n:2 * n + 2, :].rearrange("p b d -> p (b d)"),
                               (mxb[1], acc)[n][0:SL, :], ACT.Copy).then_inc(svo_out, 1)

        @block.vector
        def _(dve):
            dve.memset(ctx4[C2:C2 + 1, :, 1, :], 1.0).then_inc(rows_set, 1)
            dve.memset(shrow[:, :], 0.0).then_inc(rows_set, 1)
            dve.wait_ge(rows_set, 2)
            dve.memset(shrow[96:99, :], 1.0).then_inc(rows_set, 1)
            dve.memset(kst[96:99, 0, :], 1.0).then_inc(ones_set, 1)

            def k_rest(c, par):
                wait(dve, k_1, c + 1)
                wait(dve, k_3, c - 1)
                dve.tensor_tensor(kres[:, par, :, :], kps[:, :].rearrange("p (g t) -> p g t", g=2),
                                  kparts[:, par, :, 0, :], ALU.subtract).then_inc(k_r, 1)

            def norm(k):
                for j in range(NT):
                    if k > 0 and j % 2 == 0:
                        dve.wait_ge(x_new, 4 * (k - 1) + j // 2 + 1)
                    dve.bn_stats(stats[:, j, :], x_sb[:, j, :]).then_inc(ln_st, 1)
                for j in range(NT):
                    dve.wait_ge(ln_st, NT * k + j + 1)
                    dve.bn_aggr(mv[:, j, :], stats[:, j, :]).then_inc(ln_ag, 1)
                dve.wait_ge(ln_sq, k + 1)
                dve.reciprocal(rstd[:, :, 1], rstd[:, :, 0]).then_inc(ln_rc, 1)
                dve.wait_ge(ln_rc, k + 1)
                for j in range(NT):
                    dve.tensor_scalar(xn[:, j, :], x_sb[:, j, :], mv[:, j, 0:1], rstd[:, j, 1:2],
                                      ALU.subtract, ALU.mult).then_inc(ln_xn, 1)

            def turned(k):
                for n in range(2):
                    dve.wait_ge(xnT_ps, 4 * k + n + 3)
                    dve.tensor_copy(xnT[:, 1, n * 512:(n + 1) * 512], (st[2], mxb[0])[n][:, :]).then_inc(xnT_dve, 1)

            def early_rest(c, par):
                k_rest(c, par)
                wait(dve, k_r, c + 1)
                dve.tensor_copy(kparts[:, par, :, 1, :], kres[:, par, :, :]).then_inc(k_2, 1)

            dve.wait_ge(x_in, 16)
            early_rest(0, 0)
            norm(0)
            early_rest(1, 1)
            turned(0)
            dve.wait_ge(wq_in, 32)
            for n in range(4):
                g, half = n // 2, n % 2
                dve.wait_ge(q_ps, n + 1)
                dve.tensor_scalar(q_sb[:, g, half * 512:(half + 1) * 512], (st[0], st[1], st[2], mxb[0])[n][:, :],
                                  bq[:, g:g + 1], DH ** -0.5, ALU.add, ALU.mult).then_inc(q_full, 1)
            dve.wait_ge(q_1, 1)
            dve.wait_ge(q_full, 4)
            dve.tensor_tensor(qres, q_sb, q1, ALU.subtract).then_inc(q_r1, 1)
            early_rest(2, 0)
            dve.wait_ge(q_r1, 1)
            dve.tensor_copy(q2, qres).then_inc(q_2, 1)
            early_rest(3, 1)
            dve.wait_ge(q_2, 1)
            dve.tensor_tensor(q3, qres, q2, ALU.subtract).then_inc(q_3, 1)

            with dve.Fori(2, KLEAD // 2 - 1, 1) as n:
                early_rest(2 * n, 0)
                early_rest(2 * n + 1, 1)

            def reduce_step(j, par, s):
                if s == 0:
                    wait(dve, m_row, j - 1)
                wait(dve, max_ps, j * ST + s + 1)
                dve.reduce_max(mxp[:, par, s // 8, s % 8:s % 8 + 1], mxb[s % 2][:, :], AX.X).then_inc(max_red, 1)

            def shift_step(j, slot, n):
                if n == 0:
                    wait(dve, max_red, (j + 1) * ST)
                    dve.reduce_max(rowmax[:, :], mxp[:, slot % 2, :, :], AX.X).then_inc(m_row, 1)
                elif n == 1:
                    wait(dve, m_row, j + 1)
                    dve.tensor_scalar(shift[:, :], rowmax[:, :], CLIP, -CLIP, ALU.min, ALU.max).then_inc(m_clip, 1)
                elif n == 2:
                    wait(dve, m_clip, j + 1)
                    wait(dve, shift_ps, j)
                    dve.tensor_scalar(sparts[:, :, 0], shift[:, :], -1.0, None, ALU.mult).then_inc(m_1, 1)
                elif n == 3:
                    wait(dve, m_1, j + 1)
                    dve.scalar_tensor_tensor(sres[:, :], shift[:, :], -1.0, sparts[:, :, 0],
                                             ALU.mult, ALU.subtract).then_inc(m_res, 1)
                elif n == 4:
                    wait(dve, m_res, j + 1)
                    dve.tensor_copy(sparts[:, :, 1], sres[:, :]).then_inc(m_2, 1)
                elif n == 5:
                    wait(dve, m_2, j + 1)
                    dve.tensor_tensor(sparts[:, :, 2], sres[:, :], sparts[:, :, 1], ALU.subtract).then_inc(m_3, 1)
                elif n == 6:
                    wait(dve, shift_ps, j + 1)
                    dve.tensor_copy(qst[96:99, slot, :], misc[96:99, 0:T]).then_inc(shift_set, 1)
                elif n == 7:
                    wait(dve, flag_set, j)
                    dve.tensor_reduce(flagf[96:97, :], misc[96:97, 0:T], AX.X, ALU.max,
                                      apply_absolute_value=True).then_inc(flag_abs, 1)

            def max_step(it, u, s, near, far):
                i = it * 4 + u
                if s < 8 and near:
                    reduce_step(i + 1, (u + 1) % 2, s + 8)
                elif s >= 8 and far:
                    reduce_step(i + 2, u % 2, s - 8)
                if s >= 8 and near:
                    shift_step(i + 1, (u + 1) % 4, s - 8)

            for s in range(8):
                reduce_step(0, 0, s)
            early_rest(18, 0)
            for s in range(ST):
                max_step(-1, 3, s, True, True)
                if s == 3:
                    early_rest(19, 1)

            def take_sums(i):
                wait(dve, fin_ps, i + 1)
                dve.reciprocal(rcp[:, :], done[:, :, DH]).then_inc(fin_rcp, 1)

            def normalise(i):
                wait(dve, fin_rcp, i + 1)
                dve.tensor_tensor(o_sb[:, bass.ds(i // H, 1), :, bass.ds(i % H * DH, DH)]
                                  .rearrange("p o q d -> p (o q) d"), done[:, :, 0:DH],
                                  rcp[:, :].unsqueeze(2).to_broadcast([P, QT, DH]), ALU.mult).then_inc(head_out, 1)

            done = misc[:, 0:64].rearrange("p (q d) -> p q d", q=2)

            def save_acc(i):
                wait(dve, pv_done, 8 * (i + 1))
                wait(dve, fin_ps, i)
                dve.tensor_copy(accs[:, :], acc[:, 0:T]).then_inc(acc_out, 1)

            def head(it, u, k_job, near, far):
                i = it * 4 + u
                first = isinstance(it, int) and i == 0
                wait(dve, flag_abs, i + 1)
                wait(dve, clip_done, ST * i)
                dve.tensor_scalar(flag[96:97, :], flagf[96:97, :], NEAR, None, ALU.is_gt).then_inc(flag_set, 1)
                for s in range(ST):
                    max_step(it, u, s, near, far)
                    if s == 2 and not first:
                        save_acc(i - 1)
                    if s == 6 and k_job:
                        k_rest(i + KLEAD, u % 2)
                    if s == 9 and not first:
                        take_sums(i - 1)
                    if s == 11 and not first:
                        normalise(i - 1)

            for u in range(4):
                head(0, u, True, True, True)
            with dve.Fori(1, 11, 1) as it:
                for u in range(4):
                    head(it, u, True, True, True)
            with dve.Fori(11, 15, 1) as it:
                for u in range(4):
                    head(it, u, False, True, True)
            for u in range(4):
                head(15, u, False, u < 3, u < 2)
            save_acc(NH - 1)
            take_sums(NH - 1)
            normalise(NH - 1)

            def add_out(k, banks):
                for n in range(4):
                    dve.wait_ge(out_ps, 4 * k + n + 1)
                    if k < 2:
                        dve.wait_ge(x_bias, 4 * k + n + 1)
                    xs = x_sb[:, 2 * n:2 * n + 2, :].rearrange("p t d -> p (t d)")
                    dve.tensor_tensor(xs, xs, banks[n][:, :], ALU.add).then_inc(x_new, 1)

            four = (mxb[1], acc, misc, kps)
            turned(1)
            add_out(0, four)
            norm(1)
            dve.wait_ge(gb_ps, 1)
            dve.tensor_scalar(gbp[:, :, :].rearrange("p n k -> p (n k)"), misc[:, 0:6], D ** -0.25, None,
                              ALU.mult).then_inc(gb_out, 1)
            turned(2)
            ring = (st[0], st[1], st[2], mxb[0])

            def kq_variance(t):
                dve.wait_ge(kq_sq, t + 1)
                dve.reduce_sum(hvar[:, t, :], sq[:, t % 4, :, :], AX.X).then_inc(kq_var, 1)

            def kq_recip(half):
                dve.wait_ge(kq_sd, half + 1)
                dve.reciprocal(hrs[:, 4 * half:4 * half + 4, :], hsd[:, 4 * half:4 * half + 4, :]).then_inc(kq_rs, 1)

            def kq_scale(t):
                dve.wait_ge(kq_rs, t // 4 + 1)
                dve.tensor_tensor(kqc[:, t, :, :], kqc[:, t, :, :],
                                  hrs[:, t, :].unsqueeze(2).to_broadcast([P, 2 * H, DH]), ALU.mult).then_inc(kq_n, 1)

            for t in range(NT):
                kq = ring[t % 4][:, :].rearrange("p (h d) -> p h d", d=DH)
                dve.wait_ge(kq_ps, t + 1)
                dve.reduce_sum(hsum[:, t, :], kq, AX.X).then_inc(kq_sum, 1)
                dve.wait_ge(kq_sum, t + 1)
                dve.scalar_tensor_tensor(kqc[:, t, :, :], hsum[:, t, :].unsqueeze(2).to_broadcast([P, 2 * H, DH]),
                                         -1.0 / DH, kq, ALU.mult, ALU.add).then_inc(kq_c, 1)
                if t >= 1:
                    kq_variance(t - 1)
                if t == 5:
                    kq_recip(0)
                if t >= 6:
                    kq_scale(2 * (t - 6))
                    kq_scale(2 * (t - 6) + 1)
            kq_variance(NT - 1)
            kq_recip(1)
            for t in range(4, NT):
                kq_scale(t)
            dve.wait_ge(gb_out, 1)
            for m in range(4):
                dve.wait_ge(kqT_ps, 2 * m + 1)
                dve.tensor_scalar(kT[:, :, m * T:(m + 1) * T], ring[m % 2][:, :].rearrange("p (g t) -> p g t", g=2),
                                  gbp[:, 0, 0:1], gbp[:, 0, 1:2], ALU.mult, ALU.add).then_inc(kT_out, 1)

            def a_maxima(n):
                u, j = n // 4, n % 4
                b, qt, g = u // 4, (u // 2) % 2, u % 2
                w = P * (qt + 1)
                h = 8 * g + 2 * j
                dve.wait_ge(a_ps, n + 1)
                dve.tensor_reduce(amax[:, 2 * b + qt, h:h + 2], four[j][:, 0:2 * w].rearrange("p (e k) -> p e k", e=2),
                                  AX.X, ALU.max, negate=True).then_inc(a_max, 1)

            def a_turned(n):
                qt = (n // 8) % 2
                w = 2 * P * (qt + 1)
                dve.wait_ge(pT_ps, n + 1)
                if n >= 8:
                    dve.wait_ge(o2_ps, n // 4 - 1)
                dve.tensor_copy(probT[(n // 4) % 2][:, n % 4, 0:w], st[n % 2][:, 0:w]).then_inc(pT_out, 1)

            def a_norm(u):
                bank = (st[2], mxb[0])[u % 2]
                dve.wait_ge(o2_ps, u + 1)
                if u >= 2:
                    dve.wait_ge(o2_out, u - 1)
                dve.reciprocal(arcp[:, u % 2, :], bank[:, P:2 * P]).then_inc(o2_rc, 1)
                dve.wait_ge(o2_rc, u + 1)
                dve.tensor_tensor(xnT[:, u % 2, (u // 2) * P:(u // 2 + 1) * P], bank[:, 0:P], arcp[:, u % 2, :],
                                  ALU.mult).then_inc(o2_out, 1)

            for n in range(4):
                a_maxima(n)
            for n in range(64):
                a_turned(n)
                if n + 4 < 64:
                    a_maxima(n + 4)
                if n % 4 == 3 and n > 4:
                    a_norm(n // 4 - 1)
            a_norm(15)
            add_out(1, four)
            norm(2)

            dve.reduce_sum(smean[:, 0, :], slotT[:, :, 0:SL], AX.X).then_inc(sm_out, 1)
            dve.wait_ge(sm_out, 1)
            dve.tensor_scalar(smean[:, 1, :], smean[:, 0, :], 1.0 / SL, None, ALU.mult).then_inc(sm_out, 1)
            dve.scalar_tensor_tensor(tau[:, 1:2], tau[:, 0:1], -1.0, tau[:, 0:1], ALU.mult, ALU.max).then_inc(tau_a, 1)
            dve.wait_ge(tau_a, 1)
            dve.tensor_scalar(tau[:, 2:3], tau[:, 1:2], 0.1, None, ALU.add).then_inc(tau_a, 1)
            dve.wait_ge(tau_a, 2)
            dve.reciprocal(tau[:, 3:4], tau[:, 2:3]).then_inc(tau_out, 1)
            dve.wait_ge(cv_ps, 1)
            dve.tensor_copy(cvec[:, :], kps[:, 0:1]).then_inc(cv_out, 1)
            turned(3)
            dve.wait_ge(lg_ps, 1)
            dve.wait_ge(tau_out, 1)
            dve.tensor_scalar(lg, misc[:, :].rearrange("p (t s) -> p t s", t=NT), tau[:, 3:4], None,
                              ALU.mult).then_inc(lg_out, 1)
            dve.wait_ge(lg_out, 1)
            for t in range(NT):
                dve.max(top8[:, t, :], lg[:, t, :]).then_inc(l_top, 1)
            for t in range(NT):
                dve.wait_ge(l_top, t + 1)
                dve.match_replace(lrep[:, t, :], top8[:, t, :], lg[:, t, :], -3e38).then_inc(l_rep, 1)
            dve.tensor_tensor(lsub, lg, top8[:, :, 0:1].to_broadcast([P, NT, SL]), ALU.subtract).then_inc(l_sub, 1)
            dve.wait_ge(l_rep, NT)
            dve.tensor_tensor(lmask, lg, lrep, ALU.not_equal).then_inc(l_mask, 1)
            dve.wait_ge(l_mask, 1)
            dve.wait_ge(l_exp, 1)
            dve.tensor_tensor(lexp, lexp, lmask, ALU.mult).then_inc(l_al, 1)
            dve.wait_ge(l_al, 1)
            dve.reduce_sum(lsum[:, :, 0], lexp, AX.X).then_inc(l_sum, 1)
            dve.wait_ge(l_sum, 1)
            dve.reciprocal(lsum[:, :, 1], lsum[:, :, 0]).then_inc(l_sum, 1)
            dve.wait_ge(l_sum, 2)
            dve.tensor_tensor(alpha, lexp, lsum[:, :, 1:2].to_broadcast([P, NT, SL]), ALU.mult).then_inc(l_out, 1)
            for r in range(2):
                dve.wait_ge(si_ps, r + 1)
                dve.tensor_scalar(den[:, r, 0:1], st[r][:, D:D + 1], 1e-8, None, ALU.add).then_inc(si_den, 1)
                dve.wait_ge(si_den, r + 1)
                dve.reciprocal(den[:, r, 1:2], den[:, r, 0:1]).then_inc(si_rc, 1)
                dve.wait_ge(si_rc, r + 1)
                dve.tensor_scalar(si[:, r, :], st[r][:, 0:D], den[:, r, 1:2], None, ALU.mult).then_inc(si_out, 1)
            dve.wait_ge(siT_ps, 1)
            dve.tensor_copy(siT.rearrange("p c s -> p (c s)"), st[2][:, :]).then_inc(siT_out, 1)
            for r in range(2):
                nb = (kps, mxb[1])[r]
                dve.wait_ge(g_rz, r + 1)
                dve.tensor_tensor(cand[:, r, :], rz[:, r, 0:D], nb[:, D:2 * D], ALU.mult).then_inc(g_rh, 1)
                dve.wait_ge(g_rh, r + 1)
                dve.tensor_tensor(snew[:, r, :], cand[:, r, :], nb[:, 0:D], ALU.add).then_inc(g_sum, 1)
            for r in range(2):
                dve.wait_ge(g_n, r + 1)
                dve.tensor_tensor(y[:, r, :], slots[:, :], cand[:, r, :], ALU.subtract).then_inc(g_d, 1)
                dve.wait_ge(g_d, r + 1)
                dve.tensor_tensor(y[:, r, :], y[:, r, :], rz[:, r, D:2 * D], ALU.mult).then_inc(g_zd, 1)
                dve.wait_ge(g_zd, r + 1)
                dve.tensor_tensor(snew[:, r, :], cand[:, r, :], y[:, r, :], ALU.add).then_inc(g_new, 1)
            dve.wait_ge(snT_ps, 1)
            dve.tensor_copy(snT.rearrange("p c s -> p (c s)"), st[1][:, :]).then_inc(snT_out, 1)
            dve.wait_ge(qk_ps, 1)
            dve.tensor_scalar(qkT[:, 0, :], st[2][0:SL, 0:T], QS ** -0.5, None, ALU.mult).then_inc(qk_out, 1)
            dve.tensor_copy(qkT[:, 1, :], st[2][0:SL, T:2 * T]).then_inc(qk_out, 1)
            dve.wait_ge(c_ps, 1)
            sc = mxb[0][:, 0:2 * SL].rearrange("p (r s) -> p r s", r=2)
            dve.reduce_max(smx[:, :, 0], sc, AX.X).then_inc(c_max, 1)
            dve.wait_ge(c_max, 1)
            dve.tensor_tensor(att, sc, smx[:, :, 0:1].to_broadcast([P, 2, SL]), ALU.subtract).then_inc(c_sub, 1)
            dve.wait_ge(c_exp, 1)
            dve.reduce_sum(smx[:, :, 1], att, AX.X).then_inc(c_sum, 1)
            dve.wait_ge(c_sum, 1)
            dve.reciprocal(smx[:, :, 2], smx[:, :, 1]).then_inc(c_sum, 1)
            dve.wait_ge(c_sum, 2)
            dve.tensor_tensor(att, att, smx[:, :, 2:3].to_broadcast([P, 2, SL]), ALU.mult).then_inc(c_out, 1)
            dve.wait_ge(cT_ps, 1)
            dve.tensor_copy(attT.rearrange("p r s -> p (r s)"), misc[0:SL, 0:2 * P]).then_inc(cT_out, 1)
            dve.wait_ge(cm_ps, 1)
            dve.wait_ge(g_new, 2)
            dve.tensor_tensor(y, snew, kps[:, :].rearrange("p (r d) -> p r d", r=2), ALU.add).then_inc(y_out, 1)
            dve.wait_ge(y_out, 1)
            for r in range(2):
                dve.bn_stats(stats[:, r, :], y[:, r, :]).then_inc(y_st, 1)
                dve.wait_ge(y_st, r + 1)
                dve.bn_aggr(mv[:, r, :], stats[:, r, :]).then_inc(y_ag, 1)
            dve.wait_ge(y_sd, 1)
            dve.reciprocal(rstd[:, 0:2, 1], rstd[:, 0:2, 0]).then_inc(y_rs, 1)
            dve.wait_ge(y_rs, 1)
            for r in range(2):
                dve.tensor_scalar(y[:, r, :], y[:, r, :], mv[:, r, 0:1], rstd[:, r, 1:2],
                                  ALU.subtract, ALU.mult).then_inc(y_n, 1)
            dve.wait_ge(yT_ps, 1)
            for c in range(2):
                dve.tensor_scalar(yT[:, c, :], st[0][:, c * T:(c + 1) * T], colv[:, 0, c:c + 1], colv[:, 1, c:c + 1],
                                  ALU.mult, ALU.add).then_inc(yT_out, 1)
            dve.wait_ge(sv_ps, 1)
            for m in range(2):
                dve.tensor_scalar(svT[:, m, :], st[1][:, m * T:(m + 1) * T], colv[:, 2, m:m + 1], None,
                                  ALU.add).then_inc(sv_out, 1)
            add_out(2, (st[2], mxb[0], misc, kps))

        @block.tensor
        def _(pe):
            def turn(k, src, ready, per):
                for n in range(4):
                    c, half = n // 2, n % 2
                    bank = (st[0], st[1], st[2], mxb[0])[n]
                    for j in range(4):
                        t = half * 4 + j
                        if c == 0:
                            pe.wait_ge(ready, per(t))
                        tr = pe.matmul(bank[:, j * P:(j + 1) * P], src(t, c), ident[:, :], start=True, stop=True)
                    tr.then_inc(xnT_ps, 1)

            def normed(t, c):
                return xn[:, t, c * P:(c + 1) * P]

            def project_k(slot, g):
                for n in range(2):
                    rows = P if n == 0 else C2 + 1
                    mm = pe.matmul(kps[:, g * CH:(g + 1) * CH], wk[0:rows, n, g * P:(g + 1) * P],
                                   ctx4[0:rows, slot, n, :], start=(n == 0), stop=(n == 1))
                if g == 1:
                    mm.then_inc(k_ps, 1)

            def project_v(bank, slot, t):
                for n in range(2):
                    rows = P if n == 0 else C2 + 1
                    mm = pe.matmul(bank[:, t * D:(t + 1) * D], ctx4[0:rows, slot, n, t * P:(t + 1) * P],
                                   wv[0:rows, n, :], start=(n == 0), stop=(n == 1))
                if t == 1:
                    mm.then_inc(v_ps, 1)

            def max_step(j, slot, s):
                qt, n = s // 8, s % 8
                wait(pe, max_red, j * ST + s - 1)
                pe.matmul(mxb[s % 2][:, :], qst[0:96, slot, qt * P:(qt + 1) * P],
                          kst[0:96, slot, n * 512:(n + 1) * 512], start=True, stop=True).then_inc(max_ps, 1)

            def max_ahead(it, u, s, near, far):
                i = it * 4 + u
                if s < 8 and near:
                    max_step(i + 1, (u + 1) % 4, s + 8)
                elif s >= 8 and far:
                    if s == 8:
                        wait(pe, stacks_in[(u + 2) % 4], 128 * (it + (u + 2) // 4 + 1))
                    max_step(i + 2, (u + 2) % 4, s - 8)
                if s == 14 and near:
                    wait(pe, m_3, i + 2)
                    wait(pe, head_out, i)
                    wait(pe, low_set, i + 1)
                    for qt in range(QT):
                        mm = pe.matmul(misc[96:99, qt * P:(qt + 1) * P], sparts[:, qt, :], identb[:, :],
                                       start=True, stop=True)
                    mm.then_inc(shift_ps, 1)

            def early_job(c, round_, slot):
                wait(pe, ctx_in[slot], 32 * round_ + 32)
                wait(pe, k_r, c)
                for g in range(2):
                    project_k(slot, g)
                wait(pe, v_out, c)
                for t in range(2):
                    project_v(mxb[1], slot, t)

            pe.wait_ge(rows_set, 3)
            pe.wait_ge(w_in, 16 * 6)
            early_job(0, 0, 0)
            early_job(1, 0, 1)
            pe.wait_ge(consts, 11)
            turn(0, normed, ln_xn, lambda t: t + 1)
            pe.wait_ge(xnT_act, 2)
            pe.wait_ge(xnT_dve, 2)
            pe.wait_ge(wq_in, 32)
            for n in range(4):
                g, half = n // 2, n % 2
                for c in range(2):
                    mm = pe.matmul((st[0], st[1], st[2], mxb[0])[n][:, :], wq[:, c, g * P:(g + 1) * P],
                                   xnT[:, c, half * 512:(half + 1) * 512], start=(c == 0), stop=(c == 1))
                mm.then_inc(q_ps, 1)
            early_job(2, 0, 2)
            early_job(3, 0, 3)
            with pe.Fori(1, 4, 1) as n:
                for u in range(4):
                    early_job(4 * n + u, n, u)
            early_job(16, 4, 0)

            def late_k(c):
                pe.wait_ge(ctx_in[c % 4], 32 * 5)
                pe.wait_ge(k_r, c)
                for g in range(2):
                    project_k(c % 4, g)

            late_k(17)
            pe.wait_ge(q_full, 4)
            pe.wait_ge(stacks_in[0], 128)
            pe.wait_ge(v_out, VLEAD)
            for s in range(8):
                max_step(0, 0, s)
            late_k(18)
            for s in range(ST):
                max_ahead(-1, 3, s, True, True)
                if s == 3:
                    late_k(19)

            def pv_group(i, par, g):
                wait(pe, exp_done, i * ST + 2 * g + 2)
                wait(pe, clip_done, i * ST + 2 * g + 2)
                for r in range(4):
                    n = 4 * g + r
                    mm = pe.matmul(acc[32 * r:32 * r + 32, 0:T], vh[:, par, n, :],
                                   prob[:, (n // 2) % 8, (n % 2) * T:(n % 2 + 1) * T],
                                   start=(g == 0), stop=(g == 7), skip_group_check=True)
                mm.then_inc(pv_done, 1)

            def finish(i):
                wait(pe, acc_out, i + 1)
                for qt in range(QT):
                    mm = pe.matmul(misc[:, qt * 32:qt * 32 + DH + 1], accs[:, qt * P:(qt + 1) * P], gsum[:, :],
                                   start=True, stop=True)
                mm.then_inc(fin_ps, 1)

            def head(it, u, k_job, v_job, near, far):
                i = it * 4 + u
                first = isinstance(it, int) and i == 0
                for s in range(ST):
                    if s == 0:
                        wait(pe, shift_set, i + 1)
                        wait(pe, exp_done, i * ST - 3)
                    elif s == 1:
                        wait(pe, exp_done, i * ST)
                    elif s >= 3:
                        wait(pe, exp_done, i * ST + (s - 2 if s < 15 else 14))
                    for n in range(2):
                        mm = pe.matmul(st[bank_of[s]][:, n * T:(n + 1) * T],
                                       kst[0:99, u, (2 * s + n) * P:(2 * s + n + 1) * P], qst[0:99, u, :],
                                       start=True, stop=True)
                    mm.then_inc(st_ps, 1)
                    max_ahead(it, u, s, near, far)
                    if s == 0:
                        wait(pe, flag_abs, i + 1)
                        pe.matmul(misc[:, 0:T], shrow[0:99, :], qst[0:99, u, :],
                                  start=True, stop=True).then_inc(low_ps, 1)
                    if s == 1 and not first:
                        pv_group(i - 1, (u + 1) % 2, 7)
                    if s in (2, 4) and k_job:
                        if s == 2:
                            wait(pe, ctx_in[u % 2], 32 * (it * 2 + u // 2 + 6))
                            wait(pe, k_r, i + KLEAD)
                            wait(pe, v_out, i + VLEAD)
                        project_k(u % 2, (s - 2) // 2)
                    if s in (10, 12) and v_job:
                        if s == 10:
                            wait(pe, ctx_in[2 + (u + 1) % 2], 32 * (it * 2 + u // 2 + 6))
                            wait(pe, k_r, i + KLEAD + 1 if k_job else NCH)
                            wait(pe, v_out, i + VLEAD)
                        project_v(kps, 2 + (u + 1) % 2, (s - 10) // 2)
                    if s % 2 == 1 and s >= 3:
                        if s == 3:
                            wait(pe, vh_ready, i + 1)
                            wait(pe, acc_out, i)
                        pv_group(i, u % 2, (s - 3) // 2)
                    if s == 6 and not first:
                        wait(pe, low_set, i + 1)
                        finish(i - 1)

            pe.wait_ge(ones_set, 1 + 16 * 3)
            for u in range(4):
                head(0, u, True, True, True, True)
            with pe.Fori(1, 11, 1) as it:
                for u in range(4):
                    head(it, u, True, True, True, True)
            for u in range(4):
                head(11, u, False, u < 3, True, True)
            with pe.Fori(12, 15, 1) as it:
                for u in range(4):
                    head(it, u, False, False, True, True)
            for u in range(4):
                head(15, u, False, False, u < 3, u < 2)
            pv_group(NH - 1, 1, 7)
            finish(NH - 1)

            four = (mxb[1], acc, misc, kps)

            pe.wait_ge(late_in, 16 * len(wt))
            pe.wait_ge(rows_in, 16 * len(bias))
            pe.wait_ge(rest_set, 13)
            pe.wait_ge(small_in, 16 * 12)
            turn(1, lambda t, c: o_sb[:, t // 2, t % 2, c * P:(c + 1) * P], head_out, lambda t: NH)
            pe.wait_ge(xnT_act, 4)
            pe.wait_ge(xnT_dve, 4)
            for n in range(4):
                for j in range(2):
                    t = 2 * n + j
                    to = four[n][:, j * D:(j + 1) * D]
                    for c in range(2):
                        mm = pe.matmul(to, xnT[:, c, t * P:(t + 1) * P], wt["L0_xattn_Wo"][:, c, :],
                                       start=(c == 0), stop=(c == 1))
                mm.then_inc(out_ps, 1)

            pe.wait_ge(x_new, 4)
            pe.matmul(misc[:, 0:2], spread[:, 0, :], gb16[:, 0:2], start=True, stop=True)
            for n in range(1, 3):
                mm = pe.matmul(misc[:, 2 * n:2 * n + 2], spread[:, n, :], gb16[:, 2:4], start=True, stop=True)
            mm.then_inc(gb_ps, 1)
            turn(2, normed, ln_xn, lambda t: NT + t + 1)
            pe.wait_ge(xnT_act, 6)
            pe.wait_ge(xnT_dve, 6)
            ring = (st[0], st[1], st[2], mxb[0])
            pe.wait_ge(gb_out, 1)
            for t in range(NT):
                if t >= 4:
                    pe.wait_ge(kq_c, t - 3)
                for c in range(2):
                    mm = pe.matmul(ring[t % 4][:, :], xnT[:, c, t * P:(t + 1) * P], wt["attn_WkqT"][:, c, :],
                                   start=(c == 0), stop=(c == 1))
                mm.then_inc(kq_ps, 1)
                for c in range(2):
                    mm = pe.matmul(four[t // 2][:, (t % 2) * D:(t % 2 + 1) * D], xnT[:, c, t * P:(t + 1) * P],
                                   wt["attn_WvT"][:, c, :], start=(c == 0), stop=(c == 1))
                if t % 2:
                    mm.then_inc(v2_ps, 1)
            pe.wait_ge(kq_c, NT)
            for m in range(4):
                for which in range(2):
                    bank = ring[which * 2 + m % 2]
                    if m >= 2:
                        pe.wait_ge(qT_out if which else kT_out, 2 * (m - 1) if which else m - 1)
                    for g in range(2):
                        for j in range(2):
                            t = 2 * m + j
                            pe.wait_ge(kq_n, t + 1)
                            tr = pe.transpose(bank[:, (g * 2 + j) * P:(g * 2 + j + 1) * P],
                                              kqc[:, t, which * H + 8 * g:which * H + 8 * g + 8, :], ident[:, :])
                    tr.then_inc(kqT_ps, 1)

            def a_scores(n):
                u, j = n // 4, n % 4
                b, qt, g = u // 4, (u // 2) % 2, u % 2
                w = P * (qt + 1)
                tok = b * T + qt * P
                if n >= 4:
                    pe.wait_ge(a_exp, 2 * (n - 4) + 2)
                for e in range(2):
                    q = (qeT, qoT)[e][32 * j:32 * j + 32, g, tok:tok + P]
                    for kt in range(qt + 1):
                        to = four[j][:, e * w + kt * P:e * w + (kt + 1) * P]
                        if kt == qt:
                            pe.matmul(to, identb[:, :], causal[:, :], start=True, stop=False)
                        mm = pe.matmul(to, q, kT[32 * j:32 * j + 32, g, b * T + kt * P:b * T + (kt + 1) * P],
                                       start=(kt < qt), stop=True)
                mm.then_inc(a_ps, 1)

            def a_turn(n):
                u, j = n // 4, n % 4
                qt = (u // 2) % 2
                w = P * (qt + 1)
                if n >= 2:
                    pe.wait_ge(pT_out, n - 1)
                pe.wait_ge(a_exp, 2 * n + 2)
                for e in range(2):
                    for kt in range(qt + 1):
                        s = (e * (qt + 1) + kt) * P
                        src = prob[:, n % 8, e * w + kt * P:e * w + (kt + 1) * P]
                        if n < 12:
                            tr = pe.matmul(st[n % 2][:, s:s + P], src, ident[:, :], start=True, stop=True)
                        else:
                            tr = pe.transpose(st[n % 2][:, s:s + P], src, ident[:, :])
                tr.then_inc(pT_ps, 1)

            def a_values(u):
                b, qt, g = u // 4, (u // 2) % 2, u % 2
                bank = (st[2], mxb[0])[u % 2]
                pe.wait_ge(pT_out, 4 * u + 4)
                if u >= 2:
                    pe.wait_ge(o2_out, u - 1)
                for which in range(2):
                    for e in range(2):
                        for kt in range(qt + 1):
                            s = (e * (qt + 1) + kt) * P
                            for j in range(4):
                                h = 8 * g + 2 * j
                                seen = (v2e, v2o)[e][:, 2 * b + kt, h * DH:(h + 2) * DH]
                                mm = pe.matmul(bank[32 * j:32 * j + 32, which * P:(which + 1) * P],
                                               halfones[:, e, :] if which else seen,
                                               probT[u % 2][:, j, s:s + P], start=(e == 0 and kt == 0),
                                               stop=(e == 1 and kt == qt), skip_group_check=True)
                mm.then_inc(o2_ps, 1)

            pe.wait_ge(kT_out, 4)
            pe.wait_ge(qT_out, 8)
            pe.wait_ge(v2_out, 8)
            for n in range(4):
                a_scores(n)
            for n in range(64):
                a_turn(n)
                if n + 4 < 64:
                    a_scores(n + 4)
                if n % 4 == 1 and n > 4:
                    a_values(n // 4 - 1)
            a_values(15)
            pe.wait_ge(o2_out, 16)
            for n in range(4):
                for j in range(2):
                    t = 2 * n + j
                    to = four[n][:, j * D:(j + 1) * D]
                    for c in range(2):
                        mm = pe.matmul(to, xnT[:, c, t * P:(t + 1) * P], wt["attn_WoT"][:, c, :],
                                       start=(c == 0), stop=(c == 1))
                mm.then_inc(out_ps, 1)

            pe.wait_ge(sm_out, 2)
            pe.wait_ge(x_new, 8)
            for c in range(2):
                pe.matmul(kps[:, 0:1], wt["L0_ffn_w1"][:, 2 + c, :], smean[:, 1, c:c + 1], start=(c == 0), stop=False)
            pe.matmul(kps[:, 0:1], bias["L0_ffn_b1"], ones[0:1, 0:1], start=False, stop=True).then_inc(cv_ps, 1)
            turn(3, normed, ln_xn, lambda t: 2 * NT + t + 1)
            pe.wait_ge(xnT_act, 8)
            pe.wait_ge(xnT_dve, 8)
            for n in range(2):
                for c in range(2):
                    mm = pe.matmul(four[n][:, :], wt["L0_ffn_w1"][:, c, :], xnT[:, c, n * 512:(n + 1) * 512],
                                   start=(c == 0), stop=(c == 1))
                mm.then_inc(h_ps, 1)
            for t in range(NT):
                pe.wait_ge(h_out, t // 4 + 1)
                to = misc[:, t * SL:(t + 1) * SL]
                pe.matmul(to, ones[0:1, 0:P], bias["L0_ffn_b2"], start=True, stop=False)
                mm = pe.matmul(to, hT[:, t * P:(t + 1) * P], wt["L0_ffn_w2"][:, 0, :], start=False, stop=True)
            mm.then_inc(lg_ps, 1)
            wih, whh = wt["ffn_WihT"], wt["ffn_WhhT"]
            bih, bhh = bias["L0_ffn_bih"], bias["L0_ffn_bhh"]
            gates = ((mxb[0], kps), (misc, mxb[1]))
            for r in range(2):
                rzb, nb = gates[r]
                if r:
                    pe.wait_ge(lg_out, 1)
                for c in range(2):
                    pe.matmul(rzb[:, :], slotT[:, c, :], whh[:, c, 0:2 * D], start=(c == 0), stop=False)
                for row in (bih, bhh):
                    pe.matmul(rzb[:, :], ones[0:1, 0:P], row[:, 0:2 * D], start=False, stop=False)
                for c in range(2):
                    pe.matmul(nb[:, D:2 * D], slotT[:, c, :], whh[:, c, 2 * D:3 * D], start=(c == 0), stop=False)
                pe.matmul(nb[:, D:2 * D], ones[0:1, 0:P], bhh[:, 2 * D:3 * D], start=False, stop=True)
                pe.matmul(nb[:, 0:D], ones[0:1, 0:P], bih[:, 2 * D:3 * D], start=True, stop=False)
            pe.wait_ge(l_out, 1)
            for b in range(B):
                rows = slice((b % 2) * SL, (b % 2 + 1) * SL)
                for q in range(2):
                    pe.matmul(st[b // 2][rows, 0:D], alpha[:, 2 * b + q, :], xn[:, 2 * b + q, :],
                              start=(q == 0), stop=(q == 1))
                for q in range(2):
                    mm = pe.matmul(st[b // 2][rows, D:D + 1], alpha[:, 2 * b + q, :], onescol[:, :],
                                   start=(q == 0), stop=(q == 1))
                if b % 2:
                    mm.then_inc(si_ps, 1)
            pe.wait_ge(si_out, 2)
            for c in range(2):
                for r in range(2):
                    tr = pe.transpose(st[2][:, (c * 2 + r) * P:(c * 2 + r + 1) * P], si[:, r, c * P:(c + 1) * P],
                                      ident[:, :])
            tr.then_inc(siT_ps, 1)
            pe.wait_ge(siT_out, 1)
            for r in range(2):
                rzb, nb = gates[r]
                for c in range(2):
                    pe.matmul(rzb[:, :], siT[:, c, r * P:(r + 1) * P], wih[:, c, 0:2 * D], start=False, stop=(c == 1))
                for c in range(2):
                    mm = pe.matmul(nb[:, 0:D], siT[:, c, r * P:(r + 1) * P], wih[:, c, 2 * D:3 * D],
                                   start=False, stop=(c == 1))
                mm.then_inc(g_ps, 1)
            for t in range(NT):
                tr = pe.transpose((acc, st[0])[t // 4][0:SL, (t % 4) * P:(t % 4 + 1) * P], alpha[:, t, :], ident[:, :])
                if t % 4 == 3:
                    tr.then_inc(alT_ps, 1)
            for c in range(2):
                for r in range(2):
                    pe.wait_ge(g_new, r + 1)
                    tr = pe.transpose(st[1][:, (c * 2 + r) * P:(c * 2 + r + 1) * P], snew[:, r, c * P:(c + 1) * P],
                                      ident[:, :])
            tr.then_inc(snT_ps, 1)
            for n, (w, row) in enumerate((("L0_ffn_wq", "L0_ffn_bq"), ("L0_ffn_wk", "L0_ffn_bk"))):
                pe.matmul(st[2][0:SL, n * T:(n + 1) * T], bias[row], ones[0:1, 0:T], start=True, stop=False)
                pe.wait_ge(snT_out, 1)
                for c in range(2):
                    mm = pe.matmul(st[2][0:SL, n * T:(n + 1) * T], wt[w][:, c, :], snT[:, c, :],
                                   start=False, stop=(c == 1))
            mm.then_inc(qk_ps, 1)
            pe.wait_ge(alT_out, 2)
            for b in range(B):
                to = (mxb[1], acc)[b // 2][0:SL, (b % 2) * D:(b % 2 + 1) * D]
                for c in range(2):
                    pe.matmul(to, snT[:, c, b * SL:(b + 1) * SL], wt["L0_ffn_wv"][:, c, :], start=(c == 0), stop=False)
                mm = pe.matmul(to, ones[0:1, 0:SL], bias["L0_ffn_bv"], start=False, stop=True)
                if b % 2:
                    mm.then_inc(v4_ps, 1)
            pe.wait_ge(qk_out, 2)
            for b in range(B):
                mm = pe.matmul(mxb[0][(b % 2) * SL:(b % 2 + 1) * SL, (b // 2) * SL:(b // 2 + 1) * SL],
                               qkT[:, 0, b * SL:(b + 1) * SL], qkT[:, 1, b * SL:(b + 1) * SL], start=True, stop=True)
            mm.then_inc(c_ps, 1)
            pe.wait_ge(c_out, 1)
            for r in range(2):
                tr = pe.transpose(misc[0:SL, r * P:(r + 1) * P], att[:, r, :], ident[:, :])
            tr.then_inc(cT_ps, 1)
            pe.wait_ge(cT_out, 1)
            pe.wait_ge(v4_out, 2)
            for b in range(B):
                mm = pe.matmul(kps[(b % 2) * SL:(b % 2 + 1) * SL, (b // 2) * D:(b // 2 + 1) * D],
                               attT[:, b // 2, (b % 2) * SL:(b % 2 + 1) * SL], v4[:, b, :], start=True, stop=True)
            mm.then_inc(cm_ps, 1)
            last = (st[2], mxb[0], misc, kps)
            for n in range(4):
                if n == 3:
                    pe.wait_ge(y_out, 1)
                pe.matmul(last[n][:, 0:D], ones[0:1, 0:P], bias["L0_ffn_bo"], start=True, stop=False)
            pe.wait_ge(y_n, 2)
            for c in range(2):
                for r in range(2):
                    tr = pe.transpose(st[0][:, (c * 2 + r) * P:(c * 2 + r + 1) * P], y[:, r, c * P:(c + 1) * P],
                                      ident[:, :])
            tr.then_inc(yT_ps, 1)
            pe.wait_ge(yT_out, 2)
            for m in range(2):
                for c in range(2):
                    mm = pe.matmul(st[1][:, m * T:(m + 1) * T], wt["L0_ffn_wvp"][:, c, m * P:(m + 1) * P],
                                   yT[:, c, :], start=(c == 0), stop=(c == 1))
            mm.then_inc(sv_ps, 1)
            pe.wait_ge(sv_out, 2)
            for b in range(B):
                to = (mxb[1], acc)[b // 2][0:SL, (b % 2) * D:(b % 2 + 1) * D]
                for m in range(2):
                    mm = pe.matmul(to, svT[:, m, b * SL:(b + 1) * SL], wt["L0_ffn_wo"][:, m, :],
                                   start=(m == 0), stop=(m == 1))
                if b % 2:
                    mm.then_inc(svo_ps, 1)
            for n in range(4):
                pe.wait_ge(svo_out, n // 2 + 1)
                for j in range(2):
                    t = 2 * n + j
                    to = last[n][:, j * D:(j + 1) * D]
                    if j == 1:
                        pe.matmul(to, ones[0:1, 0:P], bias["L0_ffn_bo"], start=True, stop=False)
                    mm = pe.matmul(to, alphaT[:, t, :], svo[:, n, :], start=False, stop=True)
                mm.then_inc(out_ps, 1)


def kernel(**inputs):
    import numpy as np
    import concourse.bacc as bacc
    from concourse.bass_utils import run_bass_kernel_spmd as run

    arrays = {k: np.ascontiguousarray(v) for k, v in inputs.items() if k != "ctx_768"}
    ctx = np.ascontiguousarray(inputs["ctx_768"]).reshape(NCH, CH, C)
    arrays["ctxT"] = np.ascontiguousarray(ctx.transpose(0, 2, 1))
    for name, key in (("attn_WvT", "L0_attn_Wv"), ("attn_WoT", "L0_attn_Wo"), ("ffn_WihT", "L0_ffn_Wih"),
                      ("ffn_WhhT", "L0_ffn_Whh"), ("ffn_slotT", "L0_ffn_slot_init")):
        arrays[name] = np.ascontiguousarray(arrays[key].T)
    arrays["attn_WkqT"] = np.ascontiguousarray(
        np.concatenate([arrays["L0_attn_Wk"], arrays["L0_attn_Wq"]], axis=0).T)
    for key in ("L0_attn_Wv", "L0_attn_Wo", "L0_attn_Wk", "L0_attn_Wq", "L0_ffn_Wih", "L0_ffn_Whh"):
        del arrays[key]
    nc = bacc.Bacc("TRN2", target_bir_lowering=False, num_devices=1)
    aps = {k: nc.dram_tensor("in_" + k, v.shape, mybir.dt.from_np(v.dtype), kind="ExternalInput").ap()
           for k, v in arrays.items()}
    out = nc.dram_tensor("out", (B, T, D), F32, kind="ExternalOutput").ap()
    build(nc, aps, out)
    r = run(nc, [{"in_" + k: v for k, v in arrays.items()}], core_ids=[0])
    return r.results[0]["out"]
```
